# Optimizing a Trainium2 kernel written in Bass

```python
import numpy as np
import jax
import jax.numpy as jnp

def _softmax(x, axis=-1):
    return jax.nn.softmax(x, axis=axis)

def _gelu(x):
    return jax.nn.gelu(x, approximate=True)

def _silu(x):
    return jax.nn.silu(x)

def _sigmoid(x):
    return jax.nn.sigmoid(x)

def _layernorm(x, axis=-1, eps=1e-05):
    m = jnp.mean(x, axis=axis, keepdims=True)
    v = jnp.var(x, axis=axis, keepdims=True)
    return (x - m) / jnp.sqrt(v + eps)

def _scatter_add(tgt, idx, src, axis=0):
    return tgt.at[idx].add(src)

def _segment_sum(src, seg, n):
    return jax.ops.segment_sum(src, seg, n)
kernel_name = 'mk_seq_preln_d1_jaxref_r8_403096'

def setup_inputs(seed: int=0):
    np.random.seed(seed)
    _w = jnp.asarray

    def _L0_attn_setup():
        import jax, jax.numpy as jnp
        import numpy as np
        import math
        B, S, E, H = (2, 256, 128, 8)
        Dh = E // H

        def _pos_encoding(s, e):
            pos = jnp.arange(s, dtype=jnp.float32)[:, None]
            div = jnp.exp(jnp.arange(0, e, 2, dtype=jnp.float32) * (-math.log(10000.0) / e))
            pe = jnp.zeros((s, e), jnp.float32)
            pe = pe.at[:, 0::2].set(jnp.sin(pos * div))
            pe = pe.at[:, 1::2].set(jnp.cos(pos * div))
            return pe

        def _rel_shift(ps):
            b, h, s1, s2 = ps.shape
            padded = jnp.pad(ps, ((0, 0), (0, 0), (0, 0), (1, 0)))
            return padded.reshape(b, h, s2 + 1, s1)[:, :, 1:, :].reshape(b, h, s1, s2)

        def _forward(inputs, ln_gamma, ln_beta, Wq, bq, Wk, bk, Wv, bv, Wp, u_bias, v_bias, Wo, bo):
            b, s, e = inputs.shape
            mu = inputs.mean(-1, keepdims=True)
            var = inputs.var(-1, keepdims=True)
            xn = (inputs - mu) / jnp.sqrt(var + 1e-05) * ln_gamma + ln_beta
            xh = xn.reshape(b, s, H, Dh)
            q = xh @ Wq + bq
            k = xh @ Wk + bk
            v = xh @ Wv + bv
            pe = _pos_encoding(s, e).reshape(s, H, Dh)
            p = pe @ Wp
            content = jnp.einsum('bqhd,bkhd->bhqk', q + u_bias, k)
            pos_score = jnp.einsum('bqhd,khd->bhqk', q + v_bias, p)
            pos_score = _rel_shift(pos_score)
            score = (content + pos_score) / jnp.sqrt(jnp.float32(e))
            attn = jax.nn.softmax(score, axis=-1)
            ctx = jnp.einsum('bhqk,bkhd->bqhd', attn, v).reshape(b, s, e)
            return ctx @ Wo + bo
        key = jax.random.key(seed)
        ks = jax.random.split(key, 9)
        g = lambda k, shp: jax.random.normal(k, shp, jnp.float32) * 0.02
        return {'inputs': jax.random.normal(ks[0], (B, S, E), jnp.float32), 'ln_gamma': jnp.ones((E,), jnp.float32), 'ln_beta': jnp.zeros((E,), jnp.float32), 'Wq': g(ks[1], (Dh, Dh)), 'bq': jnp.zeros((Dh,), jnp.float32), 'Wk': g(ks[2], (Dh, Dh)), 'bk': jnp.zeros((Dh,), jnp.float32), 'Wv': g(ks[3], (Dh, Dh)), 'bv': jnp.zeros((Dh,), jnp.float32), 'Wp': g(ks[4], (Dh, Dh)), 'u_bias': g(ks[5], (H, Dh)), 'v_bias': g(ks[6], (H, Dh)), 'Wo': g(ks[7], (E, E)), 'bo': jnp.zeros((E,), jnp.float32)}
    _L0_attn_in = _L0_attn_setup()

    def _L0_ffn_setup():
        import jax, jax.numpy as jnp
        import numpy as np
        SQRT_2_PI = 0.7978845608028654
        GELU_COEF = 0.044715
        LN_EPS = 1e-06
        TOP_K = 2

        def gelu_kernel(x):
            inner = SQRT_2_PI * (x + GELU_COEF * x ** 3)
            return 0.5 * x * (1.0 + jnp.tanh(inner))
        key = jax.random.key(seed)
        ks = jax.random.split(key, 8)
        B, S, D, F, E = (2, 256, 128, 512, 8)
        s = lambda d: 1.0 / np.sqrt(d)
        return {'x': jax.random.normal(ks[0], (B, S, D), jnp.float32), 'Wr1': jax.random.normal(ks[1], (D, D // 2), jnp.float32) * s(D), 'br1': jnp.zeros((D // 2,), jnp.float32), 'ln_scale': jnp.ones((D // 2,), jnp.float32), 'ln_bias': jnp.zeros((D // 2,), jnp.float32), 'Wr2': jax.random.normal(ks[2], (D // 2, E), jnp.float32) * s(D // 2), 'br2': jnp.zeros((E,), jnp.float32), 'W1': jax.random.normal(ks[3], (E, D, 2 * F), jnp.float32) * s(D), 'b1': jnp.zeros((E, 2 * F), jnp.float32), 'W2': jax.random.normal(ks[4], (E, F, D), jnp.float32) * s(F), 'b2': jnp.zeros((E, D), jnp.float32)}
    _L0_ffn_in = _L0_ffn_setup()
    _d = {'L0_attn_inputs': _L0_attn_in['inputs'], 'L0_attn_ln_gamma': _L0_attn_in['ln_gamma'], 'L0_attn_ln_beta': _L0_attn_in['ln_beta'], 'L0_attn_Wq': _L0_attn_in['Wq'], 'L0_attn_bq': _L0_attn_in['bq'], 'L0_attn_Wk': _L0_attn_in['Wk'], 'L0_attn_bk': _L0_attn_in['bk'], 'L0_attn_Wv': _L0_attn_in['Wv'], 'L0_attn_bv': _L0_attn_in['bv'], 'L0_attn_Wp': _L0_attn_in['Wp'], 'L0_attn_u_bias': _L0_attn_in['u_bias'], 'L0_attn_v_bias': _L0_attn_in['v_bias'], 'L0_attn_Wo': _L0_attn_in['Wo'], 'L0_attn_bo': _L0_attn_in['bo'], 'L0_ffn_Wr1': _L0_ffn_in['Wr1'], 'L0_ffn_br1': _L0_ffn_in['br1'], 'L0_ffn_ln_scale': _L0_ffn_in['ln_scale'], 'L0_ffn_ln_bias': _L0_ffn_in['ln_bias'], 'L0_ffn_Wr2': _L0_ffn_in['Wr2'], 'L0_ffn_br2': _L0_ffn_in['br2'], 'L0_ffn_W1': _L0_ffn_in['W1'], 'L0_ffn_b1': _L0_ffn_in['b1'], 'L0_ffn_W2': _L0_ffn_in['W2'], 'L0_ffn_b2': _L0_ffn_in['b2']}
    _x0 = _d['L0_attn_inputs']
    _d['L0_attn_inputs'] = jax.random.normal(jax.random.fold_in(jax.random.key(seed), 1), (8, 1024, 128), dtype=_x0.dtype)
    del _x0
    return _d

def reference(L0_attn_inputs, L0_attn_ln_gamma, L0_attn_ln_beta, L0_attn_Wq, L0_attn_bq, L0_attn_Wk, L0_attn_bk, L0_attn_Wv, L0_attn_bv, L0_attn_Wp, L0_attn_u_bias, L0_attn_v_bias, L0_attn_Wo, L0_attn_bo, L0_ffn_Wr1, L0_ffn_br1, L0_ffn_ln_scale, L0_ffn_ln_bias, L0_ffn_Wr2, L0_ffn_br2, L0_ffn_W1, L0_ffn_b1, L0_ffn_W2, L0_ffn_b2):

    def _L0_attn_ref(inputs, ln_gamma, ln_beta, Wq, bq, Wk, bk, Wv, bv, Wp, u_bias, v_bias, Wo, bo):
        import jax, jax.numpy as jnp
        import numpy as np
        import math
        B, S, E, H = (2, 256, 128, 8)
        Dh = E // H

        def _pos_encoding(s, e):
            pos = jnp.arange(s, dtype=jnp.float32)[:, None]
            div = jnp.exp(jnp.arange(0, e, 2, dtype=jnp.float32) * (-math.log(10000.0) / e))
            pe = jnp.zeros((s, e), jnp.float32)
            pe = pe.at[:, 0::2].set(jnp.sin(pos * div))
            pe = pe.at[:, 1::2].set(jnp.cos(pos * div))
            return pe

        def _rel_shift(ps):
            b, h, s1, s2 = ps.shape
            padded = jnp.pad(ps, ((0, 0), (0, 0), (0, 0), (1, 0)))
            return padded.reshape(b, h, s2 + 1, s1)[:, :, 1:, :].reshape(b, h, s1, s2)

        def _forward(inputs, ln_gamma, ln_beta, Wq, bq, Wk, bk, Wv, bv, Wp, u_bias, v_bias, Wo, bo):
            b, s, e = inputs.shape
            mu = inputs.mean(-1, keepdims=True)
            var = inputs.var(-1, keepdims=True)
            xn = (inputs - mu) / jnp.sqrt(var + 1e-05) * ln_gamma + ln_beta
            xh = xn.reshape(b, s, H, Dh)
            q = xh @ Wq + bq
            k = xh @ Wk + bk
            v = xh @ Wv + bv
            pe = _pos_encoding(s, e).reshape(s, H, Dh)
            p = pe @ Wp
            content = jnp.einsum('bqhd,bkhd->bhqk', q + u_bias, k)
            pos_score = jnp.einsum('bqhd,khd->bhqk', q + v_bias, p)
            pos_score = _rel_shift(pos_score)
            score = (content + pos_score) / jnp.sqrt(jnp.float32(e))
            attn = jax.nn.softmax(score, axis=-1)
            ctx = jnp.einsum('bhqk,bkhd->bqhd', attn, v).reshape(b, s, e)
            return ctx @ Wo + bo
        return _forward(inputs, ln_gamma, ln_beta, Wq, bq, Wk, bk, Wv, bv, Wp, u_bias, v_bias, Wo, bo)

    def _L0_ffn_ref(x, Wr1, br1, ln_scale, ln_bias, Wr2, br2, W1, b1, W2, b2):
        import jax, jax.numpy as jnp
        import numpy as np
        SQRT_2_PI = 0.7978845608028654
        GELU_COEF = 0.044715
        LN_EPS = 1e-06
        TOP_K = 2

        def gelu_kernel(x):
            inner = SQRT_2_PI * (x + GELU_COEF * x ** 3)
            return 0.5 * x * (1.0 + jnp.tanh(inner))
        E = W1.shape[0]
        h = jnp.einsum('bsd,dk->bsk', x, Wr1) + br1
        mu = jnp.mean(h, axis=-1, keepdims=True)
        var = jnp.mean((h - mu) ** 2, axis=-1, keepdims=True)
        h = (h - mu) * jax.lax.rsqrt(var + LN_EPS) * ln_scale + ln_bias
        h = gelu_kernel(h)
        router_logits = jnp.einsum('bsk,ke->bse', h, Wr2) + br2
        routing_probs = jax.nn.softmax(router_logits, axis=-1)
        top_k_probs, top_k_indices = jax.lax.top_k(routing_probs, TOP_K)
        top_k_probs = top_k_probs / jnp.sum(top_k_probs, axis=-1, keepdims=True)
        expert_mask = jnp.sum(jax.nn.one_hot(top_k_indices, E, dtype=x.dtype) * top_k_probs[..., None], axis=-2)
        output = jnp.zeros_like(x)
        for e in range(E):
            x12 = jnp.einsum('bsd,df->bsf', x, W1[e]) + b1[e]
            x1, x2 = jnp.split(x12, 2, axis=-1)
            g = x1 * gelu_kernel(x2)
            y = jnp.einsum('bsf,fd->bsd', g, W2[e]) + b2[e]
            output = output + y * expert_mask[:, :, e][:, :, None]
        return output
    x = L0_attn_inputs
    x = x + _L0_attn_ref(_layernorm(x, axis=-1), L0_attn_ln_gamma, L0_attn_ln_beta, L0_attn_Wq, L0_attn_bq, L0_attn_Wk, L0_attn_bk, L0_attn_Wv, L0_attn_bv, L0_attn_Wp, L0_attn_u_bias, L0_attn_v_bias, L0_attn_Wo, L0_attn_bo)
    x = x + _L0_ffn_ref(_layernorm(x, axis=-1), L0_ffn_Wr1, L0_ffn_br1, L0_ffn_ln_scale, L0_ffn_ln_bias, L0_ffn_Wr2, L0_ffn_br2, L0_ffn_W1, L0_ffn_b1, L0_ffn_W2, L0_ffn_b2)
    return x

_drawn_inputs = setup_inputs


def setup_inputs(seed=0):
    import zlib

    import numpy as np

    out = dict(_drawn_inputs(seed))
    spreads = {'L0_attn_ln_gamma': (1.0, 0.6),
     'L0_attn_ln_beta': (0.0, 0.585),
     'L0_attn_bq': (0.0, 0.8),
     'L0_attn_bk': (0.0, 2.0),
     'L0_attn_bv': (0.0, 0.1),
     'L0_attn_bo': (0.0, 0.1),
     'L0_ffn_br1': (0.0, 0.1),
     'L0_ffn_ln_scale': (1.0, 0.2),
     'L0_ffn_ln_bias': (0.0, 0.1),
     'L0_ffn_br2': (0.0, 0.1),
     'L0_ffn_b1': (0.0, 0.1),
     'L0_ffn_b2': (0.0, 0.1)}
    factors = {'L0_attn_Wq': 8.0,
     'L0_attn_Wk': 8.0,
     'L0_attn_Wv': 5.541,
     'L0_attn_Wp': 46.883,
     'L0_attn_u_bias': 26.954,
     'L0_attn_v_bias': 173.546}
    for name, (base, spread) in spreads.items():
        noise = np.random.default_rng([zlib.crc32(name.encode()), seed]).standard_normal(out[name].shape)
        drawn = base * np.exp(spread * noise) if base else spread * noise
        out[name] = jnp.asarray(drawn.astype(out[name].dtype))
    for name, factor in factors.items():
        out[name] = (out[name] * factor).astype(out[name].dtype)
    return out
```

```python
from contextlib import ExitStack

import concourse.bass as bass
from concourse import mybir

F32, F32R, BF16 = mybir.dt.float32, mybir.dt.float32r, mybir.dt.bfloat16
I32, U32 = mybir.dt.int32, mybir.dt.uint32
ALU = mybir.AluOpType
ACT = mybir.ActivationFunctionType
AX = mybir.AxisListType

B, S, E, H = 8, 1024, 128, 8
D = E // H
P = 128
NB = S // P
SCALE = float(E) ** -0.5
LN_EPS = 1e-5
FAR = -1.0e30
HALF = 512
HPB = S // HALF
S1U = NB * HPB + HPB
S2U = NB + 1
RING = 3
SLOTS = 4
AHEAD = 2
FEAT = 2 * D
KROWS = 3 * FEAT
MROW = KROWS
STK = 18 * 16
VW = 32
RH = 64
NX = 8
TOPK = 2
F = 512
ROUTER_EPS = 1e-6
TOKENS = B * S
REGION = TOKENS + P
ROW = E + 2
TILES = TOPK * TOKENS // P + NX
TABLE = TILES + 2
UNROLL = 4


def known(eng, value):
    return value if isinstance(value, int) else eng.to_reg(value)


def attention_phase(nc, dram):
    ctx = ExitStack()
    with ctx:
        def sb(name, shape, dt=F32):
            return ctx.enter_context(nc.sbuf_tensor(name, shape, dt))

        def pb(name, shape):
            return ctx.enter_context(nc.psum_tensor(name, shape, F32))

        def sem(name):
            return ctx.enter_context(nc.semaphore(name))

        w_q, w_k, w_v, w_p, w_ps, w_o = (sb(n, [P, P]) for n in ("w_q", "w_k", "w_v", "w_p", "w_ps", "w_o"))
        cols = sb("cols", [P, 4])
        bias_qv, bias_qu = sb("bias_qv", [P, 1]), sb("bias_qu", [P, 1])
        rows = sb("rows", [P, 2, P])
        vu = sb("vu", [P, 2])
        rot = [sb(n, [P, S]) for n in ("cos_lo", "sin_lo", "cos_up", "sin_up")]
        ident, fold, hsum = sb("ident", [P, P]), sb("fold", [P, VW]), sb("hsum", [P, H])
        lmask, umask = sb("lmask", [P, 15 * P], BF16), sb("umask", [P, P])
        cmask = sb("cmask", [P, H, NB])
        xt = sb("xt", [P, NB, E])
        st6, mv, rs = sb("st6", [P, NB, 6]), sb("mv", [P, NB, 2]), sb("rs", [P, 3, NB])
        mhalf = sb("mhalf", [P, NB])
        xnT = sb("xnT", [P, S + 1])
        qv, qu, kc = sb("qv", [P, S]), sb("qu", [P, S]), sb("kc", [P, S + 1])
        rp, rq = sb("rp", [P, S + 1]), sb("rq", [P, S + 1])
        g_lo, g_up, t2, t3 = (sb(n, [P, S]) for n in ("g_lo", "g_up", "t2", "t3"))
        xn = g_up[:, :].rearrange("p (t e) -> p t e", e=E)
        parts = {n: (sb(n + "_h", [P, S], F32R), sb(n + "_l", [P, S], F32R)) for n in ("c", "k", "gl", "gu", "pe")}
        QL, QU, K = (sb(n, [P, SLOTS, S], F32R) for n in ("QL", "QU", "K"))
        prob = [sb(f"prob{i}", [P, S]) for i in range(RING)]
        ctxp = [sb(f"ctxp{i}", [P, S]) for i in range(2)]
        ctx_all = sb("ctx_all", [P, NB, H, D + 1])
        vext = sb("vext", [P, NB, H, VW])
        vsh = sb("vsh", [P, NB, H, D])
        acc = sb("acc", [P, H, NB, 4])
        mneg = sb("mneg", [P, H, NB], F32R)
        dsup, psup = sb("dsup", [P, H, NB]), sb("psup", [P, H, NB])
        den = sb("den", [P, NB, H])
        mrow = [sb(f"mrow{i}", [NB, P], F32R) for i in range(2)]
        tmpd, junk = sb("tmpd", [P, HALF]), sb("junk", [P, 2, HALF], BF16)
        ctxT = t3
        xres = sb("xres", [P, NB, E])
        pA = [pb(f"pA{i}", [P, HALF]) for i in range(2)]
        pB, pC = pb("pB", [P, S]), pb("pC", [P, S])
        pM, pE = pb("pM", [P, HALF]), pb("pE", [P, HALF])

        d_w, d_cst, d_x, d_res, d_x2 = sem("weights_in"), sem("constants_in"), sem("x_in"), sem("residual_in"), sem("x2_out")
        set_pool, set_dve = sem("set_pool"), sem("set_dve")
        s1_ready, s1_read, dred = sem("s1_ready"), sem("s1_read"), sem("diagonals_reduced")
        mx_done, dsup_done = sem("mx_done"), sem("dsup_done")
        mrow_in = [sem(f"mrow_in{i}") for i in range(2)]
        s2_ready, p_exp, p_mask, pv_done = sem("s2_ready"), sem("p_exp"), sem("p_mask"), sem("pv_done")
        ctx_evac, psup_done = sem("ctx_evac"), sem("psup_done")
        m_ready, m_done = sem("m_ready"), sem("m_done")
        e_ready, e_done, hi_done = sem("e_ready"), sem("e_done"), sem("hi_done")
        ln, pd, norm, fin, rs_done = sem("ln"), sem("pd"), sem("norm"), sem("fin"), sem("rs_done")
        stk = [sem(f"stk{i}") for i in range(SLOTS)]
        block = ctx.enter_context(nc.Block())

        LN_N, PD_N, NORM_N, HI_N, RS_N = 3 * NB, 11, 5, 4, 7
        E_AT = [1, 2, 4, 6, 7, 8, 9, 10, 11, 12]
        E_N = E_AT[-1]
        M_PRO = 3
        M_N = 25
        M_ROW = [0, 2, 8, 13, 15, 17, 19, 23]
        M_FOLD = [1, 3, 9, 14, 16, 18, 20, 24]
        M_FIN, M_VB, M_VSH, M_C, M_VA = 4, 10, 11, 21, 22
        DVE_SET, POOL_SET = 12, 12
        D_W, D_CST = 16 * 10, 16 * 7

        def piece(n):
            qb, k0 = n // HPB, (n % HPB) * HALF
            return qb, k0, min(max(P * (qb + 1) - k0, 0), HALF)

        @block.sync
        def _(sp):
            for t, n in ((w_q, "wq"), (w_k, "wk"), (w_v, "wv"), (w_p, "wp"), (w_ps, "wps"), (w_o, "wo")):
                sp.dma_start(t[:, :], dram[n]).then_inc(d_w, 16)
            sp.dma_start(cols[:, :], dram["cols"]).then_inc(d_w, 16)
            sp.dma_start(vu[:, :], dram["vu"]).then_inc(d_w, 16)
            sp.dma_start(rows[:, 0, :], dram["bv"].partition_broadcast(P)).then_inc(d_w, 16)
            sp.dma_start(rows[:, 1, :], dram["bo"].partition_broadcast(P)).then_inc(d_w, 16)
            sp.dma_start(xt[:, :, :], dram["x"][0].rearrange("(t p) e -> p t e", p=P)).then_inc(d_x, 16)
            for i, t in enumerate(rot):
                sp.dma_start(t[:, :], dram["rot"][i]).then_inc(d_cst, 16)
            sp.dma_start(g_lo[:, :], dram["pe"]).then_inc(d_cst, 16)
            sp.dma_start(fold[:, :], dram["fold"]).then_inc(d_cst, 16)
            sp.dma_start(hsum[:, :], dram["hsum"]).then_inc(d_cst, 16)

            def stack(h, groups=(0, 1, 2)):
                s, r = h % SLOTS, D * (h % H)
                for dst, con, pos, order in ((QL, "c", "gl", (0, 1, 0)), (QU, "c", "gu", (0, 1, 0)), (K, "k", "pe", (0, 0, 1))):
                    for g in groups:
                        which = order[g]
                        for c, name in ((0, con), (1, pos)):
                            row = FEAT * g + D * c
                            sp.dma_start(dst[row:row + D, s, :].bitcast(F32),
                                         parts[name][which][r:r + D, :].bitcast(F32)).then_inc(stk[s], 16)

            def maximum_row(h):
                s = h % SLOTS
                for dst in (QL, QU):
                    sp.dma_start(dst[MROW:MROW + 1, s, :].bitcast(F32).rearrange("o (n p) -> o n p", p=P),
                                 mrow[h % 2][:, :].bitcast(F32)).then_inc(mrow_in[h % 2], 16)

            sp.sem_inc(d_x2, 16)
            sp.wait_ge(set_dve, DVE_SET)
            sp.wait_ge(hi_done, HI_N)
            sp.wait_ge(pd, PD_N)
            for h in range(3):
                stack(h)
            sp.wait_ge(m_done, M_PRO)
            maximum_row(0)
            with sp.Fori(0, B) as b:
                for h in range(H):
                    if h == 0:
                        stored = known(sp, b * 16 + 16)
                        sp.wait_ge(set_dve, DVE_SET)
                        sp.wait_ge(d_x2, stored)
                        sp.dma_start(xres[:, :, :], dram["x"][bass.ds((b + B - 1) % B, 1)].rearrange("o (t p) e -> p (o t) e", p=P)).then_inc(d_res, 16)
                        normed = known(sp, (b + 1) * LN_N)
                        sp.wait_ge(set_dve, DVE_SET)
                        sp.wait_ge(ln, normed)
                        sp.dma_start(xt[:, :, :], dram["x"][bass.ds((b + 1) % B, 1)].rearrange("o (t p) e -> p (o t) e", p=P)).then_inc(d_x, 16)
                    if h + 3 == H:
                        sp.wait_ge(m_done, b * M_N + M_PRO + M_ROW[h] + 1)
                        maximum_row(h + 1)
                        highs, lows = known(sp, (b + 2) * HI_N), known(sp, (b + 2) * PD_N)
                        through = known(sp, b * (H * S2U) + h * S2U + 1)
                        sp.wait_ge(set_dve, DVE_SET)
                        sp.wait_ge(hi_done, highs)
                        sp.wait_ge(pd, lows)
                    else:
                        through = known(sp, b * (H * S2U) + h * S2U + 1)
                    sp.wait_ge(s2_ready, through)
                    stack(h + 3, (0,))
                    if h + 3 != H:
                        sp.wait_ge(m_done, b * M_N + M_PRO + M_ROW[h] + 1)
                        maximum_row(h + 1)
                    stack(h + 3, (1, 2))
                    if h == 2:
                        sp.wait_ge(m_done, b * M_N + M_PRO + M_FIN + 4)
                        sp.dma_start(dram["x2s"][bass.ds(b, 1)].rearrange("o (t p) e -> p (o t) e", p=P), xres[:, :, :]).then_inc(d_x2, 16)
            sp.wait_ge(d_x2, (B + 1) * 16)
            sp.dma_start(xres[:, :, :], dram["x"][B - 1].rearrange("(t p) e -> p t e", p=P)).then_inc(d_res, 16)
            sp.wait_ge(m_done, B * M_N + M_PRO + 5)
            sp.dma_start(dram["x2s"][B].rearrange("(t p) e -> p t e", p=P), xres[:, :, :]).then_inc(d_x2, 16)
            sp.wait_ge(d_x2, (B + 2) * 16)
            for s in range(SLOTS):
                sp.wait_ge(stk[s], (2 * B + (s < 3)) * STK)
            for i in range(2):
                sp.wait_ge(mrow_in[i], (4 * B + 1 - i) * 32)
            sp.wait_ge(d_x, (B + 1) * 16)

        @block.gpsimd
        def _(po):
            po.memset(ident[:, :], 0.0).then_inc(set_pool, 1)
            po.memset(lmask[:, :], 0.0).then_inc(set_pool, 1)
            po.memset(umask[:, :], 0.0).then_inc(set_pool, 1)
            po.memset(cmask[:, :, :], 0.0).then_inc(set_pool, 1)
            po.memset(vext[:, :, :, :], 0.0).then_inc(set_pool, 1)
            po.memset(ctxp[1][:, :], 1.0).then_inc(set_pool, 1)
            po.memset(mhalf[:, :], -0.5).then_inc(set_pool, 1)
            po.wait_ge(set_pool, 7)
            po.affine_select(out=ident[:, :], in_=ident[:, :], compare_op=ALU.not_equal, fill=1.0, base=0,
                             pattern=[[-1, P]], channel_multiplier=1).then_inc(set_pool, 1)
            po.affine_select(out=lmask[:, 7 * P:8 * P], in_=lmask[:, 7 * P:8 * P], compare_op=ALU.is_ge, fill=FAR, base=0,
                             pattern=[[-1, P]], channel_multiplier=1).then_inc(set_pool, 1)
            po.affine_select(out=umask[:, :], in_=umask[:, :], compare_op=ALU.is_ge, fill=FAR, base=-2,
                             pattern=[[1, P]], channel_multiplier=-1).then_inc(set_pool, 1)
            po.affine_select(out=cmask[:, :, :], in_=cmask[:, :, :], compare_op=ALU.not_equal, fill=FAR, base=1 - S,
                             pattern=[[0, H], [P, NB]], channel_multiplier=1).then_inc(set_pool, 1)
            po.memset(vext[:, :, :, D:D + 1], 1.0).then_inc(set_pool, 1)

            def rstd(nb):
                at = nb * RS_N
                variances, sums = known(po, nb * LN_N + 2 * NB), known(po, at + 4)
                po.wait_ge(set_pool, POOL_SET)
                po.wait_ge(ln, variances)
                po.tensor_scalar(rs[:, 0, :], mv[:, :, 1], LN_EPS, None, ALU.add).then_inc(rs_done, 1)
                po.wait_ge(rs_done, at + 1)
                po.tensor_tensor(rs[:, 0, :], rs[:, 0, :], mhalf[:, :], ALU.pow).then_inc(rs_done, 1)
                po.wait_ge(rs_done, at + 2)
                po.tensor_tensor(rs[:, 1, :], rs[:, 0, :], rs[:, 0, :], ALU.mult).then_inc(rs_done, 1)
                po.wait_ge(rs_done, at + 3)
                po.tensor_tensor(rs[:, 2, :], rs[:, 1, :], mv[:, :, 1], ALU.mult).then_inc(rs_done, 1)
                po.wait_ge(set_pool, POOL_SET)
                po.wait_ge(rs_done, sums)
                po.tensor_scalar(rs[:, 2, :], rs[:, 2, :], LN_EPS, None, ALU.add).then_inc(rs_done, 1)
                po.wait_ge(rs_done, at + 5)
                po.tensor_tensor(rs[:, 2, :], rs[:, 2, :], mhalf[:, :], ALU.pow).then_inc(rs_done, 1)
                po.wait_ge(rs_done, at + 6)
                po.tensor_tensor(rs[:, 2, :], rs[:, 2, :], rs[:, 0, :], ALU.mult).then_inc(rs_done, 1)

            rstd(0)
            with po.Fori(0, B) as b:
                for h in range(H):
                    for u in range(S2U):
                        if h == 1 and u == 8:
                            rstd(b + 1)
                        n = h * S2U + u
                        units = known(po, b * (H * S2U) + n + 2)
                        po.wait_ge(set_pool, POOL_SET)
                        po.wait_ge(p_exp, units)
                        if u < NB:
                            p = prob[n % RING][:, P * u:P * u + P]
                            po.affine_select(out=p, in_=p, compare_op=ALU.is_ge, fill=0.0, base=0,
                                             pattern=[[1, P]], channel_multiplier=-1).then_inc(p_mask, 1)
                        else:
                            p = prob[n % RING][:, :].rearrange("p (n q) -> p n q", q=P)
                            po.affine_select(out=p, in_=p, compare_op=ALU.is_ge, fill=0.0, base=-2,
                                             pattern=[[0, NB], [-1, P]], channel_multiplier=1).then_inc(p_mask, 1)

        @block.tensor
        def _(pe):
            pe.wait_ge(d_w, D_W)
            pe.wait_ge(d_cst, D_CST)
            pe.wait_ge(set_pool, POOL_SET)
            pe.wait_ge(set_dve, DVE_SET)
            pe.sem_inc(s2_ready, 1)
            pe.sem_inc(pv_done, RING)

            def project(nb, j):
                if j == 0:
                    pe.wait_ge(ln, (nb + 1) * LN_N)
                pe.wait_ge(e_done, nb * E_N + (E_AT[j - 1] if j else 0)) if not (isinstance(nb, int) and nb == 0 and j == 0) else None
                half = slice(HALF * (j % 2), HALF * (j % 2) + HALF)
                if j < 2:
                    for t in range(4):
                        mm = pe.transpose(pE[:, P * t:P * t + P], xn[:, 4 * j + t, :], ident[:, :])
                else:
                    w, src = ((w_q, xnT), (w_k, xnT), (w_p, qv), (w_ps, qv))[j // 2 - 1]
                    mm = pe.matmul(pE[:, :], w[:, :], src[:, half], start=True, stop=True)
                mm.then_inc(e_ready, 1)

            def claim_m(b, i):
                pe.wait_ge(m_done, b * M_N + M_PRO + i)

            def super_scores():
                for blk in range(NB):
                    mm = pe.matmul(pM[:, H * blk:H * blk + H], t2[:, P * blk:P * blk + P], hsum[:, :], start=True, stop=True)
                mm.then_inc(m_ready, 1)

            def values(half):
                for t in range(NB):
                    mm = pe.matmul(pM[:, 64 * t:64 * t + 64], xnT[:, P * t:P * t + P], w_v[:, 64 * half:64 * half + 64], start=True, stop=True)
                mm.then_inc(m_ready, 1)

            def values_shifted(half):
                for t in range(4):
                    c = P * (4 * half + t) + 1
                    mm = pe.matmul(pM[:, P * t:P * t + P], xnT[:, c:c + P], w_v[:, :], start=True, stop=True)
                mm.then_inc(m_ready, 1)

            def row_of_maxima(b, h):
                pe.wait_ge(mx_done, b * H + h + 1)
                pe.transpose(pM[0:NB, 0:P], mneg[:, h % H, :].bitcast(F32), ident[:, :]).then_inc(m_ready, 1)

            def fold_context(b, h, par):
                pe.wait_ge(ctx_evac, b * H + h + 2)
                for blk in range(NB):
                    mm = pe.matmul(pM[:, VW * blk:VW * blk + VW], ctxp[par][:, P * blk:P * blk + P], fold[:, :], start=True, stop=True)
                mm.then_inc(m_ready, 1)

            def first_pass(b, h, n):
                s = h % SLOTS
                if n == 0:
                    pe.wait_ge(stk[s], b * (2 * STK) + (h // SLOTS + 1) * STK)
                if not (isinstance(b, int) and h == 0 and n < 2):
                    pe.wait_ge(s1_read, b * (H * S1U) + h * S1U + n - 1)
                dst = pA[n % 2]
                if n < NB * HPB:
                    qb, k0, low = piece(n)
                    q = slice(P * qb, P * qb + P)
                    if low > 0:
                        mm = pe.matmul(dst[:, 0:low], QL[0:KROWS, s, q], K[0:KROWS, s, k0:k0 + low], start=True, stop=True)
                    if low < HALF:
                        mm = pe.matmul(dst[:, low:HALF], QU[0:KROWS, s, q], K[0:KROWS, s, k0 + low:k0 + HALF], start=True, stop=True)
                else:
                    for i in range(4):
                        q = slice(P * (4 * (n % 2) + i), P * (4 * (n % 2) + i) + P)
                        mm = pe.matmul(dst[:, P * i:P * i + P], QU[0:KROWS, s, q], K[0:KROWS, s, q], start=True, stop=True)
                mm.then_inc(s1_ready, 1)

            def second_pass(b, h, u):
                s = h % SLOTS
                if u == 0:
                    pe.wait_ge(mrow_in[h % 2], b * (H * 16) + (h // 2 + 1) * 32)
                pe.wait_ge(p_exp, b * (H * S2U) + h * S2U + u + 1)
                r = MROW + 1
                if u < NB:
                    k = slice(P * u, P * u + P)
                    for q0 in range(0, S, HALF):
                        up = min(max(P * u - q0, 0), HALF)
                        if up > 0:
                            mm = pe.matmul(pB[:, q0:q0 + up], K[0:r, s, k], QU[0:r, s, q0:q0 + up], start=True, stop=True)
                        if up < HALF:
                            mm = pe.matmul(pB[:, q0 + up:q0 + HALF], K[0:r, s, k], QL[0:r, s, q0 + up:q0 + HALF], start=True, stop=True)
                else:
                    for blk in range(NB):
                        k = slice(P * blk, P * blk + P)
                        mm = pe.matmul(pB[:, k], K[0:r, s, k], QU[0:r, s, k], start=True, stop=True)
                mm.then_inc(s2_ready, 1)

            def context(b, h, u):
                n = h * S2U + u
                pe.wait_ge(p_mask, b * (H * S2U) + n + 1)
                if u == 0:
                    pe.wait_ge(ctx_evac, b * H + h + 1)
                for kb in ([u] if u < NB else range(NB)):
                    j = VW * (kb % 4)
                    w = HALF if u < NB else P
                    for q0 in (range(0, S, HALF) if u < NB else [P * kb]):
                        mm = pe.matmul(pC[j:j + VW, q0:q0 + w], vext[:, kb, h, :], prob[n % RING][:, q0:q0 + w],
                                       start=(u < 4), stop=(u == NB), skip_group_check=True)
                mm.then_inc(pv_done, 1)

            for j in range(10):
                project(0, j)
            pe.wait_ge(pd, 1)
            super_scores()
            pe.wait_ge(m_done, 1)
            values(0)
            for h in range(AHEAD):
                for n in range(S1U):
                    first_pass(0, h, n)
            pe.wait_ge(m_done, 2)
            row_of_maxima(0, 0)
            with pe.Fori(0, B) as b:
                for h in range(H):
                    for u in range(S2U):
                        second_pass(b, h, u)
                        first_pass(b, h + AHEAD, 2 * u)
                        first_pass(b, h + AHEAD, 2 * u + 1)
                        if u > 0:
                            context(b, h, u - 1)
                        elif h > 0:
                            context(b, h - 1, S2U - 1)
                        if u == 1:
                            claim_m(b, M_ROW[h])
                            row_of_maxima(b, h + 1)
                        if u == 3:
                            claim_m(b, M_FOLD[h])
                            fold_context(b, h - 1, (h - 1) % 2)
                        if h == 1 and u in (4, 5):
                            if u == 4:
                                pe.wait_ge(norm, b * NORM_N + NORM_N)
                            claim_m(b, M_FIN + u - 4)
                            for t in range(4):
                                mm = pe.transpose(pM[:, P * t:P * t + P], vsh[:, 4 * (u - 4) + t, :, :].rearrange("p h d -> p (h d)"), ident[:, :])
                            mm.then_inc(m_ready, 1)
                        if h == 1 and u in (6, 7):
                            claim_m(b, M_FIN + u - 4)
                            for t in range(4):
                                c = P * (4 * (u - 6) + t)
                                mm = pe.matmul(pM[:, P * t:P * t + P], ctxT[:, c:c + P], w_o[:, :], start=True, stop=True)
                            mm.then_inc(m_ready, 1)
                        if h == 2 and u == 4:
                            claim_m(b, M_VB)
                            values(1)
                        if h == 2 and u in (5, 6):
                            claim_m(b, M_VSH + u - 5)
                            values_shifted(u - 5)
                        if h == 3:
                            project(b + 1, u)
                        if h == 4 and u == 0:
                            project(b + 1, 9)
                        if h == 6 and u == 4:
                            pe.wait_ge(pd, (b + 1) * PD_N + 1)
                            claim_m(b, M_C)
                            super_scores()
                        if h == 6 and u == 5:
                            claim_m(b, M_VA)
                            values(0)
                context(b, H - 1, S2U - 1)
            claim_m(B, 0)
            fold_context(B, -1, 1)
            pe.wait_ge(norm, (B + 1) * NORM_N)
            for j in range(4):
                claim_m(B, 1 + j)
                for t in range(4):
                    if j < 2:
                        mm = pe.transpose(pM[:, P * t:P * t + P], vsh[:, 4 * j + t, :, :].rearrange("p h d -> p (h d)"), ident[:, :])
                    else:
                        c = P * (4 * (j - 2) + t)
                        mm = pe.matmul(pM[:, P * t:P * t + P], ctxT[:, c:c + P], w_o[:, :], start=True, stop=True)
                mm.then_inc(m_ready, 1)

        @block.scalar
        def _(act):
            act.sem_inc(p_exp, 1)
            act.sem_inc(ctx_evac, 1)
            act.sem_inc(psup_done, 1)
            act.wait_ge(d_w, D_W)
            act.wait_ge(set_dve, DVE_SET)

            def evacuate(nb, j):
                act.wait_ge(e_ready, nb * 10 + j + 1)
                half = slice(HALF * (j % 2), HALF * (j % 2) + HALF)
                if j < 2:
                    act.activation(xnT[:, half], pE[:, :], ACT.Identity, bias=cols[:, 1:2], scale=cols[:, 0:1]).then_inc(e_done, 1)
                elif j < 4:
                    act.activation(qv[:, half], pE[:, :], ACT.Identity, bias=bias_qv[:, :]).then_inc(e_done, 1)
                    act.activation(qu[:, half], pE[:, :], ACT.Identity, bias=bias_qu[:, :]).then_inc(e_done, 1)
                elif j < 6:
                    act.activation(kc[:, half], pE[:, :], ACT.Identity, bias=cols[:, 3:4]).then_inc(e_done, 1)
                else:
                    act.activation((rp if j < 8 else rq)[:, half], pE[:, :], ACT.Copy).then_inc(e_done, 1)

            def high(nb, i):
                name, src = (("c", qu), ("k", kc), ("gl", g_lo), ("gu", g_up))[i]
                if i < 2:
                    act.wait_ge(e_done, nb * E_N + E_N)
                else:
                    act.wait_ge(pd, nb * PD_N + (4 if i == 2 else 7))
                act.activation(parts[name][0][:, :], src[:, 0:S], ACT.Copy).then_inc(hi_done, 1)

            def context_out(b, h):
                act.wait_ge(pv_done, b * (H * S2U) + (h + 1) * S2U + RING)
                act.activation(ctxp[h % 2][:, :], pC[:, :], ACT.Copy).then_inc(ctx_evac, 1)

            for j in range(10):
                evacuate(0, j)
            for i in range(4):
                high(0, i)
            with act.Fori(0, B) as b:
                for h in range(H):
                    for u in range(S2U):
                        n = h * S2U + u
                        act.wait_ge(s2_ready, b * (H * S2U) + n + 2)
                        act.wait_ge(pv_done, b * (H * S2U) + n + 1)
                        act.activation(prob[n % RING][:, :], pB[:, :], ACT.Exp, scale=SCALE).then_inc(p_exp, 1)
                        if u == 0 and h > 0:
                            context_out(b, h - 1)
                        if h == 3:
                            evacuate(b + 1, u)
                        if h == 4 and u == 0:
                            evacuate(b + 1, 9)
                        if (h, u) == (4, 6):
                            for s in range(SLOTS):
                                act.wait_ge(stk[s], b * (2 * STK) + 2 * STK)
                        if (h, u) in ((4, 6), (4, 7), (4, 8), (5, 0)):
                            high(b + 1, ((4, 6), (4, 7), (4, 8), (5, 0)).index((h, u)))
                    if h == 0:
                        act.wait_ge(norm, b * NORM_N + 2)
                        act.wait_ge(norm, b * NORM_N + NORM_N)
                    act.wait_ge(dsup_done, b * H + h + 1)
                    act.activation(psup[:, h, :], dsup[:, h, :], ACT.Exp, scale=SCALE).then_inc(psup_done, 1)
                context_out(b, H - 1)

        @block.vector
        def _(v):
            for t in (xnT, kc, rp, rq):
                v.memset(t[:, S:S + 1], 0.0).then_inc(set_dve, 1)
            v.memset(ctx_all[:, :, :, :], 1.0).then_inc(set_dve, 1)
            v.memset(psup[:, :, :], 0.0).then_inc(set_dve, 1)
            v.memset(vsh[:, :, :, :], 0.0).then_inc(set_dve, 1)
            v.memset(K[MROW:MROW + 1, :, :].bitcast(F32), 1.0).then_inc(set_dve, 1)
            v.wait_ge(d_w, D_W)
            v.tensor_tensor(bias_qv[:, :], cols[:, 2:3], vu[:, 0:1], ALU.add).then_inc(set_dve, 1)
            v.tensor_tensor(bias_qu[:, :], cols[:, 2:3], vu[:, 1:2], ALU.add).then_inc(set_dve, 1)
            v.wait_ge(d_cst, D_CST)
            v.tensor_copy(parts["pe"][0][:, :], g_lo[:, :]).then_inc(set_dve, 1)
            v.wait_ge(set_dve, 11)
            v.tensor_tensor(parts["pe"][1][:, :], g_lo[:, :], parts["pe"][0][:, :].bitcast(F32), ALU.subtract).then_inc(set_dve, 1)
            v.wait_ge(set_dve, DVE_SET)
            v.wait_ge(set_pool, POOL_SET)

            def stats(nb, t):
                at = nb * LN_N
                if t == 0:
                    v.wait_ge(d_x, nb * 16 + 16)
                v.bn_stats(st6[:, t, :], xt[:, t, :]).then_inc(ln, 1)
                own = known(v, at + 2 * t + 1)
                v.wait_ge(set_dve, DVE_SET)
                v.wait_ge(ln, own)
                v.bn_aggr(mv[:, t, :], st6[:, t, :]).then_inc(ln, 1)

            def normalize(nb, t):
                if t == 0:
                    v.wait_ge(rs_done, nb * RS_N + RS_N)
                v.tensor_scalar(xn[:, t, :], xt[:, t, :], mv[:, t, 0:1], rs[:, 2, t:t + 1], ALU.subtract, ALU.mult).then_inc(ln, 1)

            def positions(nb, i):
                at = nb * PD_N
                if i == 0:
                    v.wait_ge(e_done, nb * E_N + E_N)
                else:
                    v.wait_ge(pd, at + i)
                if i == 0:
                    v.tensor_tensor(t2[:, :], qu[:, :], kc[:, 1:S + 1], ALU.mult).then_inc(pd, 1)
                elif i in (1, 4):
                    src, g, c = (rp[:, 0:S], g_lo, rot[0]) if i == 1 else (rp[:, 1:S + 1], g_up, rot[2])
                    v.tensor_tensor(g[:, :], src, c[:, :], ALU.mult).then_inc(pd, 1)
                elif i in (2, 5):
                    src, c = (rq[:, 0:S], rot[1]) if i == 2 else (rq[:, 1:S + 1], rot[3])
                    v.tensor_tensor(t3[:, :], src, c[:, :], ALU.mult).then_inc(pd, 1)
                else:
                    g = g_lo if i == 3 else g_up
                    v.tensor_tensor(g[:, :], g[:, :], t3[:, :], ALU.add).then_inc(pd, 1)

            def low(nb, i):
                name, src = (("c", qu), ("k", kc), ("gl", g_lo), ("gu", g_up))[i]
                v.wait_ge(hi_done, nb * HI_N + i + 1)
                v.tensor_tensor(parts[name][1][:, :], src[:, 0:S], parts[name][0][:, :].bitcast(F32), ALU.subtract).then_inc(pd, 1)

            def arrived_m(b, i):
                v.wait_ge(m_ready, b * M_N + M_PRO + i + 1)

            def super_out():
                v.tensor_tensor(acc[:, :, :, 3], pM[:, 0:NB * H].rearrange("p (n h) -> p h n", h=H), cmask[:, :, :], ALU.add).then_inc(m_done, 1)

            def values_out(half):
                v.tensor_tensor(vext[:, :, 4 * half:4 * half + 4, 0:D], pM[:, :].rearrange("p (t h d) -> p t h d", h=4, d=D),
                                rows[:, 0, 64 * half:64 * half + 64].rearrange("p (h d) -> p h d", d=D).unsqueeze(1).to_broadcast([P, NB, 4, D]), ALU.add).then_inc(m_done, 1)

            def first_pass(b, h, n):
                s = h % H
                pieces = known(v, b * (H * S1U) + h * S1U + n + 1)
                v.wait_ge(set_pool, POOL_SET)
                v.wait_ge(s1_ready, pieces)
                if n < NB * HPB:
                    qb, k0, _ = piece(n)
                    at = 7 * P - P * qb + k0
                    v.tensor_tensor_reduce(junk[:, n % 2, :], pA[n % 2][:, :], lmask[:, at:at + HALF], 1.0, -3.0e38, ALU.add, ALU.max,
                                           acc[:, s, qb, n % 2:n % 2 + 1]).then_inc(s1_read, 1)
                else:
                    g = n % 2
                    v.tensor_tensor(tmpd[:, :].rearrange("p (n k) -> p n k", k=P), pA[n % 2][:, :].rearrange("p (n k) -> p n k", k=P),
                                    umask[:, :].unsqueeze(1).to_broadcast([P, 4, P]), ALU.add).then_inc(s1_read, 1)
                    v.wait_ge(s1_read, b * (H * S1U) + h * S1U + n + 1)
                    v.tensor_reduce(acc[:, s, 4 * g:4 * g + 4, 2], tmpd[:, :].rearrange("p (n k) -> p n k", k=P), AX.X, ALU.max).then_inc(dred, 1)
                    if g == 0:
                        v.wait_ge(dred, b * (2 * H) + 2 * h + 1)

            def maxima(b, h):
                s = h % H
                v.wait_ge(s1_read, b * (H * S1U) + (h + 1) * S1U)
                v.wait_ge(dred, b * (2 * H) + 2 * (h + 1))
                v.tensor_reduce(mneg[:, s, :], acc[:, s, :, :], AX.X, ALU.max, negate=True).then_inc(mx_done, 1)
                v.wait_ge(mx_done, b * H + h + 1)
                v.tensor_tensor(dsup[:, s, :], acc[:, s, :, 3], mneg[:, s, :].bitcast(F32), ALU.add).then_inc(dsup_done, 1)

            def row_out(h):
                v.tensor_copy(mrow[h % 2][:, :], pM[0:NB, 0:P]).then_inc(m_done, 1)

            def fold_out(h):
                v.tensor_copy(ctx_all[:, :, h % H, :], pM[:, 0:NB * VW].rearrange("p (n w) -> p n w", w=VW)[:, :, 0:D + 1]).then_inc(m_done, 1)

            def normalized(b, i):
                pq = psup[:, :, :].rearrange("p h n -> p n h")
                if i == 0:
                    v.wait_ge(psup_done, b * H + 1)
                else:
                    v.wait_ge(norm, b * NORM_N + i)
                if i == 0:
                    v.tensor_tensor(vsh[:, :, :, :], vsh[:, :, :, :], pq.unsqueeze(3).to_broadcast([P, NB, H, D]), ALU.mult).then_inc(norm, 1)
                elif i == 1:
                    v.tensor_tensor(den[:, :, :], ctx_all[:, :, :, D], pq, ALU.add).then_inc(norm, 1)
                elif i == 2:
                    v.reciprocal(den[:, :, :], den[:, :, :]).then_inc(norm, 1)
                elif i == 3:
                    v.tensor_tensor(vsh[:, :, :, :], vsh[:, :, :, :], ctx_all[:, :, :, 0:D], ALU.add).then_inc(norm, 1)
                else:
                    v.tensor_tensor(vsh[:, :, :, :], vsh[:, :, :, :], den[:, :, :].unsqueeze(3).to_broadcast([P, NB, H, D]), ALU.mult).then_inc(norm, 1)

            def final(j):
                half = slice(HALF * (j % 2), HALF * (j % 2) + HALF)
                if j < 2:
                    v.tensor_copy(ctxT[:, half], pM[:, :]).then_inc(m_done, 1)
                else:
                    x2 = xres[:, 4 * (j - 2):4 * (j - 2) + 4, :]
                    v.tensor_tensor(x2, x2, pM[:, :].rearrange("p (t e) -> p t e", e=E), ALU.add).then_inc(fin, 1)

            def bias_out(b, j):
                v.wait_ge(fin, b * 2 + j - 1)
                x2 = xres[:, 4 * (j - 2):4 * (j - 2) + 4, :]
                v.tensor_tensor(x2, x2, rows[:, 1, :].unsqueeze(1).to_broadcast([P, 4, E]), ALU.add).then_inc(m_done, 1)

            for t in range(NB):
                stats(0, t)
            for t in range(NB):
                normalize(0, t)
            for i in range(7):
                positions(0, i)
            for i in range(4):
                low(0, i)
            v.wait_ge(m_ready, 1)
            super_out()
            v.wait_ge(m_ready, 2)
            values_out(0)
            v.wait_ge(m_done, 1)
            for h in range(AHEAD):
                for n in range(S1U):
                    first_pass(0, h, n)
                maxima(0, h)
            v.wait_ge(m_ready, 3)
            v.tensor_copy(mrow[0][:, :], pM[0:NB, 0:P]).then_inc(m_done, 1)
            with v.Fori(0, B) as b:
                for h in range(H):
                    for u in range(S2U):
                        first_pass(b, h + AHEAD, 2 * u)
                        first_pass(b, h + AHEAD, 2 * u + 1)
                        if u == 1:
                            arrived_m(b, M_ROW[h])
                            row_out(h + 1)
                        if u == 3:
                            arrived_m(b, M_FOLD[h])
                            fold_out(h - 1)
                        if h == 0 and u in (4, 5, 6, 7, 8):
                            if u == 4:
                                v.wait_ge(m_done, b * M_N + M_PRO + M_FOLD[0] + 1)
                            normalized(b, u - 4)
                        if h == 1 and u < 4:
                            stats(b + 1, 2 * u)
                            stats(b + 1, 2 * u + 1)
                        if h == 1 and 4 <= u < 8:
                            arrived_m(b, M_FIN + u - 4)
                            if u == 6:
                                v.wait_ge(d_res, b * 16 + 16)
                            final(u - 4)
                            if u >= 6:
                                bias_out(b, u - 4)
                        if h == 2 and u in (0, 1):
                            for t in range(4 * u, 4 * u + 4):
                                normalize(b + 1, t)
                        if h == 2 and u == 4:
                            arrived_m(b, M_VB)
                            values_out(1)
                        if h == 2 and u in (5, 6):
                            arrived_m(b, M_VSH + u - 5)
                            v.tensor_tensor(vsh[:, 4 * (u - 5):4 * (u - 5) + 4, :, :].rearrange("p t h d -> p t (h d)"), pM[:, :].rearrange("p (t e) -> p t e", e=E),
                                            rows[:, 0, :].unsqueeze(1).to_broadcast([P, 4, E]), ALU.add).then_inc(m_done, 1)
                        if h == 4 and 2 <= u:
                            positions(b + 1, u - 2)
                        if h == 5 and u in (1, 2, 3, 4):
                            low(b + 1, u - 1)
                        if h == 6 and u == 4:
                            arrived_m(b, M_C)
                            super_out()
                        if h == 6 and u == 5:
                            arrived_m(b, M_VA)
                            values_out(0)
                    if h == 6:
                        v.wait_ge(m_done, b * M_N + M_PRO + M_C + 1)
                    maxima(b, h + AHEAD)
            v.wait_ge(m_ready, B * M_N + M_PRO + 1)
            fold_out(H - 1)
            v.wait_ge(m_done, B * M_N + M_PRO + 1)
            for i in range(5):
                normalized(B, i)
            v.wait_ge(d_res, (B + 1) * 16)
            for j in range(4):
                v.wait_ge(m_ready, B * M_N + M_PRO + 2 + j)
                final(j)
                if j >= 2:
                    bias_out(B, j)


def att_consts():
    import numpy as np
    div = np.exp(np.arange(0, E, 2, dtype=np.float32) * np.float32(-np.log(10000.0) / E)).astype(np.float64)
    w = np.repeat(div, 2)[:, None]
    q = np.arange(S)[None, :].astype(np.float64)
    odd = (np.arange(E) % 2 == 1)[:, None]
    sg = np.where(odd, 1.0, -1.0)
    rot = np.stack([np.cos((S - 1 - q) * w), sg * np.sin((S - 1 - q) * w), np.cos((q + 2) * w), -sg * np.sin((q + 2) * w)]).astype(np.float32)
    pe = np.where(odd, np.cos(q * w), np.sin(q * w)).astype(np.float32)
    p = np.arange(P)
    fold = (p[:, None] % VW == np.arange(VW)[None, :]).astype(np.float32)
    hsum = (p[:, None] // D == np.arange(H)[None, :]).astype(np.float32)
    return rot, pe, fold, hsum

def att_layout(i):
    import numpy as np
    a = {k[8:]: np.asarray(v) for k, v in i.items() if k.startswith("L0_attn_")}
    def diag(m):
        out = np.zeros((P, P), np.float32)
        for h in range(H):
            out[D * h:D * h + D, D * h:D * h + D] = m
        return out
    rot, pe, fold, hsum = att_consts()
    swap = np.arange(D) ^ 1
    return {"x": a["inputs"][:B], "wq": diag(a["Wq"]), "wk": diag(a["Wk"]), "wv": diag(a["Wv"]), "wp": diag(a["Wp"].T), "wps": diag(a["Wp"].T[:, swap]),
            "wo": a["Wo"], "cols": np.stack([a["ln_gamma"], a["ln_beta"], np.tile(a["bq"], H), np.tile(a["bk"], H)], 1),
            "vu": np.stack([a["v_bias"].reshape(-1), a["u_bias"].reshape(-1)], 1), "bv": np.tile(a["bv"], H), "bo": a["bo"],
            "rot": rot, "pe": pe, "fold": fold, "hsum": hsum}


def shared_tensors(nc, ctx):
    def sb(name, shape, dt=F32):
        return ctx.enter_context(nc.sbuf_tensor(name, shape, dt))
    return {"w1": sb("w1_all", [P, NX * 2 * F]), "w2": sb("w2_all", [P, NX * (F // P) * E]),
            "b1": sb("b1_all", [P, NX * 2 * F]), "b2": sb("b2_all", [P, NX * E]),
            "ident": sb("ident_f", [P, P]), "gate": sb("gate", [P, TOPK, B * NB]),
            "tile_expert": sb("tile_expert", [P, TABLE]),
            "expert_no": sb("expert_no", [1, TABLE], I32), "row_no": sb("row_no", [1, TABLE], I32)}


def routing_phase(nc, dram, keep):
    ctx = ExitStack()
    with ctx:
        def sb(name, shape, dt=F32):
            return ctx.enter_context(nc.sbuf_tensor(name, shape, dt))

        def sem(name):
            return ctx.enter_context(nc.semaphore(name))

        wr1, wr2 = sb("wr1", [P, RH]), sb("wr2", [RH, NX])
        br1, lns, lnb, br2 = sb("br1", [P, RH]), sb("lns", [P, RH]), sb("lnb", [P, RH]), sb("br2", [P, NX])
        ident = keep["ident"]
        tri, ones = sb("tri", [P, P]), sb("ones", [P, P])
        mhalf, iota8 = sb("mhalf_r", [P, NB]), sb("iota8", [P, NX])
        xb = [sb(f"xb{i}", [P, NB, E]) for i in range(UNROLL)]
        rows = [sb(f"rows_r{i}", [P, NB, ROW]) for i in range(UNROLL)]
        idx = [sb(f"idx{i}", [P, NB, TOPK], U32) for i in range(UNROLL)]
        st, mv, rs = sb("st_r", [P, NB, 6]), sb("mv_r", [P, NB, 2]), sb("rs_r", [P, NB])
        st2, mv2, rs2 = sb("st2", [P, NB, 6]), sb("mv2", [P, NB, 2]), sb("rs2", [P, NB])
        hT, gT = sb("hT", [P, S]), sb("gT_r", [RH, S])
        hr, hg = sb("hr", [P, NB, RH]), sb("hg", [P, NB, RH])
        lg, mx, mi = sb("lg", [P, NB, NX]), sb("mx", [P, NB, NX]), sb("mi", [P, NB, NX], U32)
        dlt, xf = sb("dlt", [P, B * NB]), sb("xf", [P, NB, TOPK])
        oh, both = sb("oh", [P, NB, TOPK, NX]), sb("both", [P, NB, NX])
        pos, prod, posf = sb("pos", [P, NB, NX]), sb("prod", [P, NB, TOPK, NX]), sb("posf", [P, NB, TOPK])
        carry = sb("carry", [P, NX])
        start = sb("start", [P, NX])
        cnt, ti32, tiles = sb("cnt", [P, NX]), sb("ti32", [P, NX], I32), sb("tiles", [P, NX])
        cum, tno = sb("cum", [P, NX]), sb("tno", [P, TABLE])
        past, used = sb("past", [P, TABLE, NX - 1]), sb("used", [P, TABLE, NX - 1])
        first, cap = sb("first", [P, TABLE]), sb("cap", [P, TABLE])
        padrow, padf, padi = sb("padrow", [P, ROW]), sb("padf", [P, NX]), sb("padi", [P, NX], U32)
        pidx = sb("pidx", [P, 1])
        ex = sb("ex", [P, B * NB])

        def pb(name, shape):
            return ctx.enter_context(nc.psum_tensor(name, shape, F32))
        pT, pH, pG = pb("pT", [P, S]), pb("pH", [P, NB * RH]), pb("pG", [RH, S])
        pL, pR = pb("pL", [P, NB * NX]), pb("pR", [P, NB * NX + NX])

        d_w, d_big = sem("router_in"), sem("experts_in")
        d_x = [sem(f"x_in_r{i}") for i in range(UNROLL)]
        setp, setd = sem("set_pool_r"), sem("set_dve_r")
        a_dve, a_rs, a_tr, a_ev = sem("a_dve"), sem("a_rs"), sem("a_tr"), sem("a_ev")
        b_h, b_dve, b_rs, b_gelu, b_gt, b_gev, b_lg = (sem(n) for n in ("b_h", "b_dve", "b_rs", "b_gelu", "b_gt", "b_gev", "b_lg"))
        c_dve, c_rank, scat, rows_free = sem("c_dve"), sem("c_rank"), sem("scattered"), sem("rows_free")
        t_dve, t_exp, t_pad = sem("t_dve"), sem("t_exp"), sem("t_pad")
        block = ctx.enter_context(nc.Block())
        A_N, A_STATS = 2 * NB + NB + 1, 2 * NB
        B_STATS, B_N = 1 + 2 * NB, 1 + 2 * NB + NB + 2
        C_N, C_BOTH, C_IDX = 1 + 2 * NB + 5 + 5, 1 + 2 * NB + 5, 1 + 2 * NB + 5 + 5
        SCAT_N = 16 * NB * TOPK
        D_W, SETP, SETD = 16 * 6, 10, 3
        D_BIG = 16 * (2 * NX + 2)

        @block.sync
        def _(sp):
            for t, n in ((wr1, "wr1"), (wr2, "wr2")):
                sp.dma_start(t[:, :], dram[n]).then_inc(d_w, 16)
            for t, n in ((br1, "br1"), (lns, "lns"), (lnb, "lnb"), (br2, "br2")):
                sp.dma_start(t[:, :], dram[n].partition_broadcast(P)).then_inc(d_w, 16)

            def load(nb, k):
                sp.dma_start(xb[k][:, :, :], dram["x2s"][bass.ds(nb % B + 1, 1)].rearrange("o (t p) e -> p (o t) e", p=P)).then_inc(d_x[k], 16)
            for k in range(UNROLL):
                load(k, k)
            for e in range(NX):
                sp.dma_start(keep["w1"][:, 2 * F * e:2 * F * (e + 1)], dram["w1"][e]).then_inc(d_big, 16)
                sp.dma_start(keep["w2"][:, F * e:F * (e + 1)].rearrange("p (c d) -> p c d", d=E),
                             dram["w2"][e].rearrange("(c p) d -> p c d", p=P)).then_inc(d_big, 16)
            sp.dma_start(keep["b1"][:, :], dram["b1"].partition_broadcast(P)).then_inc(d_big, 16)
            sp.dma_start(keep["b2"][:, :], dram["b2"].partition_broadcast(P)).then_inc(d_big, 16)
            with sp.Fori(0, B // UNROLL) as it:
                for k in range(UNROLL):
                    nb = it * UNROLL + k
                    sp.wait_ge(d_w, D_W)
                    sp.wait_ge(a_dve, known(sp, nb * A_N + A_N))
                    load(nb + UNROLL, k)
            for k in range(UNROLL):
                sp.wait_ge(d_x[k], (B // UNROLL + 1) * 16)
            sp.wait_ge(d_big, D_BIG)

        @block.gpsimd
        def _(po):
            po.memset(ident[:, :], 0.0).then_inc(setp, 1)
            po.memset(tri[:, :], 1.0).then_inc(setp, 1)
            po.memset(mhalf[:, :], -0.5).then_inc(setp, 1)
            po.iota(iota8[:, :], pattern=[[1, NX]], base=0, channel_multiplier=0, allow_small_or_imprecise_dtypes=True).then_inc(setp, 1)
            po.iota(rows[UNROLL - 1][:, :, E], pattern=[[P, NB]], base=-S, channel_multiplier=1, allow_small_or_imprecise_dtypes=True).then_inc(setp, 1)
            po.iota(carry[:, :], pattern=[[REGION, NX]], base=0, channel_multiplier=0, allow_small_or_imprecise_dtypes=True).then_inc(setp, 1)
            po.iota(tno[:, :], pattern=[[1, TABLE]], base=0, channel_multiplier=0, allow_small_or_imprecise_dtypes=True).then_inc(setp, 1)
            po.iota(pidx[:, :], pattern=[[0, 1]], base=0, channel_multiplier=1, allow_small_or_imprecise_dtypes=True).then_inc(setp, 1)
            po.wait_ge(setp, 8)
            po.affine_select(out=ident[:, :], in_=ident[:, :], compare_op=ALU.not_equal, fill=1.0, base=0,
                             pattern=[[-1, P]], channel_multiplier=1).then_inc(setp, 1)
            po.affine_select(out=tri[:, :], in_=tri[:, :], compare_op=ALU.is_gt, fill=0.0, base=0,
                             pattern=[[1, P]], channel_multiplier=-1).then_inc(setp, 1)

            def rstd(done, out, var, eps, stats, stats_n, nb):
                have, mine = known(po, stats_n), known(po, nb * 2 + 1)
                po.wait_ge(setp, SETP)
                po.wait_ge(stats, have)
                po.tensor_scalar(out[:, :], var[:, :, 1], eps, None, ALU.add).then_inc(done, 1)
                po.wait_ge(done, mine)
                po.tensor_tensor(out[:, :], out[:, :], mhalf[:, :], ALU.pow).then_inc(done, 1)

            def rstd_a(nb):
                rstd(a_rs, rs, mv, LN_EPS, a_dve, nb * A_N + A_STATS, nb)

            def rstd_b(nb):
                rstd(b_rs, rs2, mv2, ROUTER_EPS, b_dve, nb * B_N + B_STATS, nb)

            po.sem_inc(rows_free, 1)
            rstd_a(0)
            rstd_b(0)
            rstd_a(1)
            with po.Fori(0, B // UNROLL) as it:
                for k in range(UNROLL):
                    nb = it * UNROLL + k
                    rstd_b(nb + 1)
                    rstd_a(nb + 2)
                    if k > 0:
                        po.wait_ge(scat, nb * SCAT_N)
                        po.sem_inc(rows_free, 2 if k == 1 else 1)
                    placed = known(po, nb * C_N + C_IDX)
                    po.wait_ge(setp, SETP)
                    po.wait_ge(c_dve, placed)
                    for t in range(NB):
                        for j in range(TOPK):
                            po.indirect_dma_start(dram["xs"], bass.IndirectOffsetOnAxis(idx[k][:, t, j:j + 1], 0),
                                                  rows[k][:, t, :], None).then_inc(scat, 16)
            po.wait_ge(t_dve, 4)
            for e in range(NX):
                po.indirect_dma_start(dram["xs"], bass.IndirectOffsetOnAxis(padi[:, e:e + 1], 0), padrow[:, :], None).then_inc(t_pad, 16)
            po.wait_ge(scat, B * SCAT_N)
            po.wait_ge(t_pad, 16 * NX)

        @block.tensor
        def _(pe):
            pe.wait_ge(d_w, D_W)
            pe.wait_ge(setp, SETP)
            pe.wait_ge(setd, SETD)

            def turn(nb, k):
                pe.wait_ge(a_dve, nb * A_N + A_N)
                if not (isinstance(nb, int) and nb == 0):
                    pe.wait_ge(a_ev, nb * 2)
                for t in range(NB):
                    mm = pe.transpose(pT[:, P * t:P * t + P], rows[k][:, t, 0:E], ident[:, :])
                mm.then_inc(a_tr, 1)

            def hidden(nb):
                pe.wait_ge(a_ev, nb * 2 + 2)
                if not (isinstance(nb, int) and nb == 0):
                    pe.wait_ge(b_dve, (nb - 1) * B_N + 1)
                for t in range(NB):
                    mm = pe.matmul(pH[:, RH * t:RH * t + RH], hT[:, P * t:P * t + P], wr1[:, :], start=True, stop=True)
                mm.then_inc(b_h, 1)

            def logits(nb):
                active, read = known(pe, nb + 1), known(pe, nb * 2)
                pe.wait_ge(setd, SETD)
                pe.wait_ge(b_gelu, active)
                if not (isinstance(nb, int) and nb == 0):
                    pe.wait_ge(b_gev, read)
                for t in range(NB):
                    mm = pe.transpose(pG[:, P * t:P * t + P], hg[:, t, :], ident[:, :])
                mm.then_inc(b_gt, 1)
                pe.wait_ge(b_gev, nb * 2 + 2)
                if not (isinstance(nb, int) and nb == 0):
                    pe.wait_ge(c_dve, (nb - 1) * C_N + 1)
                for t in range(NB):
                    mm = pe.matmul(pL[:, NX * t:NX * t + NX], gT[:, P * t:P * t + P], wr2[:, :], start=True, stop=True)
                mm.then_inc(b_lg, 1)

            def ranks(nb):
                pe.wait_ge(c_dve, nb * C_N + C_BOTH)
                pe.matmul(pR[:, 0:NB * NX], tri[:, :], both[:, :, :].rearrange("p t e -> p (t e)"), start=True, stop=False, skip_group_check=True)
                for t in range(NB - 1):
                    w = NB - 1 - t
                    pe.matmul(pR[:, NX * (t + 1):NX * NB].rearrange("p (t e) -> p t e", e=NX), ones[:, :],
                              both[:, t:t + 1, :].to_broadcast([P, w, NX]), start=False, stop=(t == NB - 2), skip_group_check=True)
                for t in range(NB):
                    mm = pe.matmul(pR[:, NX * NB:NX * NB + NX], ones[:, :], both[:, t, :], start=(t == 0), stop=(t == NB - 1), skip_group_check=True)
                mm.then_inc(c_rank, 1)

            turn(0, 0)
            hidden(0)
            logits(0)
            turn(1, 1)
            with pe.Fori(0, B // UNROLL) as it:
                for k in range(UNROLL):
                    nb = it * UNROLL + k
                    hidden(nb + 1)
                    ranks(nb)
                    logits(nb + 1)
                    turn(nb + 2, (k + 2) % UNROLL)

        @block.scalar
        def _(act):
            act.wait_ge(setp, SETP)

            def turned(nb):
                act.wait_ge(a_tr, nb + 1)
                if not (isinstance(nb, int) and nb == 0):
                    act.wait_ge(b_h, nb)
                for i in range(2):
                    act.activation(hT[:, 512 * i:512 * i + 512], pT[:, 512 * i:512 * i + 512], ACT.Copy).then_inc(a_ev, 1)

            def gelu(nb):
                act.wait_ge(b_dve, nb * B_N + B_N)
                if not (isinstance(nb, int) and nb == 0):
                    act.wait_ge(b_gt, nb)
                act.activation(hg[:, :, :], hr[:, :, :], ACT.Gelu_apprx_tanh).then_inc(b_gelu, 1)
                act.wait_ge(b_gt, nb + 1)
                if not (isinstance(nb, int) and nb == 0):
                    act.wait_ge(b_lg, nb)
                for i in range(2):
                    act.activation(gT[:, 512 * i:512 * i + 512], pG[:, 512 * i:512 * i + 512], ACT.Copy).then_inc(b_gev, 1)

            turned(0)
            gelu(0)
            turned(1)
            with act.Fori(0, B // UNROLL) as it:
                for k in range(UNROLL):
                    nb = it * UNROLL + k
                    gelu(nb + 1)
                    turned(nb + 2)
            act.wait_ge(c_dve, B * C_N)
            act.activation(ex[:, :], dlt[:, :], ACT.Exp).then_inc(t_exp, 1)

        @block.vector
        def _(v):
            v.memset(ones[:, :], 1.0).then_inc(setd, 1)
            v.memset(padrow[:, 0:E], 0.0).then_inc(setd, 1)
            v.memset(padrow[:, E + 1:E + 2], -1.0).then_inc(setd, 1)
            v.wait_ge(d_w, D_W)
            v.wait_ge(setp, SETP)
            v.wait_ge(setd, SETD)

            def stats(nb, k, sem_, at, src, st_, mv_):
                for t in range(NB):
                    v.bn_stats(st_[:, t, :], src(t)).then_inc(sem_, 1)
                v.wait_ge(sem_, at + NB)
                for t in range(NB):
                    v.bn_aggr(mv_[:, t, :], st_[:, t, :]).then_inc(sem_, 1)

            def a1(nb, k, m):
                have = known(v, nb * A_N + NB)
                v.wait_ge(d_x[k], m * 16 + 16)
                for t in range(NB):
                    v.bn_stats(st[:, t, :], xb[k][:, t, :]).then_inc(a_dve, 1)
                v.wait_ge(setp, SETP)
                v.wait_ge(a_dve, have)
                for t in range(NB):
                    v.bn_aggr(mv[:, t, :], st[:, t, :]).then_inc(a_dve, 1)

            def a2(nb, k, waits=True):
                if waits:
                    v.wait_ge(rows_free, nb - 1)
                last = rows[(k - 1) % UNROLL][:, :, E]
                v.wait_ge(a_dve, nb * A_N) if not (isinstance(nb, int) and nb == 0) else None
                v.tensor_scalar(rows[k][:, :, E], last, float(S), None, ALU.add).then_inc(a_dve, 1)
                v.wait_ge(a_rs, nb * 2 + 2)
                for t in range(NB):
                    v.tensor_scalar(rows[k][:, t, 0:E], xb[k][:, t, :], mv[:, t, 0:1], rs[:, t:t + 1], ALU.subtract, ALU.mult).then_inc(a_dve, 1)

            def b1(nb):
                have, bias = known(v, nb * B_N + 1 + NB), known(v, nb * B_N + 1)
                v.wait_ge(b_h, nb + 1)
                if not (isinstance(nb, int) and nb == 0):
                    v.wait_ge(b_gelu, nb)
                v.tensor_tensor(hr[:, :, :], pH[:, :].rearrange("p (t e) -> p t e", e=RH),
                                br1[:, :].unsqueeze(1).to_broadcast([P, NB, RH]), ALU.add).then_inc(b_dve, 1)
                v.wait_ge(setp, SETP)
                v.wait_ge(b_dve, bias)
                for t in range(NB):
                    v.bn_stats(st2[:, t, :], hr[:, t, :]).then_inc(b_dve, 1)
                v.wait_ge(setp, SETP)
                v.wait_ge(b_dve, have)
                for t in range(NB):
                    v.bn_aggr(mv2[:, t, :], st2[:, t, :]).then_inc(b_dve, 1)

            def b2(nb):
                v.wait_ge(b_rs, nb * 2 + 2)
                for t in range(NB):
                    v.tensor_scalar(hr[:, t, :], hr[:, t, :], mv2[:, t, 0:1], rs2[:, t:t + 1], ALU.subtract, ALU.mult).then_inc(b_dve, 1)
                v.wait_ge(b_dve, nb * B_N + B_STATS + NB)
                v.tensor_tensor(hr[:, :, :], hr[:, :, :], lns[:, :].unsqueeze(1).to_broadcast([P, NB, RH]), ALU.mult).then_inc(b_dve, 1)
                v.wait_ge(b_dve, nb * B_N + B_STATS + NB + 1)
                v.tensor_tensor(hr[:, :, :], hr[:, :, :], lnb[:, :].unsqueeze(1).to_broadcast([P, NB, RH]), ALU.add).then_inc(b_dve, 1)

            def c1(nb, k):
                at = nb * C_N
                v.wait_ge(b_lg, nb + 1)
                v.tensor_tensor(lg[:, :, :], pL[:, :].rearrange("p (t e) -> p t e", e=NX),
                                br2[:, :].unsqueeze(1).to_broadcast([P, NB, NX]), ALU.add).then_inc(c_dve, 1)
                biased, best = known(v, at + 1), known(v, at + 1 + NB)
                v.wait_ge(setp, SETP)
                v.wait_ge(c_dve, biased)
                for t in range(NB):
                    v.max(mx[:, t, :], lg[:, t, :]).then_inc(c_dve, 1)
                v.wait_ge(setp, SETP)
                v.wait_ge(c_dve, best)
                for t in range(NB):
                    v.max_index(mi[:, t, :], mx[:, t, :], lg[:, t, :]).then_inc(c_dve, 1)
                v.tensor_tensor(dlt[:, bass.ds(nb * NB, NB)], mx[:, :, 1], mx[:, :, 0], ALU.subtract).then_inc(c_dve, 1)
                v.wait_ge(c_dve, at + 2 + 2 * NB)
                v.tensor_copy(xf[:, :, :], mi[:, :, 0:TOPK]).then_inc(c_dve, 1)
                v.wait_ge(c_dve, at + 3 + 2 * NB)
                v.tensor_copy(rows[k][:, :, E + 1], xf[:, :, 0]).then_inc(c_dve, 1)
                v.tensor_tensor(oh[:, :, :, :], xf[:, :, :].unsqueeze(3).to_broadcast([P, NB, TOPK, NX]),
                                iota8[:, :].unsqueeze(1).unsqueeze(1).to_broadcast([P, NB, TOPK, NX]), ALU.is_equal).then_inc(c_dve, 1)
                v.wait_ge(c_dve, at + 5 + 2 * NB)
                v.tensor_tensor(both[:, :, :], oh[:, :, 0, :], oh[:, :, 1, :], ALU.add).then_inc(c_dve, 1)

            def c2(nb, k):
                at = nb * C_N + C_BOTH
                v.wait_ge(c_rank, nb + 1)
                v.tensor_tensor(pos[:, :, :], pR[:, 0:NB * NX].rearrange("p (t e) -> p t e", e=NX),
                                carry[:, :].unsqueeze(1).to_broadcast([P, NB, NX]), ALU.add).then_inc(c_dve, 1)
                v.wait_ge(c_dve, at + 1)
                v.tensor_tensor(carry[:, :], carry[:, :], pR[:, NB * NX:NB * NX + NX], ALU.add).then_inc(c_dve, 1)
                v.wait_ge(c_dve, at + 2)
                v.tensor_tensor(prod[:, :, :, :], oh[:, :, :, :], pos[:, :, :].unsqueeze(2).to_broadcast([P, NB, TOPK, NX]), ALU.mult).then_inc(c_dve, 1)
                v.wait_ge(c_dve, at + 3)
                v.tensor_reduce(posf[:, :, :], prod[:, :, :, :], AX.X, ALU.add).then_inc(c_dve, 1)
                v.wait_ge(c_dve, at + 4)
                v.tensor_copy(idx[k][:, :, :], posf[:, :, :]).then_inc(c_dve, 1)

            a1(0, 0, 0)
            a2(0, 0, False)
            b1(0)
            a1(1, 1, 0)
            b2(0)
            a2(1, 1, False)
            with v.Fori(0, B // UNROLL) as it:
                for k in range(UNROLL):
                    nb = it * UNROLL + k
                    c1(nb, k)
                    b1(nb + 1)
                    a1(nb + 2, (k + 2) % UNROLL, it + (k + 2) // UNROLL)
                    c2(nb, k)
                    b2(nb + 1)
                    a2(nb + 2, (k + 2) % UNROLL)
            v.wait_ge(setp, SETP)
            v.wait_ge(c_dve, B * C_N)
            v.tensor_scalar(padrow[:, E:E + 1], pidx[:, :], float(TOPK * TOKENS), None, ALU.add).then_inc(t_dve, 1)
            v.tensor_tensor(padf[:, :], carry[:, :], pidx[:, :].to_broadcast([P, NX]), ALU.add).then_inc(t_dve, 1)
            v.tensor_scalar(start[:, :], iota8[:, :], float(REGION), None, ALU.mult).then_inc(t_dve, 1)
            v.wait_ge(t_dve, 3)
            v.tensor_copy(padi[:, :], padf[:, :]).then_inc(t_dve, 1)
            v.tensor_tensor(cnt[:, :], carry[:, :], start[:, :], ALU.subtract).then_inc(t_dve, 1)
            v.wait_ge(t_dve, 5)
            v.tensor_scalar(ti32[:, :], cnt[:, :], float(P - 1), None, ALU.add).then_inc(t_dve, 1)
            v.wait_ge(t_dve, 6)
            v.tensor_scalar(ti32[:, :], ti32[:, :], 7, None, ALU.arith_shift_right).then_inc(t_dve, 1)
            v.wait_ge(t_dve, 7)
            v.tensor_copy(tiles[:, :], ti32[:, :]).then_inc(t_dve, 1)
            v.wait_ge(t_dve, 8)
            v.tensor_copy(cum[:, 0:1], tiles[:, 0:1]).then_inc(t_dve, 1)
            for e in range(1, NX):
                v.wait_ge(t_dve, 8 + e)
                v.tensor_tensor(cum[:, e:e + 1], cum[:, e - 1:e], tiles[:, e:e + 1], ALU.add).then_inc(t_dve, 1)
            v.wait_ge(t_dve, 16)
            every = lambda a: a.unsqueeze(1).to_broadcast([P, TABLE, NX - 1])
            v.tensor_tensor(past[:, :, :], tno[:, :].unsqueeze(2).to_broadcast([P, TABLE, NX - 1]), every(cum[:, 0:NX - 1]), ALU.is_ge).then_inc(t_dve, 1)
            v.wait_ge(t_dve, 17)
            v.tensor_reduce(keep["tile_expert"][:, :], past[:, :, :], AX.X, ALU.add).then_inc(t_dve, 1)
            v.tensor_tensor(used[:, :, :], past[:, :, :], every(tiles[:, 0:NX - 1]), ALU.mult).then_inc(t_dve, 1)
            v.wait_ge(t_dve, 19)
            v.tensor_reduce(first[:, :], used[:, :, :], AX.X, ALU.add).then_inc(t_dve, 1)
            v.tensor_scalar(cap[:, :], keep["tile_expert"][:, :], float(NX - 1), -float(REGION), ALU.subtract, ALU.mult).then_inc(t_dve, 1)
            v.wait_ge(t_dve, 21)
            v.tensor_tensor(first[:, :], tno[:, :], first[:, :], ALU.subtract).then_inc(t_dve, 1)
            v.tensor_scalar(cap[:, :], cap[:, :], cnt[:, NX - 1:NX], None, ALU.add).then_inc(t_dve, 1)
            v.wait_ge(t_dve, 23)
            v.tensor_scalar(first[:, :], first[:, :], float(P), None, ALU.mult).then_inc(t_dve, 1)
            v.wait_ge(t_dve, 24)
            v.tensor_tensor(first[:, :], first[:, :], cap[:, :], ALU.min).then_inc(t_dve, 1)
            v.wait_ge(t_dve, 25)
            v.tensor_scalar(cap[:, :], keep["tile_expert"][:, :], float(REGION), None, ALU.mult).then_inc(t_dve, 1)
            v.wait_ge(t_dve, 26)
            v.tensor_tensor(keep["row_no"][:, :], first[0:1, :], cap[0:1, :], ALU.add).then_inc(t_dve, 1)
            v.tensor_copy(keep["expert_no"][:, :], keep["tile_expert"][0:1, :]).then_inc(t_dve, 1)
            v.wait_ge(t_exp, 1)
            g0, g1 = keep["gate"][:, 0, :], keep["gate"][:, 1, :]
            v.tensor_scalar(g0, ex[:, :], 1.0, None, ALU.add).then_inc(t_dve, 1)
            v.wait_ge(t_dve, 29)
            v.reciprocal(g0, g0).then_inc(t_dve, 1)
            v.wait_ge(t_dve, 30)
            v.tensor_tensor(g1, ex[:, :], g0, ALU.mult).then_inc(t_dve, 1)
            v.wait_ge(t_dve, 31)


def expert_phase(nc, dram, keep):
    ctx = ExitStack()
    with ctx:
        def sb(name, shape, dt=F32):
            return ctx.enter_context(nc.sbuf_tensor(name, shape, dt))

        def pb(name, shape):
            return ctx.enter_context(nc.psum_tensor(name, shape, F32))

        def sem(name):
            return ctx.enter_context(nc.semaphore(name))
        two = range(2)
        ident = keep["ident"]
        xg = [sb(f"xg{i}", [P, ROW]) for i in two]
        xT = [sb(f"xT{i}", [P, P]) for i in two]
        gate_in, lin = [sb(f"gate_in{i}", [P, F]) for i in two], [sb(f"lin{i}", [P, F]) for i in two]
        gl, g = [sb(f"gl{i}", [P, F]) for i in two], [sb(f"g{i}", [P, F]) for i in two]
        gT = [sb(f"gT{i}", [P, F]) for i in two]
        yb = [sb(f"yb{i}", [P, E]) for i in two]
        other, dst = [sb(f"other{i}", [P, 1]) for i in two], [sb(f"dst{i}", [P, 1], U32) for i in two]
        pLin, pGate = [pb(f"pLin{i}", [P, F]) for i in two], [pb(f"pGate{i}", [P, F]) for i in two]
        pTurn = pb("pTurn", [P, P])
        pGT = pb("pGT", [P, F])
        pY = [pb(f"pY{i}", [P, E]) for i in two]
        x_in = [sem(f"rows_in{i}") for i in two]
        x_tr, x_ev, up = sem("x_turned"), sem("x_evacuated"), sem("up_done")
        b2_done, b1_done, gelu, prod, places = sem("gate_biased"), sem("linear_biased"), sem("gelu_done"), sem("product_done"), sem("places")
        gt, gt_ev, down, y_done = sem("g_turned"), sem("g_evacuated"), sem("down_done"), sem("y_done")
        going = sem("going")
        y_out = [sem(f"y_out{i}") for i in two]
        block = ctx.enter_context(nc.Block())
        STEPS = TILES // 2

        def first(i, n=1):
            return isinstance(i, int) and i < n

        def load_expert(eng, i):
            return eng.value_load(keep["expert_no"][0:1, bass.ds(i, 1)], min_val=0, max_val=NX - 1)

        @block.sync
        def _(sp):
            def load(i, k, m):
                if not first(i, 2):
                    sp.wait_ge(x_tr, known(sp, i - 1))
                    sp.wait_ge(places, known(sp, i * 2 - 2))
                row = sp.value_load(keep["row_no"][0:1, bass.ds(i, 1)], min_val=0, max_val=NX * REGION - P)
                sp.dma_start(xg[k][:, :], dram["xs"][bass.ds(row, P), :]).then_inc(x_in[k], 16)
            load(0, 0, 0)
            load(1, 1, 0)
            load(2, 0, 1)
            load(3, 1, 1)
            with sp.Fori(1, STEPS) as it:
                for k in two:
                    load(it * 2 + k + 2, k, it + 1)
            for k in two:
                sp.wait_ge(x_in[k], (STEPS + 1) * 16)

        @block.gpsimd
        def _(po):
            def scatter(i, k):
                outputs = known(po, i + 1)
                po.wait_ge(going, 1)
                po.wait_ge(y_done, outputs)
                po.indirect_dma_start(dram["ys"], bass.IndirectOffsetOnAxis(dst[k][:, :], 0), yb[k][:, :], None).then_inc(y_out[k], 16)

            po.sem_inc(going, 1)
            for k in two:
                scatter(k, k)
            with po.Fori(1, STEPS) as it:
                for k in two:
                    scatter(it * 2 + k, k)
            for k in two:
                po.wait_ge(y_out[k], STEPS * 16)

        @block.tensor
        def _(pe):
            def turn(i, k, m):
                pe.wait_ge(x_in[k], (m + 1) * 16)
                if not first(i):
                    pe.wait_ge(x_ev, i)
                pe.transpose(pTurn[:, :], xg[k][:, 0:E], ident[:, :]).then_inc(x_tr, 1)

            def up_half(i, k, ex, half):
                if half == 1:
                    if not first(i, 2):
                        pe.wait_ge(b2_done, i - 1)
                    pe.wait_ge(x_ev, i + 1)
                    dst_ = pGate[k]
                else:
                    if not first(i, 2):
                        pe.wait_ge(b1_done, i - 1)
                    dst_ = pLin[k]
                pe.matmul(dst_[:, :], xT[k][:, :], keep["w1"][:, bass.ds(ex * (2 * F) + half * F, F)], start=True, stop=True).then_inc(up, 1)

            def turn_g(i, k):
                pe.wait_ge(prod, i + 1)
                if not first(i):
                    pe.wait_ge(gt_ev, i)
                for c in range(F // P):
                    mm = pe.transpose(pGT[:, P * c:P * c + P], g[k][:, P * c:P * c + P], ident[:, :])
                mm.then_inc(gt, 1)

            def out(i, k, ex):
                pe.wait_ge(gt_ev, i + 1)
                if not first(i, 2):
                    pe.wait_ge(y_done, i - 1)
                for c in range(F // P):
                    mm = pe.matmul(pY[k][:, :], gT[k][:, P * c:P * c + P], keep["w2"][:, bass.ds(ex * F + c * E, E)], start=(c == 0), stop=(c == F // P - 1))
                mm.then_inc(down, 1)

            turn(0, 0, 0)
            turn(1, 1, 0)
            ex = load_expert(pe, 0)
            up_half(0, 0, ex, 1)
            up_half(0, 0, ex, 0)

            def step(it, k):
                i = it * 2 + k
                this, nxt = load_expert(pe, i), load_expert(pe, i + 1)
                up_half(i + 1, 1 - k, nxt, 1)
                turn_g(i, k)
                up_half(i + 1, 1 - k, nxt, 0)
                turn(i + 2, k, it + 1)
                out(i, k, this)

            for k in two:
                step(0, k)
            with pe.Fori(1, STEPS) as it:
                for k in two:
                    step(it, k)

        @block.scalar
        def _(act):
            def turned(i, k):
                act.wait_ge(x_tr, i + 1)
                if not first(i, 2):
                    act.wait_ge(up, i * 2 - 2)
                act.activation(xT[k][:, :], pTurn[:, :], ACT.Copy).then_inc(x_ev, 1)

            def gelu_of(i, k):
                act.wait_ge(b2_done, i + 1)
                if not first(i, 2):
                    act.wait_ge(prod, i - 1)
                act.activation(gl[k][:, :], gate_in[k][:, :], ACT.Gelu_apprx_tanh).then_inc(gelu, 1)

            def turned_g(i, k):
                act.wait_ge(gt, i + 1)
                if not first(i, 2):
                    act.wait_ge(down, i - 1)
                act.activation(gT[k][:, :], pGT[:, :], ACT.Copy).then_inc(gt_ev, 1)

            turned(0, 0)
            turned(1, 1)
            gelu_of(0, 0)

            def step(i, k):
                turned_g(i, k)
                turned(i + 2, k)
                gelu_of(i + 1, 1 - k)

            for k in two:
                step(k, k)
            with act.Fori(1, STEPS) as it:
                for k in two:
                    step(it * 2 + k, k)

        @block.vector
        def _(v):
            def biases(i, k, ex):
                if not first(i, 2):
                    v.wait_ge(gelu, i - 1)
                v.wait_ge(up, i * 2 + 1)
                v.tensor_tensor(gate_in[k][:, :], pGate[k][:, :], keep["b1"][:, bass.ds(ex * (2 * F) + F, F)], ALU.add).then_inc(b2_done, 1)
                v.wait_ge(up, i * 2 + 2)
                v.tensor_tensor(lin[k][:, :], pLin[k][:, :], keep["b1"][:, bass.ds(ex * (2 * F), F)], ALU.add).then_inc(b1_done, 1)

            def place(i, k, m):
                if not first(i, 2):
                    v.wait_ge(y_out[k], m * 16)
                v.wait_ge(x_in[k], m * 16 + 16)
                v.tensor_scalar(other[k][:, :], xg[k][:, E + 1:E + 2], keep["tile_expert"][:, bass.ds(i, 1)], float(TOKENS), ALU.not_equal, ALU.mult).then_inc(places, 1)
                v.wait_ge(places, i * 2 + 1)
                v.tensor_tensor(dst[k][:, :], xg[k][:, E:E + 1], other[k][:, :], ALU.add).then_inc(places, 1)

            def product(i, k):
                v.wait_ge(gelu, i + 1)
                v.wait_ge(b1_done, i + 1)
                if not first(i, 2):
                    v.wait_ge(gt, i - 1)
                v.tensor_tensor(g[k][:, :], lin[k][:, :], gl[k][:, :], ALU.mult).then_inc(prod, 1)

            def result(i, k, ex):
                v.wait_ge(down, i + 1)
                v.tensor_tensor(yb[k][:, :], pY[k][:, :], keep["b2"][:, bass.ds(ex * E, E)], ALU.add).then_inc(y_done, 1)

            ex = load_expert(v, 0)
            biases(0, 0, ex)
            place(0, 0, 0)
            product(0, 0)

            def step(it, k):
                i = it * 2 + k
                this, nxt = load_expert(v, i), load_expert(v, i + 1)
                biases(i + 1, 1 - k, nxt)
                place(i + 1, 1 - k, it + k)
                product(i + 1, 1 - k)
                result(i, k, this)

            for k in two:
                step(0, k)
            with v.Fori(1, STEPS) as it:
                for k in two:
                    step(it, k)


def combine_phase(nc, dram, keep):
    ctx = ExitStack()
    with ctx:
        def sb(name, shape, dt=F32):
            return ctx.enter_context(nc.sbuf_tensor(name, shape, dt))

        def sem(name):
            return ctx.enter_context(nc.semaphore(name))
        x2 = [sb(f"x2_{b}", [P, NB, E]) for b in range(B)]
        y = [[sb(f"y{j}_{b}", [P, NB, E]) for b in range(B)] for j in range(TOPK)]
        d_in = [sem(f"sum_in{b}") for b in range(B)]
        s_dve, d_out = sem("summed"), sem("out_done")
        block = ctx.enter_context(nc.Block())

        @block.sync
        def _(sp):
            for b in range(B):
                sp.dma_start(x2[b][:, :, :], dram["x2s"][b + 1].rearrange("(t p) e -> p t e", p=P)).then_inc(d_in[b], 16)
                for j in range(TOPK):
                    lo = TOKENS * j + S * b
                    sp.dma_start(y[j][b][:, :, :], dram["ys"][lo:lo + S].rearrange("(t p) e -> p t e", p=P)).then_inc(d_in[b], 16)
            sp.wait_ge(d_out, B * 16)

        @block.vector
        def _(v):
            n = 0
            for b in range(B):
                v.wait_ge(d_in[b], 3 * 16)
                for j in range(TOPK):
                    for t in range(NB):
                        c = b * NB + t
                        if j and t == 0:
                            v.wait_ge(s_dve, n)
                        v.scalar_tensor_tensor(x2[b][:, t, :], y[j][b][:, t, :], keep["gate"][:, j, c:c + 1], x2[b][:, t, :], ALU.mult, ALU.add).then_inc(s_dve, 1)
                        n += 1

        @block.scalar
        def _(act):
            for b in range(B):
                act.wait_ge(s_dve, (b + 1) * TOPK * NB)
                act.dma_start(dram["out"][b].rearrange("(t p) e -> p t e", p=P), x2[b][:, :, :]).then_inc(d_out, 16)


def ffn_layout(i):
    import numpy as np
    a = {k[7:]: np.asarray(v) for k, v in i.items() if k.startswith("L0_ffn_")}
    return {"wr1": a["Wr1"], "br1": a["br1"], "lns": a["ln_scale"], "lnb": a["ln_bias"], "wr2": a["Wr2"], "br2": a["br2"],
            "w1": a["W1"], "w2": a["W2"], "b1": a["b1"].reshape(-1), "b2": a["b2"].reshape(-1)}


def kernel(**inputs):
    import numpy as np
    import concourse.bacc as bacc
    from concourse.bass_utils import run_bass_kernel_spmd as run
    nc = bacc.Bacc("TRN2", target_bir_lowering=False, num_devices=1)
    arrays = {k: np.ascontiguousarray(v) for k, v in {**att_layout(inputs), **ffn_layout(inputs)}.items()}
    dram = {k: nc.dram_tensor("in_" + k, v.shape, F32, kind="ExternalInput").ap() for k, v in arrays.items()}
    dram["out"] = nc.dram_tensor("out", [B, S, E], F32, kind="ExternalOutput").ap()
    dram["x2s"] = nc.dram_tensor("after_attention", [B + 1, S, E], F32).ap()
    dram["xs"] = nc.dram_tensor("routed_rows", [NX * REGION, ROW], F32).ap()
    dram["ys"] = nc.dram_tensor("expert_rows", [TOPK * TOKENS + TOKENS + P, E], F32).ap()
    attention_phase(nc, dram)
    with ExitStack() as ctx:
        keep = shared_tensors(nc, ctx)
        routing_phase(nc, dram, keep)
        expert_phase(nc, dram, keep)
        combine_phase(nc, dram, keep)
    return run(nc, [{"in_" + k: v for k, v in arrays.items()}], core_ids=[0]).results[0]["out"]
```

```python
from contextlib import ExitStack

import concourse.bass as bass
from concourse import mybir

F32, F32R, BF16 = mybir.dt.float32, mybir.dt.float32r, mybir.dt.bfloat16
I32, U32 = mybir.dt.int32, mybir.dt.uint32
ALU = mybir.AluOpType
ACT = mybir.ActivationFunctionType
AX = mybir.AxisListType

B, S, E, H = 8, 1024, 128, 8
D = E // H
P = 128
NB = S // P
SCALE = float(E) ** -0.5
LN_EPS = 1e-5
FAR = -1.0e30
HALF = 512
HPB = S // HALF
S1U = NB * HPB + HPB
S2U = NB + 1
S1_BUFS = 3
RING = 4
LATE = 2
SLOTS = 4
AHEAD = 2
FEAT = 2 * D
KROWS = 3 * FEAT
MROW = KROWS
STK = 6 * 16
STRIPS = 4
VW = 32
RH = 64
NX = 8
TOPK = 2
F = 512
ROUTER_EPS = 1e-6
TOKENS = B * S
REGION = TOKENS + P
ROW = E + 2
TILES = TOPK * TOKENS // P + NX
TABLE = TILES + 4
TURNS = 4
UNROLL = 4


def known(eng, value):
    return value if isinstance(value, int) else eng.to_reg(value)


def attention_phase(nc, dram):
    ctx = ExitStack()
    with ctx:
        def sb(name, shape, dt=F32):
            return ctx.enter_context(nc.sbuf_tensor(name, shape, dt))

        def pb(name, shape):
            return ctx.enter_context(nc.psum_tensor(name, shape, F32))

        def sem(name):
            return ctx.enter_context(nc.semaphore(name))

        w_q, w_k, w_v, w_p, w_ps, w_o = (sb(n, [P, P]) for n in ("w_q", "w_k", "w_v", "w_p", "w_ps", "w_o"))
        cols = sb("cols", [P, 5])
        bv_wide = sb("bv_wide", [P, P])
        bias_qv, bias_qu = sb("bias_qv", [P, 1]), sb("bias_qu", [P, 1])
        bo_rows = sb("bo_rows", [P, E])
        vu = sb("vu", [P, 2])
        rot = [sb(n, [P, S]) for n in ("cos_lo", "sin_lo", "cos_up", "sin_up")]
        ident, hsum = sb("ident", [P, P]), sb("hsum", [P, H])
        lmask, umask = sb("lmask", [P, 15 * P], BF16), sb("umask", [P, P])
        cmask = sb("cmask", [P, H, NB])
        xt = sb("xt", [P, NB, E])
        st6, mv, rs = sb("st6", [P, NB, 6]), sb("mv", [P, NB, 2]), sb("rs", [P, 3, NB])
        mhalf = sb("mhalf", [P, NB])
        xnT = sb("xnT", [P, S + 1])
        qv, qu, kc = sb("qv", [P, S]), sb("qu", [P, S]), sb("kc", [P, S + 1])
        rp, rq = sb("rp", [P, S + 1]), sb("rq", [P, S + 1])
        g_lo, g_up, t2, t3 = (sb(n, [P, S]) for n in ("g_lo", "g_up", "t2", "t3"))
        xn = g_up[:, :].rearrange("p (t e) -> p t e", e=E)
        parts = {n: (sb(n + "_h", [P, S], F32R), sb(n + "_l", [P, S], F32R)) for n in ("c", "k", "gl", "gu", "pe")}
        QL, QU, K = (sb(n, [P, SLOTS, S], F32R) for n in ("QL", "QU", "K"))
        prob = [sb(f"prob{i}", [P, S]) for i in range(RING)]
        ctxp = sb("ctxp", [P, S // STRIPS])
        ctx_all = sb("ctx_all", [P, NB, H, D + 1])
        vext = sb("vext", [P, NB, H, VW])
        vsh = sb("vsh", [P, NB, H, D])
        acc = sb("acc", [P, H, NB, 4])
        mneg = sb("mneg", [P, H, NB], F32R)
        dsup, psup = sb("dsup", [P, H, NB]), sb("psup", [P, H, NB])
        den = sb("den", [P, NB, H])
        mrow = [sb(f"mrow{i}", [NB, P], F32R) for i in range(2)]
        junk = sb("junk", [P, S1_BUFS, HALF], BF16)
        ctxT = t3
        xres = sb("xres", [P, NB, E])
        pA = [pb(f"pA{i}", [P, HALF]) for i in range(S1_BUFS)]
        pB, pC = pb("pB", [P, S]), pb("pC", [P, S // STRIPS])
        pM, pE = pb("pM", [P, HALF]), pb("pE", [P, HALF])

        d_w, d_cst, d_x, d_res, d_x2 = sem("weights_in"), sem("constants_in"), sem("x_in"), sem("residual_in"), sem("x2_out")
        set_pool, set_dve = sem("set_pool"), sem("set_dve")
        s1_ready, s1_read = sem("s1_ready"), sem("s1_read")
        mx_done, dsup_done = sem("mx_done"), sem("dsup_done")
        mrow_in = [sem(f"mrow_in{i}") for i in range(2)]
        s2_ready, p_exp, p_mask, pv_done = sem("s2_ready"), sem("p_exp"), sem("p_mask"), sem("pv_done")
        ctx_evac, psup_done = sem("ctx_evac"), sem("psup_done")
        m_ready, m_done, w_ready, w_done = sem("m_ready"), sem("m_done"), sem("w_ready"), sem("w_done")
        e_ready, e_done, hi_done = sem("e_ready"), sem("e_done"), sem("hi_done")
        ln, low_done, pos, norm, rs_done, res_done = (sem(n) for n in ("ln", "low_done", "positions", "norm", "rs_done", "residual_biased"))
        upper = sem("first_upper_form")
        stk, stored = [sem(f"stk{i}") for i in range(SLOTS)], sem("operands_stored")
        block = ctx.enter_context(nc.Block())

        LN_N, LOW_N, POS_N, NORM_N, HI_N, RS_N = 3 * NB, 4, 14, 5, 4, 7
        E_AT = [1, 2, 4, 6, 7, 8, 9, 10, 11, 12]
        E_N = E_AT[-1]
        M_ORDER = {(h, u): name for h in range(H) for u, name in ((1, "row"), (3, "context"))}
        M_ORDER.update({(0, 6): "values 1", (1, 5): "project 1", (1, 7): "shifted 1", (6, 7): "values 0"})
        W_ORDER = {(1, 0): "turn 0", (1, 2): "turn 1", (1, 4): "project 0", (1, 6): "shifted 0", (6, 5): "super"}
        SPREAD = {"values 1": ((0, 5), (0, 6)), "values 0": ((6, 6), (6, 7)), "super": ((6, 0), (6, 2), (6, 4), (6, 5))}
        PARTS = {**{place: (name, 0, 1) for order in (M_ORDER, W_ORDER) for place, name in order.items() if name not in SPREAD},
                 **{place: (name, i, len(places)) for name, places in SPREAD.items() for i, place in enumerate(places)}}
        HIGH_AT = ((3, 3), (3, 4), (4, 1), (4, 6))
        LOW_AT = ((3, 4), (3, 5), (4, 2), (4, 7))
        NORMALIZE_AT = (1, 4, 5, 6, 7)
        COPIES = ("values 0", "values 1", "turn 0", "turn 1", "shifted 0", "shifted 1")
        M_PLACES = sorted(M_ORDER)
        M_PRO, M_N = 4, len(M_PLACES)
        M_IDX = {place: n for n, place in enumerate(M_PLACES)}
        M_OF = {M_ORDER[place]: n for place, n in M_IDX.items()}
        W_OF = {W_ORDER[place]: n for n, place in enumerate(sorted(W_ORDER))}
        W_PRO, W_N = 1, len(W_ORDER)
        PLACES = {"c": ((0, 0), (1, 0)), "k": ((2, 0),), "pe": ((2, 1),), "gl": ((0, 1),), "gu": ((1, 1),)}
        ST_N = 16 * 2 * sum(len(p) for p in PLACES.values())
        DVE_SET, DVE_BIAS, POOL_SET = 14, 12, 15
        D_W, D_CST = 16 * 9, 16 * 6

        def piece(n):
            qb, k0 = n // HPB, (n % HPB) * HALF
            return qb, k0, min(max(P * (qb + 1) - k0, 0), HALF)

        @block.sync
        def _(sp):
            sp.dma_start(xt[:, :, :], dram["x"][0].rearrange("(t p) e -> p t e", p=P)).then_inc(d_x, 16)
            for t, n in ((w_q, "wq"), (w_k, "wk"), (w_v, "wv"), (w_p, "wp"), (w_ps, "wps"), (w_o, "wo")):
                sp.dma_start(t[:, :], dram[n]).then_inc(d_w, 16)
            sp.dma_start(cols[:, :], dram["cols"]).then_inc(d_w, 16)
            sp.dma_start(vu[:, :], dram["vu"]).then_inc(d_w, 16)
            sp.dma_start(bo_rows[:, :], dram["bo"].partition_broadcast(P)).then_inc(d_w, 16)
            for i, t in enumerate(rot):
                sp.dma_start(t[:, :], dram["rot"][i]).then_inc(d_cst, 16)
            sp.dma_start(g_lo[:, :], dram["pe"]).then_inc(d_cst, 16)
            sp.dma_start(hsum[:, :], dram["hsum"]).then_inc(d_cst, 16)

            def store(nb, names):
                for name in names:
                    for op, row in PLACES[name]:
                        for low in range(2):
                            sp.dma_start(dram["operands"][bass.ds(nb, 1), op, :, 2 * low + row, :, :].rearrange("o h d s -> (o h) d s"),
                                         parts[name][low][:, :].bitcast(F32)).then_inc(stored, 16)

            def stack(nb, h):
                s = h % SLOTS
                for op, dst in enumerate((QL, QU, K)):
                    split = FEAT if dst is K else 2 * FEAT
                    for lo, hi in ((0, split), (split, KROWS)):
                        sp.dma_start(dst[lo:hi, s, :].bitcast(F32),
                                     dram["operands"][bass.ds(nb, 1), op, h % H, 0:(hi - lo) // D, :, :].rearrange("o g d s -> (o g) d s")).then_inc(stk[s], 16)

            def maximum_row(h):
                s = h % SLOTS
                for dst in (QL, QU):
                    sp.dma_start(dst[MROW:MROW + 1, s, :].bitcast(F32).rearrange("o (n p) -> o n p", p=P),
                                 mrow[h % 2][:, :].bitcast(F32)).then_inc(mrow_in[h % 2], 16)

            sp.sem_inc(d_x2, 16)
            sp.wait_ge(set_dve, DVE_SET)
            sp.wait_ge(ln, LN_N)
            sp.dma_start(xt[:, :, :], dram["x"][1 % B].rearrange("(t p) e -> p t e", p=P)).then_inc(d_x, 16)
            for names, n in ((("c", "k", "pe"), 2), (("gl",), 3), (("gu",), 4)):
                sp.wait_ge(hi_done, n)
                sp.wait_ge(low_done, n)
                store(0, names)
            sp.wait_ge(stored, ST_N)
            for h in range(3):
                stack(0, h)
            sp.wait_ge(m_done, M_PRO)
            maximum_row(0)
            with sp.Fori(0, B) as b:
                for h in range(H):
                    if h == 0:
                        written = known(sp, b * 16 + 16)
                        sp.wait_ge(set_dve, DVE_SET)
                        sp.wait_ge(d_x2, written)
                        sp.dma_start(xres[:, :, :], dram["x"][bass.ds((b + B - 1) % B, 1)].rearrange("o (t p) e -> p (o t) e", p=P)).then_inc(d_res, 16)
                    if h == 3:
                        normed = known(sp, (b + 2) * LN_N)
                        sp.wait_ge(set_dve, DVE_SET)
                        sp.wait_ge(ln, normed)
                        sp.dma_start(xt[:, :, :], dram["x"][bass.ds((b + 2) % B, 1)].rearrange("o (t p) e -> p (o t) e", p=P)).then_inc(d_x, 16)
                    through, in_dram = known(sp, HPB * (b * (H * S2U) + h * S2U) + 1), known(sp, (b + 2) * ST_N)
                    sp.wait_ge(set_dve, DVE_SET)
                    sp.wait_ge(s2_ready, through)
                    if h + 3 == H:
                        sp.wait_ge(stored, in_dram)
                    stack(b + (h + 3) // H, h + 3)
                    sp.wait_ge(m_done, b * M_N + M_PRO + M_IDX[h, 1] + 1)
                    maximum_row(h + 1)
                    if h in (3, 4):
                        highs, lows = known(sp, (b + 1) * HI_N + 2 * (h - 2)), known(sp, (b + 1) * LOW_N + 2 * (h - 2))
                        sp.wait_ge(set_dve, DVE_SET)
                        sp.wait_ge(hi_done, highs)
                        sp.wait_ge(low_done, lows)
                        store(b + 1, ("c", "k", "pe") if h == 3 else ("gl", "gu"))
                    if h == 2:
                        sp.wait_ge(m_done, b * M_N + M_PRO + M_OF["project 1"] + 1)
                        sp.dma_start(dram["x2s"][bass.ds(b, 1)].rearrange("o (t p) e -> p (o t) e", p=P), xres[:, :, :]).then_inc(d_x2, 16)
            sp.wait_ge(d_x2, (B + 1) * 16)
            sp.dma_start(xres[:, :, :], dram["x"][B - 1].rearrange("(t p) e -> p t e", p=P)).then_inc(d_res, 16)
            sp.wait_ge(m_done, B * M_N + M_PRO + 5)
            sp.dma_start(dram["x2s"][B].rearrange("(t p) e -> p t e", p=P), xres[:, :, :]).then_inc(d_x2, 16)
            sp.wait_ge(d_x2, (B + 2) * 16)
            for s in range(SLOTS):
                sp.wait_ge(stk[s], (2 * B + (s < 3)) * STK)
            for i in range(2):
                sp.wait_ge(mrow_in[i], (4 * B + 1 - i) * 32)
            sp.wait_ge(stored, (B + 1) * ST_N)
            sp.wait_ge(d_x, (B + 2) * 16)

        @block.gpsimd
        def _(po):
            po.memset(ident[:, :], 0.0).then_inc(set_pool, 1)
            po.memset(lmask[:, :], 0.0).then_inc(set_pool, 1)
            po.memset(umask[:, :], 0.0).then_inc(set_pool, 1)
            po.memset(cmask[:, :, :], 0.0).then_inc(set_pool, 1)
            po.memset(vext[:, :, :, :], 0.0).then_inc(set_pool, 1)
            for i in range(1, RING):
                po.memset(prob[i][:, :], 1.0).then_inc(set_pool, 1)
            po.memset(mhalf[:, :], -0.5).then_inc(set_pool, 1)
            po.wait_ge(set_pool, 9)
            po.affine_select(out=ident[:, :], in_=ident[:, :], compare_op=ALU.not_equal, fill=1.0, base=0,
                             pattern=[[-1, P]], channel_multiplier=1).then_inc(set_pool, 1)
            po.affine_select(out=lmask[:, 7 * P:8 * P], in_=lmask[:, 7 * P:8 * P], compare_op=ALU.is_ge, fill=FAR, base=0,
                             pattern=[[-1, P]], channel_multiplier=1).then_inc(set_pool, 1)
            po.affine_select(out=umask[:, :], in_=umask[:, :], compare_op=ALU.is_ge, fill=FAR, base=-2,
                             pattern=[[1, P]], channel_multiplier=-1).then_inc(set_pool, 1)
            po.affine_select(out=cmask[:, :, :], in_=cmask[:, :, :], compare_op=ALU.not_equal, fill=FAR, base=1 - S,
                             pattern=[[0, H], [P, NB]], channel_multiplier=1).then_inc(set_pool, 1)
            po.affine_select(out=lmask[:, 8 * P:8 * P + 1], in_=lmask[:, 8 * P:8 * P + 1], compare_op=ALU.not_equal, fill=FAR, base=1 - P,
                             pattern=[[0, 1]], channel_multiplier=1).then_inc(set_pool, 1)
            po.memset(vext[:, :, :, D:D + 1], 1.0).then_inc(set_pool, 1)

            def rstd(nb, i):
                at = nb * RS_N
                if i == 0:
                    variances = known(po, nb * LN_N + 2 * NB)
                    po.wait_ge(set_pool, POOL_SET)
                    po.wait_ge(ln, variances)
                else:
                    before = known(po, at + i)
                    po.wait_ge(set_pool, POOL_SET)
                    po.wait_ge(rs_done, before)
                if i == 0:
                    step = po.tensor_scalar(rs[:, 0, :], mv[:, :, 1], LN_EPS, None, ALU.add)
                elif i == 1:
                    step = po.tensor_tensor(rs[:, 0, :], rs[:, 0, :], mhalf[:, :], ALU.pow)
                elif i == 2:
                    step = po.tensor_tensor(rs[:, 1, :], rs[:, 0, :], rs[:, 0, :], ALU.mult)
                elif i == 3:
                    step = po.tensor_tensor(rs[:, 2, :], rs[:, 1, :], mv[:, :, 1], ALU.mult)
                elif i == 4:
                    step = po.tensor_scalar(rs[:, 2, :], rs[:, 2, :], LN_EPS, None, ALU.add)
                elif i == 5:
                    step = po.tensor_tensor(rs[:, 2, :], rs[:, 2, :], mhalf[:, :], ALU.pow)
                else:
                    step = po.tensor_tensor(rs[:, 2, :], rs[:, 2, :], rs[:, 0, :], ALU.mult)
                step.then_inc(rs_done, 1)

            def positions(nb, i):
                at = nb * POS_N
                half = i % 2
                cut = slice(HALF * half, HALF * half + HALF)
                if i < 2:
                    po.wait_ge(e_done, nb * E_N + E_N)
                    po.tensor_tensor(t2[:, cut], qu[:, cut], kc[:, 1 + HALF * half:1 + HALF * half + HALF], ALU.mult).then_inc(pos, 1)
                    return
                form, step = divmod(i - 2, 6)
                g, cos, sin = ((g_lo, rot[0], rot[1]), (g_up, rot[2], rot[3]))[form]
                src = slice(HALF * half + form, HALF * half + form + HALF)
                if step < 2:
                    po.wait_ge(pos, at + 2 + 6 * form)
                    po.tensor_tensor(g[:, cut], rp[:, src], cos[:, cut], ALU.mult).then_inc(pos, 1)
                elif step < 4:
                    po.wait_ge(pos, at + 2 + 6 * form)
                    po.tensor_tensor(t3[:, cut], rq[:, src], sin[:, cut], ALU.mult).then_inc(pos, 1)
                else:
                    po.wait_ge(pos, at + i - 1)
                    po.tensor_tensor(g[:, cut], g[:, cut], t3[:, cut], ALU.add).then_inc(pos, 1)

            def residual(b):
                po.wait_ge(d_res, b * 16 + 16)
                po.tensor_tensor(xres[:, :, :], xres[:, :, :], bo_rows[:, :].unsqueeze(1).to_broadcast([P, NB, E]), ALU.add).then_inc(res_done, 1)

            po.sem_inc(p_mask, LATE)
            for i in range(RS_N):
                rstd(0, i)
            po.wait_ge(d_w, D_W)
            po.wait_ge(d_cst, D_CST)
            po.wait_ge(set_dve, DVE_SET)
            for i in range(POS_N - 6):
                positions(0, i)
            po.wait_ge(pos, POS_N - 6)
            po.wait_ge(upper, 3)
            for _ in range(6):
                po.sem_inc(pos, 1)
            for i in range(RS_N):
                rstd(1, i)
            with po.Fori(0, B) as b:
                for h in range(H):
                    for u in range(S2U):
                        n = h * S2U + u
                        units = known(po, HPB * (b * (H * S2U) + n + 2))
                        po.wait_ge(set_pool, POOL_SET)
                        po.wait_ge(p_exp, units)
                        if 0 < u < NB:
                            po.memset(prob[n % RING][0:1, P * u - 1:P * u], 0.0)
                        if u < NB:
                            p = prob[n % RING][:, P * u:P * u + P]
                            po.affine_select(out=p, in_=p, compare_op=ALU.is_ge, fill=0.0, base=0,
                                             pattern=[[1, P]], channel_multiplier=-1).then_inc(p_mask, 1)
                        else:
                            p = prob[n % RING][:, :].rearrange("p (n q) -> p n q", q=P)
                            po.affine_select(out=p, in_=p, compare_op=ALU.is_ge, fill=0.0, base=-2,
                                             pattern=[[0, NB], [-1, P]], channel_multiplier=1).then_inc(p_mask, 1)
                        if (h, u) == (0, 6):
                            residual(b)
                        if h == 7 and u < RS_N:
                            rstd(b + 2, u)
                        if (3, 1) <= (h, u) <= (4, 5):
                            positions(b + 1, (h - 3) * S2U + u - 1)
            residual(B)

        @block.tensor
        def _(pe):
            pe.wait_ge(d_w, D_W)
            pe.wait_ge(d_cst, D_CST)
            pe.wait_ge(set_pool, POOL_SET)
            pe.wait_ge(set_dve, DVE_BIAS)
            pe.sem_inc(s2_ready, 1)
            pe.sem_inc(pv_done, RING - LATE)
            pe.sem_inc(w_done, W_PRO)

            def project(nb, j):
                first = isinstance(nb, int)
                dst = (pE, *pA)[j % 4] if first else pE
                if j == 0:
                    pe.wait_ge(ln, (nb + 1) * LN_N)
                if not first:
                    pe.wait_ge(e_done, nb * E_N + (E_AT[j - 1] if j else 0))
                elif j >= 2:
                    pe.wait_ge(e_done, E_AT[max(j - 4, j % 2 + (2 if j >= 6 else 0))])
                half = slice(HALF * (j % 2), HALF * (j % 2) + HALF)
                if j < 2:
                    for t in range(4):
                        mm = pe.transpose(dst[:, P * t:P * t + P], xn[:, 4 * j + t, :], ident[:, :])
                else:
                    w, src = ((w_q, xnT), (w_k, xnT), (w_p, qv), (w_ps, qv))[j // 2 - 1]
                    mm = pe.matmul(dst[:, :], w[:, :], src[:, half], start=True, stop=True)
                mm.then_inc(e_ready, 1)

            pe.matmul(pM[:, 0:E], bv_wide[:, :], w_o[:, :], start=True, stop=True).then_inc(m_ready, 1)

            def super_scores(part=0, parts=1):
                for blk in range(NB * part // parts, NB * (part + 1) // parts):
                    mm = pe.matmul((pM if parts == 1 else pE)[:, H * blk:H * blk + H], t2[:, P * blk:P * blk + P], hsum[:, :], start=True, stop=True)
                return mm

            def values(half, part=0, parts=1):
                for t in range(NB * part // parts, NB * (part + 1) // parts):
                    mm = pe.matmul(pM[:, 64 * t:64 * t + 64], xnT[:, P * t:P * t + P], w_v[:, 64 * half:64 * half + 64], start=True, stop=True)
                return mm

            def values_shifted(half):
                for t in range(4):
                    c = P * (4 * half + t) + 1
                    mm = pe.matmul((pE, pM)[half][:, P * t:P * t + P], xnT[:, c:c + P], w_v[:, :], start=True, stop=True)
                return mm

            def row_of_maxima(b, h):
                pe.wait_ge(mx_done, b * H + h + 1)
                return pe.transpose(pM[0:NB, 0:P], mneg[:, h % H, :].bitcast(F32), ident[:, :])

            def context_turned(b, h):
                pe.wait_ge(ctx_evac, b * H + h + 2)
                for i in range(S // STRIPS // P):
                    mm = pe.transpose(pM[:, P * i:P * i + P], ctxp[:, P * i:P * i + P], ident[:, :])
                return mm

            def first_pass(b, h, n):
                s = h % SLOTS
                if n == 0:
                    pe.wait_ge(stk[s], b * (2 * STK) + (h // SLOTS + 1) * STK)
                if not (isinstance(b, int) and h == 0 and n < S1_BUFS):
                    pe.wait_ge(s1_read, b * (H * S1U) + h * S1U + n - S1_BUFS + 1)
                dst = pA[n % S1_BUFS]
                if n < NB * HPB:
                    qb, k0, low = piece(n)
                    q = slice(P * qb, P * qb + P)
                    if low > 0:
                        mm = pe.matmul(dst[:, 0:low], QL[0:KROWS, s, q], K[0:KROWS, s, k0:k0 + low], start=True, stop=True)
                    if low < HALF:
                        mm = pe.matmul(dst[:, low:HALF], QU[0:KROWS, s, q], K[0:KROWS, s, k0 + low:k0 + HALF], start=True, stop=True)
                else:
                    for i in range(4):
                        q = slice(P * (4 * (n % 2) + i), P * (4 * (n % 2) + i) + P)
                        mm = pe.matmul(dst[:, P * i:P * i + P], QU[0:KROWS, s, q], K[0:KROWS, s, q], start=True, stop=True)
                mm.then_inc(s1_ready, 1)

            def second_pass(b, h, u, half):
                s = h % SLOTS
                if u == 0 and half == 0:
                    pe.wait_ge(mrow_in[h % 2], b * (H * 16) + (h // 2 + 1) * 32)
                pe.wait_ge(p_exp, HPB * (b * (H * S2U) + h * S2U + u) + half + 1)
                r, q0 = MROW + 1, HALF * half
                if u < NB:
                    k = slice(P * u, P * u + P)
                    up = min(max(P * u - q0, 0), HALF)
                    if up > 0:
                        mm = pe.matmul(pB[:, q0:q0 + up], K[0:r, s, k], QU[0:r, s, q0:q0 + up], start=True, stop=True)
                    if up < HALF:
                        mm = pe.matmul(pB[:, q0 + up:q0 + HALF], K[0:r, s, k], QL[0:r, s, q0 + up:q0 + HALF], start=True, stop=True)
                else:
                    for k0 in range(q0, q0 + HALF, P):
                        k = slice(k0, k0 + P)
                        mm = pe.matmul(pB[:, k], K[0:r, s, k], QU[0:r, s, k], start=True, stop=True)
                mm.then_inc(s2_ready, 1)

            def context(b, h, u):
                n, quarter = h * S2U + u, S // STRIPS
                pe.wait_ge(p_mask, b * (H * S2U) + n + 1 + LATE)
                if u == 0:
                    pe.wait_ge(ctx_evac, b * H + h + 1)
                if u < NB:
                    pieces = [(u, quarter * strip, quarter) for strip in range(STRIPS)]
                else:
                    pieces = [(kb, P * kb, P) for i in range(2) for kb in range(i, NB, 2)]
                for kb, q0, w in pieces:
                    strip, at = VW * (q0 // quarter), q0 % quarter
                    mm = pe.matmul(pC[strip:strip + VW, at:at + w], vext[:, kb, h % H, :], prob[n % RING][:, q0:q0 + w],
                                   start=(u == 0), stop=(u == NB), skip_group_check=True)
                mm.then_inc(pv_done, 1)

            for j in range(10):
                project(0, j)
            pe.wait_ge(e_done, E_N)
            pe.wait_ge(m_done, 1)
            pe.wait_ge(pos, 2)
            super_scores().then_inc(m_ready, 1)
            pe.wait_ge(m_done, 2)
            values(0).then_inc(m_ready, 1)
            for h in range(AHEAD):
                for n in range(S1U):
                    first_pass(0, h, n)
            pe.wait_ge(m_done, 3)
            row_of_maxima(0, 0).then_inc(m_ready, 1)

            def turn_context(half, dst):
                for t in range(4):
                    mm = pe.transpose(dst[:, P * t:P * t + P], vsh[:, 4 * half + t, :, :].rearrange("p h d -> p (h d)"), ident[:, :])
                return mm

            def project_out(half, dst):
                for t in range(4):
                    c = P * (4 * half + t)
                    mm = pe.matmul(dst[:, P * t:P * t + P], ctxT[:, c:c + P], w_o[:, :], start=True, stop=True)
                return mm

            def small_piece(b, place):
                h = place[0]
                name, part, parts = PARTS[place]
                if part == 0 and name in W_OF:
                    pe.wait_ge(w_done, b * W_N + W_PRO + W_OF[name])
                elif part == 0:
                    last = next(p for p in M_PLACES if p >= place)
                    pe.wait_ge(m_done, b * M_N + M_PRO + M_IDX[last])
                if name == "row":
                    mm = row_of_maxima(b, h + 1)
                elif name == "context":
                    mm = context_turned(b, h - 1)
                elif name in ("turn 0", "turn 1"):
                    if name == "turn 0":
                        pe.wait_ge(norm, b * NORM_N + NORM_N)
                    mm = turn_context(int(name[-1]), pE)
                elif name in ("project 0", "project 1"):
                    mm = project_out(int(name[-1]), (pE, pM)[int(name[-1])])
                elif name in ("shifted 0", "shifted 1"):
                    mm = values_shifted(int(name[-1]))
                elif name == "super":
                    if part == 0:
                        pe.wait_ge(pos, b * POS_N + POS_N + 2)
                    mm = super_scores(part, parts)
                else:
                    mm = values(int(name[-1]), part, parts)
                if part == parts - 1:
                    mm.then_inc(w_ready if name in W_OF else m_ready, 1)

            for j in range(0, P, VW):
                pe.matmul(pC[j:j + VW, :], vext[:, 0, H - 1, :], prob[1][:, 0:S // STRIPS], start=True, stop=False, skip_group_check=True)
            with pe.Fori(0, B) as b:
                for h in range(H):
                    for u in range(S2U):
                        second_pass(b, h, u, 0)
                        first_pass(b, h + AHEAD, 2 * u)
                        second_pass(b, h, u, 1)
                        first_pass(b, h + AHEAD, 2 * u + 1)
                        if u < LATE:
                            context(b, h - 1, S2U - LATE + u)
                        else:
                            context(b, h, u - LATE)
                        if (h, u) in PARTS:
                            small_piece(b, (h, u))
                        if (h, u) == (2, 0):
                            pe.wait_ge(w_done, b * W_N + W_PRO + W_OF["shifted 0"] + 1)
                        if h == 2:
                            project(b + 1, u)
                        if h == 3 and u == 0:
                            project(b + 1, 9)
            for u in range(LATE):
                context(B, -1, S2U - LATE + u)
            pe.wait_ge(m_done, B * M_N + M_PRO)
            context_turned(B, -1).then_inc(m_ready, 1)
            pe.wait_ge(norm, (B + 1) * NORM_N)
            for j in range(4):
                pe.wait_ge(m_done, B * M_N + M_PRO + 1 + j)
                mm = turn_context(j, pM) if j < 2 else project_out(j - 2, pM)
                mm.then_inc(m_ready, 1)

        @block.scalar
        def _(act):
            act.sem_inc(p_exp, HPB)
            act.sem_inc(psup_done, 1)
            act.wait_ge(d_w, D_W)
            act.wait_ge(set_dve, DVE_BIAS)

            def evacuate(nb, j):
                act.wait_ge(e_ready, nb * 10 + j + 1)
                half = slice(HALF * (j % 2), HALF * (j % 2) + HALF)
                src = (pE, *pA)[j % 4] if isinstance(nb, int) else pE
                if j < 2:
                    act.activation(xnT[:, half], src[:, :], ACT.Identity, bias=cols[:, 1:2], scale=cols[:, 0:1]).then_inc(e_done, 1)
                elif j < 4:
                    act.activation(qv[:, half], src[:, :], ACT.Identity, bias=bias_qv[:, :]).then_inc(e_done, 1)
                    act.activation(qu[:, half], src[:, :], ACT.Identity, bias=bias_qu[:, :]).then_inc(e_done, 1)
                elif j < 6:
                    act.activation(kc[:, half], src[:, :], ACT.Identity, bias=cols[:, 3:4]).then_inc(e_done, 1)
                else:
                    act.activation((rp if j < 8 else rq)[:, half], src[:, :], ACT.Copy).then_inc(e_done, 1)

            def high(nb, i):
                name, src = (("c", qu), ("k", kc), ("gl", g_lo), ("gu", g_up))[i]
                if i < 2:
                    act.wait_ge(e_done, nb * E_N + E_N)
                else:
                    act.wait_ge(pos, nb * POS_N + (8 if i == 2 else 14))
                act.activation(parts[name][0][:, :], src[:, 0:S], ACT.Copy).then_inc(hi_done, 1)

            def copied(name, src, done):
                half = int(name[-1])
                four = slice(4 * half, 4 * half + 4)
                if name.startswith("values"):
                    dst, src = vext[:, :, four, 0:D], src[:, :].rearrange("p (t h d) -> p t h d", h=4, d=D)
                elif name.startswith("turn"):
                    dst, src = ctxT[:, HALF * half:HALF * half + HALF], src[:, :]
                else:
                    dst, src = vsh[:, four, :, :].rearrange("p t h d -> p t (h d)"), src[:, :].rearrange("p (t e) -> p t e", e=E)
                act.activation(dst, src, ACT.Copy).then_inc(done, 1)

            def context_out(b, h):
                act.wait_ge(pv_done, b * (H * S2U) + (h + 1) * S2U + RING)
                act.activation(ctxp[:, :], pC[:, :], ACT.Copy).then_inc(ctx_evac, 1)

            for j in range(10):
                evacuate(0, j)
            for i in range(4):
                high(0, i)
            act.wait_ge(set_pool, POOL_SET)
            act.wait_ge(m_ready, 3)
            copied("values 0", pM, m_done)
            with act.Fori(0, B) as b:
                for h in range(H):
                    for u in range(S2U):
                        n = h * S2U + u
                        if (2, 1) <= (h, u) <= (3, 1):
                            evacuate(b + 1, (h - 2) * S2U + u - 1)
                        if u == LATE:
                            context_out(b, h - 1)
                        before = (h, u - 1) if u else (h - 1, S2U - 1)
                        if M_ORDER.get(before) in COPIES:
                            act.wait_ge(m_ready, b * M_N + M_PRO + M_IDX[before] + 1)
                            copied(M_ORDER[before], pM, m_done)
                        if W_ORDER.get(before) in COPIES:
                            act.wait_ge(w_ready, b * W_N + W_OF[W_ORDER[before]] + 1)
                            copied(W_ORDER[before], pE, w_done)
                        act.wait_ge(s2_ready, HPB * (b * (H * S2U) + n) + 2)
                        act.wait_ge(pv_done, b * (H * S2U) + n + 1)
                        act.activation(prob[n % RING][:, 0:HALF], pB[:, 0:HALF], ACT.Exp, scale=SCALE).then_inc(p_exp, 1)
                        act.wait_ge(s2_ready, HPB * (b * (H * S2U) + n) + 3)
                        act.activation(prob[n % RING][:, HALF:S], pB[:, HALF:S], ACT.Exp, scale=SCALE).then_inc(p_exp, 1)
                        if (h, u) == (3, 3):
                            act.wait_ge(stored, (b + 1) * ST_N)
                        if (h, u) in HIGH_AT:
                            high(b + 1, HIGH_AT.index((h, u)))
                    if h == 0:
                        act.wait_ge(norm, b * NORM_N + 2)
                        act.wait_ge(norm, b * NORM_N + NORM_N)
                    act.wait_ge(dsup_done, b * H + h + 1)
                    act.activation(psup[:, h, :], dsup[:, h, :], ACT.Exp, scale=SCALE).then_inc(psup_done, 1)
            context_out(B, -1)
            for j in range(2):
                act.wait_ge(m_ready, B * M_N + M_PRO + 2 + j)
                copied(f"turn {j}", pM, m_done)

        @block.vector
        def _(v):
            def stats(nb, t):
                at = nb * LN_N
                if t == 0:
                    v.wait_ge(d_x, nb * 16 + 16)
                v.bn_stats(st6[:, t, :], xt[:, t, :]).then_inc(ln, 1)
                own = known(v, at + 2 * t + 1)
                if not isinstance(nb, int):
                    v.wait_ge(set_dve, DVE_SET)
                v.wait_ge(ln, own)
                v.bn_aggr(mv[:, t, :], st6[:, t, :]).then_inc(ln, 1)

            def normalize(nb, t):
                if t == 0:
                    v.wait_ge(rs_done, nb * RS_N + RS_N)
                v.tensor_scalar(xn[:, t, :], xt[:, t, :], mv[:, t, 0:1], rs[:, 2, t:t + 1], ALU.subtract, ALU.mult).then_inc(ln, 1)

            def low(nb, i):
                name, src = (("c", qu), ("k", kc), ("gl", g_lo), ("gu", g_up))[i]
                v.wait_ge(hi_done, nb * HI_N + i + 1)
                v.tensor_tensor(parts[name][1][:, :], src[:, 0:S], parts[name][0][:, :].bitcast(F32), ALU.subtract).then_inc(low_done, 1)

            def arrived_m(b, i):
                v.wait_ge(m_ready, b * M_N + M_PRO + i + 1)

            def super_out(src, done):
                v.tensor_tensor(acc[:, :, :, 3], src[:, 0:NB * H].rearrange("p (n h) -> p h n", h=H), cmask[:, :, :], ALU.add).then_inc(done, 1)

            def first_pass(b, h, n):
                s = h % H
                pieces = known(v, b * (H * S1U) + h * S1U + n + 1)
                v.wait_ge(set_pool, POOL_SET)
                v.wait_ge(s1_ready, pieces)
                if n < NB * HPB:
                    qb, k0, _ = piece(n)
                    at = 7 * P - P * qb + k0
                    v.tensor_tensor_reduce(junk[:, n % S1_BUFS, :], pA[n % S1_BUFS][:, :], lmask[:, at:at + HALF], 1.0, -3.0e38, ALU.add, ALU.max,
                                           acc[:, s, qb, n % 2:n % 2 + 1]).then_inc(s1_read, 1)
                else:
                    g = n % 2
                    for i in range(4):
                        blk = 4 * g + i
                        ttr = v.tensor_tensor_reduce(junk[:, n % S1_BUFS, P * i:P * i + P], pA[n % S1_BUFS][:, P * i:P * i + P], umask[:, :], 1.0, -3.0e38, ALU.add, ALU.max,
                                                     acc[:, s, blk, 2:3])
                    ttr.then_inc(s1_read, 1)

            def maxima(b, h):
                s = h % H
                v.wait_ge(s1_read, b * (H * S1U) + (h + 1) * S1U)
                v.tensor_reduce(mneg[:, s, :], acc[:, s, :, :], AX.X, ALU.max, negate=True).then_inc(mx_done, 1)
                v.wait_ge(mx_done, b * H + h + 1)
                v.tensor_tensor(dsup[:, s, :], acc[:, s, :, 3], mneg[:, s, :].bitcast(F32), ALU.add).then_inc(dsup_done, 1)

            def row_out(h):
                v.tensor_copy(mrow[h % 2][:, :], pM[0:NB, 0:P]).then_inc(m_done, 1)

            def context_placed(h):
                v.tensor_copy(ctx_all[:, :, h % H, :].rearrange("p (c i) d -> p i c d", c=STRIPS),
                              pM[:, 0:S // STRIPS].rearrange("p (i c w) -> p i c w", c=STRIPS, w=VW)[:, :, :, 0:D + 1]).then_inc(m_done, 1)

            def normalized(b, i):
                pq = psup[:, :, :].rearrange("p h n -> p n h")
                if i == 0:
                    v.wait_ge(psup_done, b * H + 1)
                else:
                    v.wait_ge(norm, b * NORM_N + i)
                if i == 0:
                    v.tensor_tensor(vsh[:, :, :, :], vsh[:, :, :, :], pq.unsqueeze(3).to_broadcast([P, NB, H, D]), ALU.mult).then_inc(norm, 1)
                elif i == 1:
                    v.tensor_tensor(den[:, :, :], ctx_all[:, :, :, D], pq, ALU.add).then_inc(norm, 1)
                elif i == 2:
                    v.reciprocal(den[:, :, :], den[:, :, :]).then_inc(norm, 1)
                elif i == 3:
                    v.tensor_tensor(vsh[:, :, :, :], vsh[:, :, :, :], ctx_all[:, :, :, 0:D], ALU.add).then_inc(norm, 1)
                else:
                    v.tensor_tensor(vsh[:, :, :, :], vsh[:, :, :, :], den[:, :, :].unsqueeze(3).to_broadcast([P, NB, H, D]), ALU.mult).then_inc(norm, 1)

            def final(half, src, done):
                x2 = xres[:, 4 * half:4 * half + 4, :]
                v.tensor_tensor(x2, x2, src[:, :].rearrange("p (t e) -> p t e", e=E), ALU.add).then_inc(done, 1)

            def small_piece(b, place):
                name, h = PARTS[place][0], place[0]
                if name in W_OF:
                    v.wait_ge(w_ready, b * W_N + W_OF[name] + 1)
                else:
                    arrived_m(b, M_IDX[place])
                if name == "row":
                    row_out(h + 1)
                elif name == "context":
                    context_placed(h - 1)
                elif name == "super":
                    super_out(pE, w_done)
                elif name == "project 0":
                    v.wait_ge(res_done, b + 1)
                    final(0, pE, w_done)
                else:
                    final(1, pM, m_done)

            for t in range(NB):
                stats(0, t)
            for t in (xnT, kc, rp, rq):
                v.memset(t[:, S:S + 1], 0.0).then_inc(set_dve, 1)
            v.memset(ctx_all[:, :, :, :], 1.0).then_inc(set_dve, 1)
            v.memset(psup[:, :, :], 0.0).then_inc(set_dve, 1)
            v.memset(vsh[:, :, :, :], 0.0).then_inc(set_dve, 1)
            v.memset(K[MROW:MROW + 1, :, :].bitcast(F32), 1.0).then_inc(set_dve, 1)
            v.wait_ge(d_w, D_W)
            v.tensor_tensor(bias_qv[:, :], cols[:, 2:3], vu[:, 0:1], ALU.add).then_inc(set_dve, 1)
            v.tensor_tensor(bias_qu[:, :], cols[:, 2:3], vu[:, 1:2], ALU.add).then_inc(set_dve, 1)
            v.memset(bv_wide[:, :], 1.0).then_inc(set_dve, 1)
            v.wait_ge(set_dve, 11)
            v.tensor_scalar(bv_wide[:, :], bv_wide[:, :], cols[:, 4:5], None, ALU.mult).then_inc(set_dve, 1)
            for t in range(NB):
                normalize(0, t)
            v.wait_ge(d_cst, D_CST)
            v.tensor_copy(parts["pe"][0][:, :], g_lo[:, :]).then_inc(set_dve, 1)
            v.wait_ge(set_dve, 13)
            v.tensor_tensor(parts["pe"][1][:, :], g_lo[:, :], parts["pe"][0][:, :].bitcast(F32), ALU.subtract).then_inc(set_dve, 1)
            v.wait_ge(set_dve, DVE_SET)
            v.wait_ge(set_pool, POOL_SET)
            v.wait_ge(m_ready, 1)
            v.tensor_tensor(bo_rows[:, :], bo_rows[:, :], pM[:, 0:E], ALU.add).then_inc(m_done, 1)
            for i in range(2):
                low(0, i)
            v.wait_ge(e_done, E_N)
            turned = xres[:, :, :].rearrange("p t e -> p (t e)")
            v.tensor_tensor(g_up[:, :], rp[:, 1:S + 1], rot[2][:, :], ALU.mult).then_inc(upper, 1)
            v.tensor_tensor(turned, rq[:, 1:S + 1], rot[3][:, :], ALU.mult).then_inc(upper, 1)
            v.wait_ge(upper, 2)
            v.tensor_tensor(g_up[:, :], g_up[:, :], turned, ALU.add).then_inc(upper, 1)
            for i in range(2, 4):
                low(0, i)
            for t in range(NB):
                stats(1, t)
            v.wait_ge(m_ready, 2)
            super_out(pM, m_done)
            v.wait_ge(m_done, 2)
            for h in range(AHEAD):
                for n in range(S1U):
                    first_pass(0, h, n)
                maxima(0, h)
            v.wait_ge(m_ready, 4)
            v.tensor_copy(mrow[0][:, :], pM[0:NB, 0:P]).then_inc(m_done, 1)
            with v.Fori(0, B) as b:
                for h in range(H):
                    for u in range(S2U):
                        first_pass(b, h + AHEAD, 2 * u)
                        before = (h, u - 1) if u else (h - 1, S2U - 1)
                        if {**M_ORDER, **W_ORDER}.get(before, COPIES[0]) not in COPIES:
                            small_piece(b, before)
                        first_pass(b, h + AHEAD, 2 * u + 1)
                        if h == 0 and u in NORMALIZE_AT:
                            if u == NORMALIZE_AT[1]:
                                v.wait_ge(m_done, b * M_N + M_PRO + M_IDX[0, 3] + 1)
                            normalized(b, NORMALIZE_AT.index(u))
                        if h == 5 and u < NB:
                            stats(b + 2, u)
                        if h == 1 and u < NB:
                            normalize(b + 1, u)
                        if (h, u) in LOW_AT:
                            low(b + 1, LOW_AT.index((h, u)))
                    if h == 6:
                        v.wait_ge(w_done, b * W_N + W_PRO + W_OF["super"] + 1)
                    maxima(b, h + AHEAD)
            v.wait_ge(m_ready, B * M_N + M_PRO + 1)
            context_placed(H - 1)
            v.wait_ge(m_done, B * M_N + M_PRO + 1)
            for i in range(5):
                normalized(B, i)
            v.wait_ge(res_done, B + 1)
            for j in range(2):
                v.wait_ge(m_ready, B * M_N + M_PRO + 4 + j)
                final(j, pM, m_done)


def att_consts():
    import numpy as np
    div = np.exp(np.arange(0, E, 2, dtype=np.float32) * np.float32(-np.log(10000.0) / E)).astype(np.float64)
    w = np.repeat(div, 2)[:, None]
    q = np.arange(S)[None, :].astype(np.float64)
    odd = (np.arange(E) % 2 == 1)[:, None]
    sg = np.where(odd, 1.0, -1.0)
    rot = np.stack([np.cos((S - 1 - q) * w), sg * np.sin((S - 1 - q) * w), np.cos((q + 2) * w), -sg * np.sin((q + 2) * w)]).astype(np.float32)
    pe = np.where(odd, np.cos(q * w), np.sin(q * w)).astype(np.float32)
    p = np.arange(P)
    hsum = (p[:, None] // D == np.arange(H)[None, :]).astype(np.float32)
    return rot, pe, hsum

def att_layout(i):
    import numpy as np
    a = {k[8:]: np.asarray(v) for k, v in i.items() if k.startswith("L0_attn_")}
    def diag(m):
        out = np.zeros((P, P), np.float32)
        for h in range(H):
            out[D * h:D * h + D, D * h:D * h + D] = m
        return out
    rot, pe, hsum = att_consts()
    swap = np.arange(D) ^ 1
    return {"x": a["inputs"][:B], "wq": diag(a["Wq"]), "wk": diag(a["Wk"]), "wv": diag(a["Wv"]), "wp": diag(a["Wp"].T), "wps": diag(a["Wp"].T[:, swap]),
            "wo": a["Wo"], "cols": np.stack([a["ln_gamma"], a["ln_beta"], np.tile(a["bq"], H), np.tile(a["bk"], H), np.tile(a["bv"], H)], 1),
            "vu": np.stack([a["v_bias"].reshape(-1), a["u_bias"].reshape(-1)], 1),  "bo": a["bo"],
            "rot": rot, "pe": pe, "hsum": hsum}


def sum_tensors(nc, ctx):
    return {"x2": [ctx.enter_context(nc.sbuf_tensor(f"x2_{b}", [P, NB, E], F32)) for b in range(B)],
            "gate": ctx.enter_context(nc.sbuf_tensor("gate", [P, TOPK, B * NB], F32))}


def expert_tensors(nc, ctx):
    def sb(name, shape, dt=F32):
        return ctx.enter_context(nc.sbuf_tensor(name, shape, dt))
    return {"w1_h": sb("w1_high", [P, NX * 2 * F], F32R), "w1_l": sb("w1_low", [P, NX * 2 * F], F32R), "w2": sb("w2_all", [P, NX * (F // P) * E]),
            "b1": sb("b1_all", [P, NX * 2 * F]), "b2": sb("b2_all", [P, NX * E]),
            "ident": sb("ident_f", [P, P]),
            "tile_expert": sb("tile_expert", [P, TABLE]),
            "expert_no": sb("expert_no", [1, TABLE], I32), "row_no": sb("row_no", [1, TABLE], I32)}


def routing_phase(nc, dram, keep):
    ctx = ExitStack()
    with ctx:
        def sb(name, shape, dt=F32):
            return ctx.enter_context(nc.sbuf_tensor(name, shape, dt))

        def sem(name):
            return ctx.enter_context(nc.semaphore(name))

        wr1, wr2 = sb("wr1", [P, RH]), sb("wr2", [RH, NX])
        br1, lns, lnb, br2 = sb("br1", [P, RH]), sb("lns", [P, RH]), sb("lnb", [P, RH]), sb("br2", [P, NX])
        ident = keep["ident"]
        tri, ones = sb("tri", [P, P], BF16), sb("ones", [P, P], BF16)
        mhalf, iota8 = sb("mhalf_r", [P, NB]), sb("iota8", [P, NX])
        xb = [sb(f"xb{i}", [P, NB, E]) for i in range(UNROLL)]
        rows = [sb(f"rows_r{i}", [P, NB, ROW]) for i in range(UNROLL)]
        idx = [sb(f"idx{i}", [P, NB, TOPK], U32) for i in range(UNROLL)]
        st, mv, rs = sb("st_r", [P, NB, 6]), sb("mv_r", [P, NB, 2]), sb("rs_r", [P, NB])
        st2, mv2, rs2 = sb("st2", [P, NB, 6]), sb("mv2", [P, NB, 2]), sb("rs2", [P, NB])
        hT, gT = sb("hT", [P, S]), sb("gT_r", [RH, S])
        hr, hg = sb("hr", [P, NB, RH]), sb("hg", [P, NB, RH])
        lg, mx, mi = sb("lg", [P, NB, NX]), sb("mx", [P, NB, NX]), sb("mi", [P, NB, NX], U32)
        dlt, xf = sb("dlt", [P, B * NB]), sb("xf", [P, NB, TOPK])
        oh, both = sb("oh", [P, NB, TOPK, NX]), sb("both", [P, NB, NX], BF16)
        pos, prod, posf = sb("pos", [P, NB, NX]), sb("prod", [P, NB, TOPK, NX]), sb("posf", [P, NB, TOPK])
        carry = sb("carry", [P, NX])
        start = sb("start", [P, NX])
        cnt, ti32, tiles = sb("cnt", [P, NX]), sb("ti32", [P, NX], I32), sb("tiles", [P, NX])
        cum, tno = sb("cum", [P, NX]), sb("tno", [P, TABLE])
        past, used = sb("past", [P, TABLE, NX - 1], BF16), sb("used", [P, TABLE, NX - 1], BF16)
        first, cap = sb("first", [P, TABLE]), sb("cap", [P, TABLE])
        padrow, padi = sb("padrow", [P, ROW]), sb("padi", [1, NX], I32)
        pidx = sb("pidx", [P, 1])
        ex = sb("ex", [P, B * NB])

        def pb(name, shape):
            return ctx.enter_context(nc.psum_tensor(name, shape, F32))
        pT, pH, pG = pb("pT", [P, S]), pb("pH", [P, NB * RH]), pb("pG", [RH, S])
        pL, pR = pb("pL", [P, NB * NX]), pb("pR", [P, NB * NX + NX])

        d_w, d_big = sem("router_in"), sem("experts_in")
        d_x = [sem(f"x_in_r{i}") for i in range(UNROLL)]
        d_w1, w1_hi, w1_lo = sem("w1_in"), sem("w1_high"), sem("w1_low")
        setp, setd = sem("set_pool_r"), sem("set_dve_r")
        a_dve, a_rs, a_tr, a_ev = sem("a_dve"), sem("a_rs"), sem("a_tr"), sem("a_ev")
        b_h, b_dve, b_rs, b_gelu, b_gt, b_gev, b_lg = (sem(n) for n in ("b_h", "b_dve", "b_rs", "b_gelu", "b_gt", "b_gev", "b_lg"))
        c_dve, c_rank, rows_free = sem("c_dve"), sem("c_rank"), sem("rows_free")
        scat = [sem(f"scattered{i}") for i in range(2)]
        t_dve, t_exp, t_pad = sem("t_dve"), sem("t_exp"), sem("t_pad")
        block = ctx.enter_context(nc.Block())
        A_N, A_STATS = 2 * NB + NB + 1, 2 * NB
        B_STATS, B_N = 1 + 2 * NB, 1 + 2 * NB + NB + 2
        C_N, C_BOTH, C_IDX = 1 + 2 * NB + 5 + 5, 1 + 2 * NB + 5, 1 + 2 * NB + 5 + 5
        SCAT_N = 16 * NB * TOPK
        D_W, SETP, SETD = 16 * 6, 10, 3
        D_BIG = 16 * (NX + 2 + B)

        @block.sync
        def _(sp):
            for t, n in ((wr1, "wr1"), (wr2, "wr2")):
                sp.dma_start(t[:, :], dram[n]).then_inc(d_w, 16)
            for t, n in ((br1, "br1"), (lns, "lns"), (lnb, "lnb"), (br2, "br2")):
                sp.dma_start(t[:, :], dram[n].partition_broadcast(P)).then_inc(d_w, 16)

            def load(nb, k):
                sp.dma_start(xb[k][:, :, :], dram["x2s"][bass.ds(nb % B + 1, 1)].rearrange("o (t p) e -> p (o t) e", p=P)).then_inc(d_x[k], 16)
            for k in range(UNROLL):
                load(k, k)
            for e in range(NX):
                sp.dma_start(keep["w1_l"][:, 2 * F * e:2 * F * (e + 1)].bitcast(F32), dram["w1"][e]).then_inc(d_w1, 16)
                sp.dma_start(keep["w2"][:, F * e:F * (e + 1)].rearrange("p (c d) -> p c d", d=E),
                             dram["w2"][e].rearrange("(c p) d -> p c d", p=P)).then_inc(d_big, 16)
            sp.dma_start(keep["b1"][:, :], dram["b1"].partition_broadcast(P)).then_inc(d_big, 16)
            sp.dma_start(keep["b2"][:, :], dram["b2"].partition_broadcast(P)).then_inc(d_big, 16)
            for b in range(B):
                sp.dma_start(keep["x2"][b][:, :, :], dram["x2s"][b + 1].rearrange("(t p) e -> p t e", p=P)).then_inc(d_big, 16)
            with sp.Fori(0, B // UNROLL) as it:
                for k in range(UNROLL):
                    nb = it * UNROLL + k
                    sp.wait_ge(d_w, D_W)
                    sp.wait_ge(a_dve, known(sp, nb * A_N + A_N))
                    load(nb + UNROLL, k)
            for k in range(UNROLL):
                sp.wait_ge(d_x[k], (B // UNROLL + 1) * 16)
            sp.wait_ge(d_big, D_BIG)
            sp.wait_ge(d_w1, 16 * NX)
            sp.wait_ge(t_dve, 2)
            for e in range(NX):
                row = nc.values_load(padi[0:1, e:e + 1], engines=(mybir.EngineType.SP,), min_val=0, max_val=NX * REGION - P,
                                     skip_runtime_bounds_check_because="a region has room for every token and a tile")
                sp.dma_start(dram["xs"][bass.ds(row, P), :], padrow[:, :]).then_inc(t_pad, 16)
            sp.wait_ge(t_pad, 16 * NX)

        @block.gpsimd
        def _(po):
            po.memset(ident[:, :], 0.0).then_inc(setp, 1)
            po.memset(tri[:, :], 1.0).then_inc(setp, 1)
            po.memset(mhalf[:, :], -0.5).then_inc(setp, 1)
            po.iota(iota8[:, :], pattern=[[1, NX]], base=0, channel_multiplier=0, allow_small_or_imprecise_dtypes=True).then_inc(setp, 1)
            po.iota(rows[UNROLL - 1][:, :, E], pattern=[[P, NB]], base=TOKENS - S, channel_multiplier=1, allow_small_or_imprecise_dtypes=True).then_inc(setp, 1)
            po.iota(carry[:, :], pattern=[[REGION, NX]], base=0, channel_multiplier=0, allow_small_or_imprecise_dtypes=True).then_inc(setp, 1)
            po.iota(tno[:, :], pattern=[[1, TABLE]], base=0, channel_multiplier=0, allow_small_or_imprecise_dtypes=True).then_inc(setp, 1)
            po.iota(pidx[:, :], pattern=[[0, 1]], base=0, channel_multiplier=1, allow_small_or_imprecise_dtypes=True).then_inc(setp, 1)
            po.wait_ge(setp, 8)
            po.affine_select(out=ident[:, :], in_=ident[:, :], compare_op=ALU.not_equal, fill=1.0, base=0,
                             pattern=[[-1, P]], channel_multiplier=1).then_inc(setp, 1)
            po.affine_select(out=tri[:, :], in_=tri[:, :], compare_op=ALU.is_gt, fill=0.0, base=0,
                             pattern=[[1, P]], channel_multiplier=-1).then_inc(setp, 1)

            def rstd(done, out, var, eps, stats, stats_n, nb):
                have, mine = known(po, stats_n), known(po, nb * 2 + 1)
                po.wait_ge(setp, SETP)
                po.wait_ge(stats, have)
                po.tensor_scalar(out[:, :], var[:, :, 1], eps, None, ALU.add).then_inc(done, 1)
                po.wait_ge(done, mine)
                po.tensor_tensor(out[:, :], out[:, :], mhalf[:, :], ALU.pow).then_inc(done, 1)

            def rstd_a(nb):
                rstd(a_rs, rs, mv, LN_EPS, a_dve, nb * A_N + A_STATS, nb)

            def rstd_b(nb):
                rstd(b_rs, rs2, mv2, ROUTER_EPS, b_dve, nb * B_N + B_STATS, nb)

            po.sem_inc(rows_free, 1)
            rstd_a(0)
            rstd_a(1)
            rstd_b(0)
            rstd_a(2)
            with po.Fori(0, B // UNROLL) as it:
                for k in range(UNROLL):
                    nb = it * UNROLL + k
                    rstd_b(nb + 1)
                    placed = known(po, nb * C_N + C_IDX)
                    po.wait_ge(setp, SETP)
                    po.wait_ge(c_dve, placed)
                    for t in range(NB):
                        if t == 3:
                            if k > 0:
                                po.wait_ge(scat[(k - 1) % 2], it * (2 * SCAT_N) + (k + 1) // 2 * SCAT_N)
                                po.sem_inc(rows_free, 1)
                            rstd_a(nb + 3)
                        for j in range(TOPK):
                            po.indirect_dma_start(dram["xs"], bass.IndirectOffsetOnAxis(idx[k][:, t, j:j + 1], 0),
                                                  rows[k][:, t, :], None).then_inc(scat[k % 2], 16)
                for k in range(2):
                    po.wait_ge(scat[k], (it + 1) * (2 * SCAT_N))
                po.sem_inc(rows_free, 1)

        @block.tensor
        def _(pe):
            pe.wait_ge(d_w, D_W)
            pe.wait_ge(setp, SETP)
            pe.wait_ge(setd, SETD)

            def turn(nb, k):
                pe.wait_ge(a_dve, nb * A_N + A_N)
                if not (isinstance(nb, int) and nb == 0):
                    pe.wait_ge(a_ev, nb * 2)
                for t in range(NB):
                    mm = pe.transpose(pT[:, P * t:P * t + P], rows[k][:, t, 0:E], ident[:, :])
                mm.then_inc(a_tr, 1)

            def hidden(nb):
                pe.wait_ge(a_ev, nb * 2 + 2)
                if not (isinstance(nb, int) and nb == 0):
                    pe.wait_ge(b_dve, (nb - 1) * B_N + 1)
                for t in range(NB):
                    mm = pe.matmul(pH[:, RH * t:RH * t + RH], hT[:, P * t:P * t + P], wr1[:, :], start=True, stop=True)
                mm.then_inc(b_h, 1)

            def logits(nb):
                active, read = known(pe, nb + 1), known(pe, nb * 2)
                pe.wait_ge(setd, SETD)
                pe.wait_ge(b_gelu, active)
                if not (isinstance(nb, int) and nb == 0):
                    pe.wait_ge(b_gev, read)
                for t in range(NB):
                    mm = pe.transpose(pG[:, P * t:P * t + P], hg[:, t, :], ident[:, :])
                mm.then_inc(b_gt, 1)
                pe.wait_ge(b_gev, nb * 2 + 2)
                if not (isinstance(nb, int) and nb == 0):
                    pe.wait_ge(c_dve, (nb - 1) * C_N + 1)
                for t in range(NB):
                    mm = pe.matmul(pL[:, NX * t:NX * t + NX], gT[:, P * t:P * t + P], wr2[:, :], start=True, stop=True)
                mm.then_inc(b_lg, 1)

            def ranks(nb):
                pe.wait_ge(c_dve, nb * C_N + C_BOTH)
                pe.matmul(pR[:, 0:NB * NX], tri[:, :], both[:, :, :].rearrange("p t e -> p (t e)"), start=True, stop=False, skip_group_check=True)
                for t in range(NB - 1):
                    w = NB - 1 - t
                    pe.matmul(pR[:, NX * (t + 1):NX * NB].rearrange("p (t e) -> p t e", e=NX), ones[:, :],
                              both[:, t:t + 1, :].to_broadcast([P, w, NX]), start=False, stop=(t == NB - 2), skip_group_check=True)
                for t in range(NB):
                    mm = pe.matmul(pR[:, NX * NB:NX * NB + NX], ones[:, :], both[:, t, :], start=(t == 0), stop=(t == NB - 1), skip_group_check=True)
                mm.then_inc(c_rank, 1)

            turn(0, 0)
            hidden(0)
            turn(1, 1)
            logits(0)
            hidden(1)
            turn(2, 2)
            with pe.Fori(0, B // UNROLL) as it:
                for k in range(UNROLL):
                    nb = it * UNROLL + k
                    ranks(nb)
                    hidden(nb + 2)
                    logits(nb + 1)
                    turn(nb + 3, (k + 3) % UNROLL)

        @block.scalar
        def _(act):
            act.wait_ge(setp, SETP)

            def turned(nb):
                act.wait_ge(a_tr, nb + 1)
                if not (isinstance(nb, int) and nb == 0):
                    act.wait_ge(b_h, nb)
                for i in range(2):
                    act.activation(hT[:, 512 * i:512 * i + 512], pT[:, 512 * i:512 * i + 512], ACT.Copy).then_inc(a_ev, 1)

            def gelu(nb):
                act.wait_ge(b_dve, nb * B_N + B_N)
                if not (isinstance(nb, int) and nb == 0):
                    act.wait_ge(b_gt, nb)
                act.activation(hg[:, :, :], hr[:, :, :], ACT.Gelu_apprx_tanh).then_inc(b_gelu, 1)
                act.wait_ge(b_gt, nb + 1)
                if not (isinstance(nb, int) and nb == 0):
                    act.wait_ge(b_lg, nb)
                for i in range(2):
                    act.activation(gT[:, 512 * i:512 * i + 512], pG[:, 512 * i:512 * i + 512], ACT.Copy).then_inc(b_gev, 1)

            turned(0)
            turned(1)
            gelu(0)
            turned(2)
            with act.Fori(0, B // UNROLL) as it:
                for k in range(UNROLL):
                    nb = it * UNROLL + k
                    act.wait_ge(d_w1, 16 * NX)
                    part = bass.ds(nb * (2 * F), 2 * F)
                    act.activation(keep["w1_h"][:, part], keep["w1_l"][:, part].bitcast(F32), ACT.Copy).then_inc(w1_hi, 1)
                    gelu(nb + 1)
                    turned(nb + 3)
            act.wait_ge(c_dve, B * C_N)
            act.activation(ex[:, :], dlt[:, :], ACT.Exp).then_inc(t_exp, 1)

        @block.vector
        def _(v):
            v.memset(ones[:, :], 1.0).then_inc(setd, 1)
            v.memset(padrow[:, 0:E], 0.0).then_inc(setd, 1)
            v.memset(padrow[:, E + 1:E + 2], -1.0).then_inc(setd, 1)
            v.wait_ge(d_w, D_W)
            v.wait_ge(setp, SETP)
            v.wait_ge(setd, SETD)

            def stats(nb, k, sem_, at, src, st_, mv_):
                for t in range(NB):
                    v.bn_stats(st_[:, t, :], src(t)).then_inc(sem_, 1)
                v.wait_ge(sem_, at + NB)
                for t in range(NB):
                    v.bn_aggr(mv_[:, t, :], st_[:, t, :]).then_inc(sem_, 1)

            def a1(nb, k, m):
                have = known(v, nb * A_N + NB)
                v.wait_ge(d_x[k], m * 16 + 16)
                for t in range(NB):
                    v.bn_stats(st[:, t, :], xb[k][:, t, :]).then_inc(a_dve, 1)
                v.wait_ge(setp, SETP)
                v.wait_ge(a_dve, have)
                for t in range(NB):
                    v.bn_aggr(mv[:, t, :], st[:, t, :]).then_inc(a_dve, 1)

            def a2(nb, k, waits=True):
                if waits:
                    v.wait_ge(rows_free, nb - 2)
                last = rows[(k - 1) % UNROLL][:, :, E]
                v.wait_ge(a_dve, nb * A_N) if not (isinstance(nb, int) and nb == 0) else None
                v.tensor_scalar(rows[k][:, :, E], last, float(S), None, ALU.add).then_inc(a_dve, 1)
                v.wait_ge(a_rs, nb * 2 + 2)
                for t in range(NB):
                    v.tensor_scalar(rows[k][:, t, 0:E], xb[k][:, t, :], mv[:, t, 0:1], rs[:, t:t + 1], ALU.subtract, ALU.mult).then_inc(a_dve, 1)

            def b1(nb):
                have, bias = known(v, nb * B_N + 1 + NB), known(v, nb * B_N + 1)
                v.wait_ge(b_h, nb + 1)
                if not (isinstance(nb, int) and nb == 0):
                    v.wait_ge(b_gelu, nb)
                v.tensor_tensor(hr[:, :, :], pH[:, :].rearrange("p (t e) -> p t e", e=RH),
                                br1[:, :].unsqueeze(1).to_broadcast([P, NB, RH]), ALU.add).then_inc(b_dve, 1)
                v.wait_ge(setp, SETP)
                v.wait_ge(b_dve, bias)
                for t in range(NB):
                    v.bn_stats(st2[:, t, :], hr[:, t, :]).then_inc(b_dve, 1)
                v.wait_ge(setp, SETP)
                v.wait_ge(b_dve, have)
                for t in range(NB):
                    v.bn_aggr(mv2[:, t, :], st2[:, t, :]).then_inc(b_dve, 1)

            def b2(nb):
                v.wait_ge(b_rs, nb * 2 + 2)
                for t in range(NB):
                    v.tensor_scalar(hr[:, t, :], hr[:, t, :], mv2[:, t, 0:1], rs2[:, t:t + 1], ALU.subtract, ALU.mult).then_inc(b_dve, 1)
                v.wait_ge(b_dve, nb * B_N + B_STATS + NB)
                v.tensor_tensor(hr[:, :, :], hr[:, :, :], lns[:, :].unsqueeze(1).to_broadcast([P, NB, RH]), ALU.mult).then_inc(b_dve, 1)
                v.wait_ge(b_dve, nb * B_N + B_STATS + NB + 1)
                v.tensor_tensor(hr[:, :, :], hr[:, :, :], lnb[:, :].unsqueeze(1).to_broadcast([P, NB, RH]), ALU.add).then_inc(b_dve, 1)

            def c1(nb, k):
                at = nb * C_N
                v.wait_ge(b_lg, nb + 1)
                v.tensor_tensor(lg[:, :, :], pL[:, :].rearrange("p (t e) -> p t e", e=NX),
                                br2[:, :].unsqueeze(1).to_broadcast([P, NB, NX]), ALU.add).then_inc(c_dve, 1)
                biased, best = known(v, at + 1), known(v, at + 1 + NB)
                v.wait_ge(setp, SETP)
                v.wait_ge(c_dve, biased)
                for t in range(NB):
                    v.max(mx[:, t, :], lg[:, t, :]).then_inc(c_dve, 1)
                v.wait_ge(setp, SETP)
                v.wait_ge(c_dve, best)
                for t in range(NB):
                    v.max_index(mi[:, t, :], mx[:, t, :], lg[:, t, :]).then_inc(c_dve, 1)
                v.tensor_tensor(dlt[:, bass.ds(nb * NB, NB)], mx[:, :, 1], mx[:, :, 0], ALU.subtract).then_inc(c_dve, 1)
                v.wait_ge(c_dve, at + 2 + 2 * NB)
                v.tensor_copy(xf[:, :, :], mi[:, :, 0:TOPK]).then_inc(c_dve, 1)
                v.wait_ge(c_dve, at + 3 + 2 * NB)
                v.tensor_copy(rows[k][:, :, E + 1], xf[:, :, 0]).then_inc(c_dve, 1)
                v.tensor_tensor(oh[:, :, :, :], xf[:, :, :].unsqueeze(3).to_broadcast([P, NB, TOPK, NX]),
                                iota8[:, :].unsqueeze(1).unsqueeze(1).to_broadcast([P, NB, TOPK, NX]), ALU.is_equal).then_inc(c_dve, 1)
                v.wait_ge(c_dve, at + 5 + 2 * NB)
                v.tensor_tensor(both[:, :, :], oh[:, :, 0, :], oh[:, :, 1, :], ALU.add).then_inc(c_dve, 1)

            def c2(nb, k):
                at = nb * C_N + C_BOTH
                v.wait_ge(c_rank, nb + 1)
                v.tensor_tensor(pos[:, :, :], pR[:, 0:NB * NX].rearrange("p (t e) -> p t e", e=NX),
                                carry[:, :].unsqueeze(1).to_broadcast([P, NB, NX]), ALU.add).then_inc(c_dve, 1)
                v.wait_ge(c_dve, at + 1)
                v.tensor_tensor(carry[:, :], carry[:, :], pR[:, NB * NX:NB * NX + NX], ALU.add).then_inc(c_dve, 1)
                v.wait_ge(c_dve, at + 2)
                v.tensor_tensor(prod[:, :, :, :], oh[:, :, :, :], pos[:, :, :].unsqueeze(2).to_broadcast([P, NB, TOPK, NX]), ALU.mult).then_inc(c_dve, 1)
                v.wait_ge(c_dve, at + 3)
                v.tensor_reduce(posf[:, :, :], prod[:, :, :, :], AX.X, ALU.add).then_inc(c_dve, 1)
                v.wait_ge(c_dve, at + 4)
                v.tensor_copy(idx[k][:, :, :], posf[:, :, :]).then_inc(c_dve, 1)

            a1(0, 0, 0)
            a2(0, 0, False)
            a1(1, 1, 0)
            a2(1, 1, False)
            b1(0)
            b2(0)
            a1(2, 2, 0)
            a2(2, 2, False)
            with v.Fori(0, B // UNROLL) as it:
                for k in range(UNROLL):
                    nb = it * UNROLL + k
                    c1(nb, k)
                    b1(nb + 1)
                    c2(nb, k)
                    b2(nb + 1)
                    a1(nb + 3, (k + 3) % UNROLL, it + (k + 3) // UNROLL)
                    v.wait_ge(w1_hi, nb + 1)
                    part = bass.ds(nb * (2 * F), 2 * F)
                    v.tensor_tensor(keep["w1_l"][:, part], keep["w1_l"][:, part].bitcast(F32), keep["w1_h"][:, part].bitcast(F32), ALU.subtract).then_inc(w1_lo, 1)
                    a2(nb + 3, (k + 3) % UNROLL)
            v.wait_ge(setp, SETP)
            v.wait_ge(c_dve, B * C_N)
            v.tensor_scalar(padrow[:, E:E + 1], pidx[:, :], float((TOPK + 1) * TOKENS), None, ALU.add).then_inc(t_dve, 1)
            v.tensor_copy(padi[:, :], carry[0:1, :]).then_inc(t_dve, 1)
            v.tensor_scalar(start[:, :], iota8[:, :], float(REGION), None, ALU.mult).then_inc(t_dve, 1)
            v.wait_ge(t_dve, 3)
            v.tensor_tensor(cnt[:, :], carry[:, :], start[:, :], ALU.subtract).then_inc(t_dve, 1)
            v.wait_ge(t_dve, 4)
            v.tensor_scalar(ti32[:, :], cnt[:, :], float(P - 1), None, ALU.add).then_inc(t_dve, 1)
            v.wait_ge(t_dve, 5)
            v.tensor_scalar(ti32[:, :], ti32[:, :], 7, None, ALU.arith_shift_right).then_inc(t_dve, 1)
            v.wait_ge(t_dve, 6)
            v.tensor_copy(tiles[:, :], ti32[:, :]).then_inc(t_dve, 1)
            v.wait_ge(t_dve, 7)
            v.tensor_copy(cum[:, 0:1], tiles[:, 0:1]).then_inc(t_dve, 1)
            for e in range(1, NX):
                v.wait_ge(t_dve, 7 + e)
                v.tensor_tensor(cum[:, e:e + 1], cum[:, e - 1:e], tiles[:, e:e + 1], ALU.add).then_inc(t_dve, 1)
            v.wait_ge(t_dve, 15)
            every = lambda a: a.unsqueeze(1).to_broadcast([P, TABLE, NX - 1])
            v.tensor_tensor(past[:, :, :], tno[:, :].unsqueeze(2).to_broadcast([P, TABLE, NX - 1]), every(cum[:, 0:NX - 1]), ALU.is_ge).then_inc(t_dve, 1)
            v.wait_ge(t_dve, 16)
            v.tensor_reduce(keep["tile_expert"][:, :], past[:, :, :], AX.X, ALU.add).then_inc(t_dve, 1)
            v.tensor_tensor(used[:, :, :], past[:, :, :], every(tiles[:, 0:NX - 1]), ALU.mult).then_inc(t_dve, 1)
            v.wait_ge(t_dve, 18)
            v.tensor_reduce(first[:, :], used[:, :, :], AX.X, ALU.add).then_inc(t_dve, 1)
            v.tensor_scalar(cap[:, :], keep["tile_expert"][:, :], float(NX - 1), -float(REGION), ALU.subtract, ALU.mult).then_inc(t_dve, 1)
            v.wait_ge(t_dve, 20)
            v.tensor_tensor(first[:, :], tno[:, :], first[:, :], ALU.subtract).then_inc(t_dve, 1)
            v.tensor_scalar(cap[:, :], cap[:, :], cnt[:, NX - 1:NX], None, ALU.add).then_inc(t_dve, 1)
            v.wait_ge(t_dve, 22)
            v.tensor_scalar(first[:, :], first[:, :], float(P), None, ALU.mult).then_inc(t_dve, 1)
            v.wait_ge(t_dve, 23)
            v.tensor_tensor(first[:, :], first[:, :], cap[:, :], ALU.min).then_inc(t_dve, 1)
            v.wait_ge(t_dve, 24)
            v.tensor_scalar(cap[:, :], keep["tile_expert"][:, :], float(REGION), None, ALU.mult).then_inc(t_dve, 1)
            v.wait_ge(t_dve, 25)
            v.tensor_tensor(keep["row_no"][:, :], first[0:1, :], cap[0:1, :], ALU.add).then_inc(t_dve, 1)
            v.tensor_copy(keep["expert_no"][:, :], keep["tile_expert"][0:1, :]).then_inc(t_dve, 1)
            v.wait_ge(t_exp, 1)
            g0, g1 = keep["gate"][:, 0, :], keep["gate"][:, 1, :]
            v.tensor_scalar(g0, ex[:, :], 1.0, None, ALU.add).then_inc(t_dve, 1)
            v.wait_ge(t_dve, 28)
            v.reciprocal(g0, g0).then_inc(t_dve, 1)
            v.wait_ge(t_dve, 29)
            v.tensor_tensor(g1, ex[:, :], g0, ALU.mult).then_inc(t_dve, 1)
            v.wait_ge(t_dve, 30)


def expert_phase(nc, dram, keep):
    ctx = ExitStack()
    with ctx:
        def sb(name, shape, dt=F32):
            return ctx.enter_context(nc.sbuf_tensor(name, shape, dt))

        def pb(name, shape):
            return ctx.enter_context(nc.psum_tensor(name, shape, F32))

        def sem(name):
            return ctx.enter_context(nc.semaphore(name))
        two = range(2)
        ident = keep["ident"]
        xg = [sb(f"xg{i}", [P, ROW]) for i in range(TURNS)]
        xT = [(sb(f"xT_h{i}", [P, P], F32R), sb(f"xT_l{i}", [P, P], F32R)) for i in range(TURNS)]
        gate_in, lin = [sb(f"gate_in{i}", [P, F]) for i in two], [sb(f"lin{i}", [P, F]) for i in two]
        gl, g = [sb(f"gl{i}", [P, F]) for i in two], [sb(f"g{i}", [P, F]) for i in two]
        gT = [sb(f"gT{i}", [P, F]) for i in two]
        yb = [sb(f"yb{i}", [P, E]) for i in range(TURNS)]
        other, dst = [sb(f"other{i}", [P, 1]) for i in range(TURNS)], [sb(f"dst{i}", [P, 1], U32) for i in range(TURNS)]
        pLin, pGate = [pb(f"pLin{i}", [P, F]) for i in two], [pb(f"pGate{i}", [P, F]) for i in two]
        pTurn, pGT = pb("pTurn", [P, P]), pb("pGT", [P, F])
        pY = [pb(f"pY{i}", [P, E]) for i in two]
        x_in = [sem(f"rows_in{i}") for i in range(TURNS)]
        x_tr, x_hi, x_lo, up_gate, up_lin = (sem(n) for n in ("x_turned", "x_high", "x_low", "gate_up", "linear_up"))
        gate_biased, lin_biased, gelu, prod, places = (sem(n) for n in ("gate_biased", "linear_biased", "gelu_done", "product_done", "places"))
        choice, pad_slot = sem("choice"), sb("pad_slot", [P, TURNS])
        gt, gt_ev, down, y_done, going = (sem(n) for n in ("g_turned", "g_evacuated", "down_done", "y_done", "going"))
        y_out = [sem(f"y_out{i}") for i in range(TURNS)]
        block = ctx.enter_context(nc.Block())
        STEPS = TILES // TURNS

        def first(i, n):
            return isinstance(i, int) and i < n

        def load_experts(engine, i, n):
            return nc.values_load_multi_w_load_instructions(keep["expert_no"][0:1, bass.ds(i, n)], engines=(engine,), min_val=0, max_val=NX - 1,
                                        skip_runtime_bounds_check_because="a count of the seven first experts")[1]

        def steps(eng, step):
            for k in range(TURNS):
                step(0, k)
            with eng.Fori(1, STEPS) as it:
                for k in range(TURNS):
                    step(it, k)

        @block.sync
        def _(sp):
            def load(i, k):
                row = nc.values_load(keep["row_no"][0:1, bass.ds(i, 1)], engines=(mybir.EngineType.SP,), min_val=0, max_val=NX * REGION - P,
                                     skip_runtime_bounds_check_because="a tile of a region")
                sp.dma_start(xg[k][:, :], dram["xs"][bass.ds(row, P), :]).then_inc(x_in[k], 16)

            def step(it, k):
                i = it * TURNS + k
                sp.wait_ge(x_tr, known(sp, i + 1))
                sp.wait_ge(places, known(sp, i + 1))
                load(i + TURNS, k)
            for k in range(TURNS):
                load(k, k)
            steps(sp, step)
            for k in range(TURNS):
                sp.wait_ge(x_in[k], (STEPS + 1) * 16)

        @block.gpsimd
        def _(po):
            def place(i, k):
                k, ahead = k % TURNS, known(po, i + 1)
                po.wait_ge(going, 2)
                po.wait_ge(choice, ahead)
                po.tensor_scalar(dst[k][:, :], other[k][:, :], xg[k][:, E:E + 1], pad_slot[:, k:k + 1], ALU.add, ALU.min).then_inc(places, 1)

            def step(it, k):
                i = it * TURNS + k
                place(i + 2, k + 2)
                tile = known(po, i + 1)
                po.wait_ge(going, 2)
                po.wait_ge(places, tile)
                po.wait_ge(y_done, tile)
                po.indirect_dma_start(dram["ys"], bass.IndirectOffsetOnAxis(dst[k][:, :], 0), yb[k][:, :], None).then_inc(y_out[k], 16)
            po.sem_inc(going, 1)
            po.iota(pad_slot[:, :], pattern=[[P, TURNS]], base=TOPK * TOKENS, channel_multiplier=1, allow_small_or_imprecise_dtypes=True).then_inc(going, 1)
            place(0, 0)
            place(1, 1)
            steps(po, step)
            for k in range(TURNS):
                po.wait_ge(y_out[k], STEPS * 16)

        @block.tensor
        def _(pe):
            def turn(it, k):
                pe.wait_ge(x_in[k], it * 16 + 16)
                pe.transpose(pTurn[:, :], xg[k][:, 0:E], ident[:, :]).then_inc(x_tr, 1)

            def up_half(k, ex, half):
                dst_ = (pLin, pGate)[half][k % 2]
                at = ex * (2 * F) + half * F
                for n, (x, w) in enumerate(((0, "w1_h"), (1, "w1_h"), (0, "w1_l"))):
                    mm = pe.matmul(dst_[:, :], xT[k % TURNS][x][:, :], keep[w][:, bass.ds(at, F)], start=(n == 0), stop=(n == 2))
                mm.then_inc((up_lin, up_gate)[half], 1)

            def turn_g(i, k):
                pe.wait_ge(prod, i + 1)
                for c in range(F // P):
                    mm = pe.transpose(pGT[:, P * c:P * c + P], g[k % 2][:, P * c:P * c + P], ident[:, :])
                mm.then_inc(gt, 1)

            def out(i, k, ex):
                pe.wait_ge(gt_ev, i + 1)
                for c in range(F // P):
                    mm = pe.matmul(pY[k % 2][:, :], gT[k % 2][:, P * c:P * c + P], keep["w2"][:, bass.ds(ex * F + c * E, E)], start=(c == 0), stop=(c == F // P - 1))
                mm.then_inc(down, 1)

            def step(it, k):
                i = it * TURNS + k
                if k == 0:
                    step.experts = load_experts(mybir.EngineType.PE, i, TURNS + 2)
                turn_g(i, k)
                pe.wait_ge(x_lo, i + 3)
                turn(it + (k + 3) // TURNS, (k + 3) % TURNS)
                up_half(k + 2, step.experts[k + 2], 1)
                up_half(k + 2, step.experts[k + 2], 0)
                out(i, k, step.experts[k])

            turn(0, 0)
            for k in range(1, 3):
                pe.wait_ge(x_lo, k)
                turn(0, k)
            ex = load_experts(mybir.EngineType.PE, 0, 2)
            for k in two:
                up_half(k, ex[k], 1)
                up_half(k, ex[k], 0)
            steps(pe, step)

        @block.scalar
        def _(act):
            def turned(i, k):
                act.wait_ge(x_tr, i + 1)
                act.activation(xT[k % TURNS][0][:, :], pTurn[:, :], ACT.Copy).then_inc(x_hi, 1)

            def gelu_of(i, k):
                act.wait_ge(gate_biased, i + 1)
                act.activation(gl[k % 2][:, :], gate_in[k % 2][:, :], ACT.Gelu_apprx_tanh).then_inc(gelu, 1)

            def step(it, k):
                i = it * TURNS + k
                gelu_of(i + 1, k + 1)
                act.wait_ge(gt, i + 1)
                act.activation(gT[k % 2][:, :], pGT[:, :], ACT.Copy).then_inc(gt_ev, 1)
                turned(i + 3, k + 3)

            turned(0, 0)
            turned(1, 1)
            turned(2, 2)
            gelu_of(0, 0)
            steps(act, step)

        @block.vector
        def _(v):
            def low(i, k):
                v.wait_ge(x_hi, i + 1)
                v.tensor_tensor(xT[k % TURNS][1][:, :], pTurn[:, :], xT[k % TURNS][0][:, :].bitcast(F32), ALU.subtract).then_inc(x_lo, 1)

            def gate_bias(i, k, ex):
                v.wait_ge(up_gate, i + 1)
                v.tensor_tensor(gate_in[k % 2][:, :], pGate[k % 2][:, :], keep["b1"][:, bass.ds(ex * (2 * F) + F, F)], ALU.add).then_inc(gate_biased, 1)

            def lin_bias(i, k, ex):
                v.wait_ge(up_lin, i + 1)
                v.tensor_tensor(lin[k % 2][:, :], pLin[k % 2][:, :], keep["b1"][:, bass.ds(ex * (2 * F), F)], ALU.add).then_inc(lin_biased, 1)

            def slot(it, k):
                if not first(it, 1):
                    v.wait_ge(y_out[k], it * 16)
                v.tensor_scalar(other[k][:, :], xg[k][:, E + 1:E + 2], keep["tile_expert"][:, bass.ds(it * TURNS + k, 1)], -float(TOKENS), ALU.is_equal, ALU.mult).then_inc(choice, 1)

            def product(i, k):
                v.wait_ge(gelu, i + 1)
                v.wait_ge(lin_biased, i + 1)
                v.tensor_tensor(g[k % 2][:, :], lin[k % 2][:, :], gl[k % 2][:, :], ALU.mult).then_inc(prod, 1)

            def step(it, k):
                i = it * TURNS + k
                if k == 0:
                    step.experts = load_experts(mybir.EngineType.DVE, i, TURNS + 2)
                this = step.experts[k]
                product(i + 1, k + 1)
                low(i + 3, k + 3)
                gate_bias(i + 2, k + 2, step.experts[k + 2])
                lin_bias(i + 2, k + 2, step.experts[k + 2])
                slot(it + (k + 2) // TURNS, (k + 2) % TURNS)
                v.wait_ge(down, i + 1)
                v.tensor_tensor(yb[k][:, :], pY[k % 2][:, :], keep["b2"][:, bass.ds(this * E, E)], ALU.add).then_inc(y_done, 1)

            for k in range(3):
                low(k, k)
            ex = load_experts(mybir.EngineType.DVE, 0, 2)
            for k in two:
                gate_bias(k, k, ex[k])
                lin_bias(k, k, ex[k])
            product(0, 0)
            slot(0, 0)
            slot(0, 1)
            steps(v, step)


def combine_phase(nc, dram, keep):
    ctx = ExitStack()
    with ctx:
        def sb(name, shape, dt=F32):
            return ctx.enter_context(nc.sbuf_tensor(name, shape, dt))

        def sem(name):
            return ctx.enter_context(nc.semaphore(name))
        x2 = keep["x2"]
        y = [[sb(f"y{j}_{b}", [P, NB, E]) for b in range(B)] for j in range(TOPK)]
        d_in = [sem(f"sum_in{b}") for b in range(B)]
        s_dve, d_out = sem("summed"), sem("out_done")
        block = ctx.enter_context(nc.Block())

        @block.sync
        def _(sp):
            for b in range(B):
                for j in range(TOPK):
                    lo = TOKENS * j + S * b
                    sp.dma_start(y[j][b][:, :, :], dram["ys"][lo:lo + S].rearrange("(t p) e -> p t e", p=P)).then_inc(d_in[b], 16)
            sp.wait_ge(d_out, B * 16)

        @block.vector
        def _(v):
            n = 0
            for b in range(B):
                v.wait_ge(d_in[b], TOPK * 16)
                for j in range(TOPK):
                    for t in range(NB):
                        c = b * NB + t
                        if j and t == 0:
                            v.wait_ge(s_dve, n)
                        v.scalar_tensor_tensor(x2[b][:, t, :], y[j][b][:, t, :], keep["gate"][:, j, c:c + 1], x2[b][:, t, :], ALU.mult, ALU.add).then_inc(s_dve, 1)
                        n += 1

        @block.scalar
        def _(act):
            for b in range(B):
                act.wait_ge(s_dve, (b + 1) * TOPK * NB)
                act.dma_start(dram["out"][b].rearrange("(t p) e -> p t e", p=P), x2[b][:, :, :]).then_inc(d_out, 16)


def ffn_layout(i):
    import numpy as np
    a = {k[7:]: np.asarray(v) for k, v in i.items() if k.startswith("L0_ffn_")}
    return {"wr1": a["Wr1"], "br1": a["br1"], "lns": a["ln_scale"], "lnb": a["ln_bias"], "wr2": a["Wr2"], "br2": a["br2"],
            "w1": a["W1"], "w2": a["W2"], "b1": a["b1"].reshape(-1), "b2": a["b2"].reshape(-1)}


def kernel(**inputs):
    import numpy as np
    import concourse.bacc as bacc
    from concourse.bass_utils import run_bass_kernel_spmd as run
    nc = bacc.Bacc("TRN2", target_bir_lowering=False, num_devices=1)
    arrays = {k: np.ascontiguousarray(v) for k, v in {**att_layout(inputs), **ffn_layout(inputs)}.items()}
    dram = {k: nc.dram_tensor("in_" + k, v.shape, F32, kind="ExternalInput").ap() for k, v in arrays.items()}
    dram["out"] = nc.dram_tensor("out", [B, S, E], F32, kind="ExternalOutput").ap()
    dram["operands"] = nc.dram_tensor("split_operands", [B + 1, 3, H, 4, D, S], F32).ap()
    dram["x2s"] = nc.dram_tensor("after_attention", [B + 1, S, E], F32).ap()
    dram["xs"] = nc.dram_tensor("routed_rows", [NX * REGION, ROW], F32).ap()
    dram["ys"] = nc.dram_tensor("expert_rows", [TOPK * TOKENS + TURNS * P, E], F32).ap()
    attention_phase(nc, dram)
    with ExitStack() as ctx:
        keep = sum_tensors(nc, ctx)
        with ExitStack() as inner:
            experts = {**keep, **expert_tensors(nc, inner)}
            routing_phase(nc, dram, experts)
            expert_phase(nc, dram, experts)
        combine_phase(nc, dram, keep)
    return run(nc, [{"in_" + k: v for k, v in arrays.items()}], core_ids=[0]).results[0]["out"]
```

```python
from contextlib import ExitStack

import concourse.bass as bass
from concourse import mybir

F32, F32R, BF16 = mybir.dt.float32, mybir.dt.float32r, mybir.dt.bfloat16
I32, U32 = mybir.dt.int32, mybir.dt.uint32
ALU = mybir.AluOpType
ACT = mybir.ActivationFunctionType
AX = mybir.AxisListType

B, S, E, H = 8, 1024, 128, 8
D = E // H
P = 128
NB = S // P
SCALE = float(E) ** -0.5
LN_EPS = 1e-5
FAR = -1.0e30
HALF = 512
HPB = S // HALF
S1U = NB * HPB + HPB
S2U = NB + 1
S1_BUFS = 3
RING = 4
LATE = 2
SLOTS = 4
AHEAD = 2
FEAT = 2 * D
KROWS = 3 * FEAT
MROW = KROWS
STK = 6 * 16
STRIPS = 4
VW = 32
RH = 64
NX = 8
TOPK = 2
F = 512
ROUTER_EPS = 1e-6
TOKENS = B * S
HALVES = 2
ROWS = HALVES * P
REGION = TOKENS + ROWS
ROW = E + 2
TILES = TOPK * TOKENS // ROWS + NX
TABLE = TILES + 4
TURNS = 4
CHUNKS = F // P
UNROLL = 4


def known(eng, value):
    return value if isinstance(value, int) else eng.to_reg(value)


def attention_phase(nc, dram):
    ctx = ExitStack()
    with ctx:
        def sb(name, shape, dt=F32):
            return ctx.enter_context(nc.sbuf_tensor(name, shape, dt))

        def pb(name, shape):
            return ctx.enter_context(nc.psum_tensor(name, shape, F32))

        def sem(name):
            return ctx.enter_context(nc.semaphore(name))

        w_q, w_k, w_v, w_p, w_o = (sb(n, [P, P]) for n in ("w_q", "w_k", "w_v", "w_p", "w_o"))
        cols = sb("cols", [P, 5])
        bv_wide = sb("bv_wide", [P, P])
        bias_qv, bias_qu = sb("bias_qv", [P, 1]), sb("bias_qu", [P, 1])
        bo_rows = sb("bo_rows", [P, E])
        vu = sb("vu", [P, 2])
        rot = [sb(n, [P, S]) for n in ("cos_lo", "sin_lo", "cos_up", "sin_up")]
        ident, hsum = sb("ident", [P, P]), sb("hsum", [P, H])
        lmask, umask = sb("lmask", [P, 15 * P], BF16), sb("umask", [P, P])
        cmask = sb("cmask", [P, H, NB])
        xt = sb("xt", [P, NB, E])
        st6, mv, rs = sb("st6", [P, NB, 6]), sb("mv", [P, NB, 2]), sb("rs", [P, 3, NB])
        mhalf = sb("mhalf", [P, NB])
        xnT = sb("xnT", [P, S + 1])
        qv, qu, kc = sb("qv", [P, S]), sb("qu", [P, S]), sb("kc", [P, S + 1])
        rp, rq = sb("rp", [P, S + 1]), sb("rq", [P, S + 1])
        g_lo, g_up, t2, t3 = (sb(n, [P, S]) for n in ("g_lo", "g_up", "t2", "t3"))
        xn = g_up[:, :].rearrange("p (t e) -> p t e", e=E)
        parts = {n: (sb(n + "_h", [P, S], F32R), sb(n + "_l", [P, S], F32R)) for n in ("c", "k", "gl", "gu", "pe")}
        QL, QU, K = (sb(n, [P, SLOTS, S], F32R) for n in ("QL", "QU", "K"))
        prob = [sb(f"prob{i}", [P, S]) for i in range(RING)]
        ctxp = sb("ctxp", [P, S // STRIPS])
        ctx_all = sb("ctx_all", [P, NB, H, D + 1])
        vext = sb("vext", [P, NB, H, VW])
        held = sb("held", [P, NB, H // 2, D])
        vsh = sb("vsh", [P, NB, H, D])
        acc = sb("acc", [P, H, NB, 4])
        mneg = sb("mneg", [P, H, NB], F32R)
        dsup, psup = sb("dsup", [P, H, NB]), sb("psup", [P, H, NB])
        den = sb("den", [P, NB, H])
        mrow = [sb(f"mrow{i}", [NB, P], F32R) for i in range(2)]
        junk = sb("junk", [P, S1_BUFS, HALF], BF16)
        ctxT = t3
        xres = sb("xres", [P, NB, E])
        pA = [pb(f"pA{i}", [P, HALF]) for i in range(S1_BUFS)]
        pB, pC = pb("pB", [P, S]), pb("pC", [P, S // STRIPS])
        pM, pE = pb("pM", [P, HALF]), pb("pE", [P, HALF])

        d_w, d_cst, d_x, d_res, d_x2 = sem("weights_in"), sem("constants_in"), sem("x_in"), sem("residual_in"), sem("x2_out")
        set_pool, set_dve = sem("set_pool"), sem("set_dve")
        s1_ready, s1_read = sem("s1_ready"), sem("s1_read")
        mx_done, dsup_done = sem("mx_done"), sem("dsup_done")
        mrow_in = [sem(f"mrow_in{i}") for i in range(2)]
        s2_ready, p_exp, p_mask, pv_done = sem("s2_ready"), sem("p_exp"), sem("p_mask"), sem("pv_done")
        ctx_evac, psup_done = sem("ctx_evac"), sem("psup_done")
        m_ready, m_done, w_ready, w_done = sem("m_ready"), sem("m_done"), sem("w_ready"), sem("w_done")
        e_ready, e_done, hi_done = sem("e_ready"), sem("e_done"), sem("hi_done")
        ln, low_done, pos, norm, rs_done, res_done = (sem(n) for n in ("ln", "low_done", "positions", "norm", "rs_done", "residual_biased"))
        placed = sem("last_heads_values")
        upper, swapped = sem("first_upper_form"), sem("r_swapped")
        stk, stored = [sem(f"stk{i}") for i in range(SLOTS)], sem("operands_stored")
        block = ctx.enter_context(nc.Block())

        LN_N, LOW_N, POS_N, NORM_N, HI_N, RS_N = 3 * NB, 4, 14, 5, 4, 7
        E_AT = [1, 2, 4, 6, 7, 8, 9, 10]
        E_N, PIECES = E_AT[-1], len(E_AT)
        M_ORDER = {(h, u): name for h in range(H) for u, name in ((1, "row"), (3, "context"))}
        M_ORDER.update({(1, 5): "project 1", (1, 7): "shifted 1", (6, 6): "values 0"})
        W_ORDER = {(1, 0): "turn 0", (1, 2): "turn 1", (1, 4): "project 0", (1, 6): "shifted 0", (6, 5): "super", (6, 7): "values 1"}
        SPREAD = {"super": ((6, 0), (6, 2), (6, 4), (6, 5))}
        PARTS = {**{place: (name, 0, 1) for order in (M_ORDER, W_ORDER) for place, name in order.items() if name not in SPREAD},
                 **{place: (name, i, len(places)) for name, places in SPREAD.items() for i, place in enumerate(places)}}
        HIGH_AT = ((3, 3), (3, 4), (4, 1), (4, 6))
        LOW_AT = ((3, 4), (3, 5), (4, 2), (4, 7))
        NORMALIZE_AT = (1, 4, 5, 6, 7)
        COPIES = ("values 0", "values 1", "turn 0", "turn 1", "shifted 0", "shifted 1")
        M_PLACES = sorted(M_ORDER)
        M_PRO, M_N = 5, len(M_PLACES)
        M_IDX = {place: n for n, place in enumerate(M_PLACES)}
        M_OF = {M_ORDER[place]: n for place, n in M_IDX.items()}
        W_OF = {W_ORDER[place]: n for n, place in enumerate(sorted(W_ORDER))}
        W_PRO, W_N = 1, len(W_ORDER)
        PLACES = {"c": ((0, 0), (1, 0)), "k": ((2, 0),), "pe": ((2, 1),), "gl": ((0, 1),), "gu": ((1, 1),)}
        ST_N = 16 * 2 * sum(len(p) for p in PLACES.values())
        DVE_SET, DVE_BIAS, POOL_SET = 14, 12, 15
        D_W, D_CST = 16 * 8, 16 * 6

        def piece(n):
            qb, k0 = n // HPB, (n % HPB) * HALF
            return qb, k0, min(max(P * (qb + 1) - k0, 0), HALF)

        @block.sync
        def _(sp):
            sp.dma_start(xt[:, :, :], dram["x"][0].rearrange("(t p) e -> p t e", p=P)).then_inc(d_x, 16)
            for t, n in ((w_q, "wq"), (w_k, "wk"), (w_v, "wv"), (w_p, "wp"), (w_o, "wo")):
                sp.dma_start(t[:, :], dram[n]).then_inc(d_w, 16)
            sp.dma_start(cols[:, :], dram["cols"]).then_inc(d_w, 16)
            sp.dma_start(vu[:, :], dram["vu"]).then_inc(d_w, 16)
            sp.dma_start(bo_rows[:, :], dram["bo"].partition_broadcast(P)).then_inc(d_w, 16)
            for i, t in enumerate(rot):
                sp.dma_start(t[:, :], dram["rot"][i]).then_inc(d_cst, 16)
            sp.dma_start(g_lo[:, :], dram["pe"]).then_inc(d_cst, 16)
            sp.dma_start(hsum[:, :], dram["hsum"]).then_inc(d_cst, 16)

            def store(nb, names):
                for name in names:
                    for op, row in PLACES[name]:
                        for low in range(2):
                            sp.dma_start(dram["operands"][bass.ds(nb, 1), op, :, 2 * low + row, :, :].rearrange("o h d s -> (o h) d s"),
                                         parts[name][low][:, :].bitcast(F32)).then_inc(stored, 16)

            def swap(nb):
                sp.wait_ge(e_done, nb * E_N + E_N)
                for odd in range(2):
                    sp.dma_start(rq[odd:P:2, 0:S], rp[1 - odd:P:2, 0:S]).then_inc(swapped, 16)

            def stack(nb, h):
                s = h % SLOTS
                for op, dst in enumerate((QL, QU, K)):
                    split = FEAT if dst is K else 2 * FEAT
                    for lo, hi in ((0, split), (split, KROWS)):
                        sp.dma_start(dst[lo:hi, s, :].bitcast(F32),
                                     dram["operands"][bass.ds(nb, 1), op, h % H, 0:(hi - lo) // D, :, :].rearrange("o g d s -> (o g) d s")).then_inc(stk[s], 16)

            def maximum_row(h):
                s = h % SLOTS
                for dst in (QL, QU):
                    sp.dma_start(dst[MROW:MROW + 1, s, :].bitcast(F32).rearrange("o (n p) -> o n p", p=P),
                                 mrow[h % 2][:, :].bitcast(F32)).then_inc(mrow_in[h % 2], 16)

            sp.sem_inc(d_x2, 16)
            sp.wait_ge(set_dve, DVE_SET)
            sp.wait_ge(ln, LN_N)
            sp.dma_start(xt[:, :, :], dram["x"][1 % B].rearrange("(t p) e -> p t e", p=P)).then_inc(d_x, 16)
            swap(0)
            for names, n in ((("c", "k", "pe"), 2), (("gl",), 3), (("gu",), 4)):
                sp.wait_ge(hi_done, n)
                sp.wait_ge(low_done, n)
                store(0, names)
            sp.wait_ge(stored, ST_N)
            for h in range(3):
                stack(0, h)
            sp.wait_ge(m_done, M_PRO)
            maximum_row(0)
            with sp.Fori(0, B) as b:
                for h in range(H):
                    if h == 0:
                        written = known(sp, b * 16 + 16)
                        sp.wait_ge(set_dve, DVE_SET)
                        sp.wait_ge(d_x2, written)
                        sp.dma_start(xres[:, :, :], dram["x"][bass.ds((b + B - 1) % B, 1)].rearrange("o (t p) e -> p (o t) e", p=P)).then_inc(d_res, 16)
                    if h == 2:
                        normed = known(sp, (b + 2) * LN_N)
                        sp.wait_ge(set_dve, DVE_SET)
                        sp.wait_ge(ln, normed)
                        sp.dma_start(xt[:, :, :], dram["x"][bass.ds((b + 2) % B, 1)].rearrange("o (t p) e -> p (o t) e", p=P)).then_inc(d_x, 16)
                    if h == 3:
                        swap(b + 1)
                    through, in_dram = known(sp, HPB * (b * (H * S2U) + h * S2U) + 1), known(sp, (b + 2) * ST_N)
                    sp.wait_ge(set_dve, DVE_SET)
                    sp.wait_ge(s2_ready, through)
                    if h + 3 == H:
                        sp.wait_ge(stored, in_dram)
                    stack(b + (h + 3) // H, h + 3)
                    sp.wait_ge(m_done, b * M_N + M_PRO + M_IDX[h, 1] + 1)
                    maximum_row(h + 1)
                    if h in (3, 4):
                        highs, lows = known(sp, (b + 1) * HI_N + 2 * (h - 2)), known(sp, (b + 1) * LOW_N + 2 * (h - 2))
                        sp.wait_ge(set_dve, DVE_SET)
                        sp.wait_ge(hi_done, highs)
                        sp.wait_ge(low_done, lows)
                        store(b + 1, ("c", "k", "pe") if h == 3 else ("gl", "gu"))
                    if h == 2:
                        sp.wait_ge(m_done, b * M_N + M_PRO + M_OF["project 1"] + 1)
                        sp.dma_start(dram["x2s"][bass.ds(b, 1)].rearrange("o (t p) e -> p (o t) e", p=P), xres[:, :, :]).then_inc(d_x2, 16)
            sp.wait_ge(d_x2, (B + 1) * 16)
            sp.dma_start(xres[:, :, :], dram["x"][B - 1].rearrange("(t p) e -> p t e", p=P)).then_inc(d_res, 16)
            sp.wait_ge(m_done, B * M_N + M_PRO + 5)
            sp.dma_start(dram["x2s"][B].rearrange("(t p) e -> p t e", p=P), xres[:, :, :]).then_inc(d_x2, 16)
            sp.wait_ge(d_x2, (B + 2) * 16)
            for s in range(SLOTS):
                sp.wait_ge(stk[s], (2 * B + (s < 3)) * STK)
            for i in range(2):
                sp.wait_ge(mrow_in[i], (4 * B + 1 - i) * 32)
            sp.wait_ge(stored, (B + 1) * ST_N)
            sp.wait_ge(swapped, (B + 1) * 32)
            sp.wait_ge(d_x, (B + 2) * 16)

        @block.gpsimd
        def _(po):
            po.memset(ident[:, :], 0.0).then_inc(set_pool, 1)
            po.memset(lmask[:, :], 0.0).then_inc(set_pool, 1)
            po.memset(umask[:, :], 0.0).then_inc(set_pool, 1)
            po.memset(cmask[:, :, :], 0.0).then_inc(set_pool, 1)
            po.memset(vext[:, :, :, :], 0.0).then_inc(set_pool, 1)
            for i in range(1, RING):
                po.memset(prob[i][:, :], 1.0).then_inc(set_pool, 1)
            po.memset(mhalf[:, :], -0.5).then_inc(set_pool, 1)
            po.wait_ge(set_pool, 9)
            po.affine_select(out=ident[:, :], in_=ident[:, :], compare_op=ALU.not_equal, fill=1.0, base=0,
                             pattern=[[-1, P]], channel_multiplier=1).then_inc(set_pool, 1)
            po.affine_select(out=lmask[:, 7 * P:8 * P], in_=lmask[:, 7 * P:8 * P], compare_op=ALU.is_ge, fill=FAR, base=0,
                             pattern=[[-1, P]], channel_multiplier=1).then_inc(set_pool, 1)
            po.affine_select(out=umask[:, :], in_=umask[:, :], compare_op=ALU.is_ge, fill=FAR, base=-2,
                             pattern=[[1, P]], channel_multiplier=-1).then_inc(set_pool, 1)
            po.affine_select(out=cmask[:, :, :], in_=cmask[:, :, :], compare_op=ALU.not_equal, fill=FAR, base=1 - S,
                             pattern=[[0, H], [P, NB]], channel_multiplier=1).then_inc(set_pool, 1)
            po.affine_select(out=lmask[:, 8 * P:8 * P + 1], in_=lmask[:, 8 * P:8 * P + 1], compare_op=ALU.not_equal, fill=FAR, base=1 - P,
                             pattern=[[0, 1]], channel_multiplier=1).then_inc(set_pool, 1)
            po.memset(vext[:, :, :, D:D + 1], 1.0).then_inc(set_pool, 1)

            def rstd(nb, i):
                at = nb * RS_N
                if i == 0:
                    variances = known(po, nb * LN_N + 2 * NB)
                    po.wait_ge(set_pool, POOL_SET)
                    po.wait_ge(ln, variances)
                else:
                    before = known(po, at + i)
                    po.wait_ge(set_pool, POOL_SET)
                    po.wait_ge(rs_done, before)
                if i == 0:
                    step = po.tensor_scalar(rs[:, 0, :], mv[:, :, 1], LN_EPS, None, ALU.add)
                elif i == 1:
                    step = po.tensor_tensor(rs[:, 0, :], rs[:, 0, :], mhalf[:, :], ALU.pow)
                elif i == 2:
                    step = po.tensor_tensor(rs[:, 1, :], rs[:, 0, :], rs[:, 0, :], ALU.mult)
                elif i == 3:
                    step = po.tensor_tensor(rs[:, 2, :], rs[:, 1, :], mv[:, :, 1], ALU.mult)
                elif i == 4:
                    step = po.tensor_scalar(rs[:, 2, :], rs[:, 2, :], LN_EPS, None, ALU.add)
                elif i == 5:
                    step = po.tensor_tensor(rs[:, 2, :], rs[:, 2, :], mhalf[:, :], ALU.pow)
                else:
                    step = po.tensor_tensor(rs[:, 2, :], rs[:, 2, :], rs[:, 0, :], ALU.mult)
                step.then_inc(rs_done, 1)

            def positions(nb, i):
                at = nb * POS_N
                half = i % 2
                cut = slice(HALF * half, HALF * half + HALF)
                if i < 2:
                    po.wait_ge(e_done, nb * E_N + E_N)
                    po.tensor_tensor(t2[:, cut], qu[:, cut], kc[:, 1 + HALF * half:1 + HALF * half + HALF], ALU.mult).then_inc(pos, 1)
                    return
                form, step = divmod(i - 2, 6)
                g, cos, sin = ((g_lo, rot[0], rot[1]), (g_up, rot[2], rot[3]))[form]
                src = slice(HALF * half + form, HALF * half + form + HALF)
                if step < 2:
                    po.wait_ge(pos, at + 2 + 6 * form)
                    po.tensor_tensor(g[:, cut], rp[:, src], cos[:, cut], ALU.mult).then_inc(pos, 1)
                elif step < 4:
                    po.wait_ge(pos, at + 2 + 6 * form)
                    if form == 0 and half == 0:
                        po.wait_ge(swapped, nb * 32 + 32)
                    po.tensor_tensor(t3[:, cut], rq[:, src], sin[:, cut], ALU.mult).then_inc(pos, 1)
                else:
                    po.wait_ge(pos, at + i - 1)
                    po.tensor_tensor(g[:, cut], g[:, cut], t3[:, cut], ALU.add).then_inc(pos, 1)

            def residual(b):
                po.wait_ge(d_res, b * 16 + 16)
                po.tensor_tensor(xres[:, :, :], xres[:, :, :], bo_rows[:, :].unsqueeze(1).to_broadcast([P, NB, E]), ALU.add).then_inc(res_done, 1)

            po.sem_inc(p_mask, LATE)
            for i in range(RS_N):
                rstd(0, i)
            po.wait_ge(d_w, D_W)
            po.wait_ge(d_cst, D_CST)
            po.wait_ge(set_dve, DVE_SET)
            for i in range(POS_N - 6):
                positions(0, i)
            po.wait_ge(pos, POS_N - 6)
            po.wait_ge(upper, 3)
            for _ in range(6):
                po.sem_inc(pos, 1)
            for i in range(RS_N):
                rstd(1, i)
            with po.Fori(0, B) as b:
                for h in range(H):
                    for u in range(S2U):
                        n = h * S2U + u
                        units = known(po, HPB * (b * (H * S2U) + n + 2))
                        po.wait_ge(set_pool, POOL_SET)
                        po.wait_ge(p_exp, units)
                        if 0 < u < NB:
                            po.memset(prob[n % RING][0:1, P * u - 1:P * u], 0.0)
                        if u < NB:
                            p = prob[n % RING][:, P * u:P * u + P]
                            po.affine_select(out=p, in_=p, compare_op=ALU.is_ge, fill=0.0, base=0,
                                             pattern=[[1, P]], channel_multiplier=-1).then_inc(p_mask, 1)
                        else:
                            p = prob[n % RING][:, :].rearrange("p (n q) -> p n q", q=P)
                            po.affine_select(out=p, in_=p, compare_op=ALU.is_ge, fill=0.0, base=-2,
                                             pattern=[[0, NB], [-1, P]], channel_multiplier=1).then_inc(p_mask, 1)
                        if (h, u) == (0, 6):
                            residual(b)
                        if h == 7 and u < RS_N:
                            rstd(b + 2, u)
                        if (3, 1) <= (h, u) <= (4, 5):
                            positions(b + 1, (h - 3) * S2U + u - 1)
            residual(B)

        @block.tensor
        def _(pe):
            pe.wait_ge(d_w, D_W)
            pe.wait_ge(d_cst, D_CST)
            pe.wait_ge(set_pool, POOL_SET)
            pe.wait_ge(set_dve, DVE_BIAS)
            pe.sem_inc(s2_ready, 1)
            pe.sem_inc(pv_done, RING - LATE)
            pe.sem_inc(w_done, W_PRO)

            def project(nb, j):
                first = isinstance(nb, int)
                dst = (pE, *pA)[j % 4] if first else pE
                if j == 0:
                    pe.wait_ge(ln, (nb + 1) * LN_N)
                if not first:
                    pe.wait_ge(e_done, nb * E_N + (E_AT[j - 1] if j else 0))
                elif j >= 2:
                    pe.wait_ge(e_done, E_AT[max(j - 4, j % 2 + (2 if j >= 6 else 0))])
                half = slice(HALF * (j % 2), HALF * (j % 2) + HALF)
                if j < 2:
                    for t in range(4):
                        mm = pe.transpose(dst[:, P * t:P * t + P], xn[:, 4 * j + t, :], ident[:, :])
                else:
                    w, src = ((w_q, xnT), (w_k, xnT), (w_p, qv))[j // 2 - 1]
                    mm = pe.matmul(dst[:, :], w[:, :], src[:, half], start=True, stop=True)
                mm.then_inc(e_ready, 1)

            pe.matmul(pM[:, 0:E], bv_wide[:, :], w_o[:, :], start=True, stop=True).then_inc(m_ready, 1)

            def super_scores(part=0, parts=1):
                for blk in range(NB * part // parts, NB * (part + 1) // parts):
                    mm = pe.matmul((pM if parts == 1 else pE)[:, H * blk:H * blk + H], t2[:, P * blk:P * blk + P], hsum[:, :], start=True, stop=True)
                return mm

            def values(half, dst):
                for t in range(4):
                    c = P * (4 * half + t)
                    mm = pe.matmul(dst[:, P * t:P * t + P], xnT[:, c:c + P], w_v[:, :], start=True, stop=True)
                return mm

            def values_shifted(half):
                for t in range(4):
                    c = P * (4 * half + t) + 1
                    mm = pe.matmul((pE, pM)[half][:, P * t:P * t + P], xnT[:, c:c + P], w_v[:, :], start=True, stop=True)
                return mm

            def row_of_maxima(b, h):
                pe.wait_ge(mx_done, b * H + h + 1)
                return pe.transpose(pM[0:NB, 0:P], mneg[:, h % H, :].bitcast(F32), ident[:, :])

            def context_turned(b, h):
                pe.wait_ge(ctx_evac, b * H + h + 2)
                for i in range(S // STRIPS // P):
                    mm = pe.transpose(pM[:, P * i:P * i + P], ctxp[:, P * i:P * i + P], ident[:, :])
                return mm

            def first_pass(b, h, n):
                s = h % SLOTS
                if n == 0:
                    pe.wait_ge(stk[s], b * (2 * STK) + (h // SLOTS + 1) * STK)
                if not (isinstance(b, int) and h == 0 and n < S1_BUFS):
                    pe.wait_ge(s1_read, b * (H * S1U) + h * S1U + n - S1_BUFS + 1)
                dst = pA[n % S1_BUFS]
                if n < NB * HPB:
                    qb, k0, low = piece(n)
                    q = slice(P * qb, P * qb + P)
                    if low > 0:
                        mm = pe.matmul(dst[:, 0:low], QL[0:KROWS, s, q], K[0:KROWS, s, k0:k0 + low], start=True, stop=True)
                    if low < HALF:
                        mm = pe.matmul(dst[:, low:HALF], QU[0:KROWS, s, q], K[0:KROWS, s, k0 + low:k0 + HALF], start=True, stop=True)
                else:
                    for i in range(4):
                        q = slice(P * (4 * (n % 2) + i), P * (4 * (n % 2) + i) + P)
                        mm = pe.matmul(dst[:, P * i:P * i + P], QU[0:KROWS, s, q], K[0:KROWS, s, q], start=True, stop=True)
                mm.then_inc(s1_ready, 1)

            def second_pass(b, h, u, half):
                s = h % SLOTS
                if u == 0 and half == 0:
                    pe.wait_ge(mrow_in[h % 2], b * (H * 16) + (h // 2 + 1) * 32)
                pe.wait_ge(p_exp, HPB * (b * (H * S2U) + h * S2U + u) + half + 1)
                r, q0 = MROW + 1, HALF * half
                if u < NB:
                    k = slice(P * u, P * u + P)
                    up = min(max(P * u - q0, 0), HALF)
                    if up > 0:
                        mm = pe.matmul(pB[:, q0:q0 + up], K[0:r, s, k], QU[0:r, s, q0:q0 + up], start=True, stop=True)
                    if up < HALF:
                        mm = pe.matmul(pB[:, q0 + up:q0 + HALF], K[0:r, s, k], QL[0:r, s, q0 + up:q0 + HALF], start=True, stop=True)
                else:
                    for k0 in range(q0, q0 + HALF, P):
                        k = slice(k0, k0 + P)
                        mm = pe.matmul(pB[:, k], K[0:r, s, k], QU[0:r, s, k], start=True, stop=True)
                mm.then_inc(s2_ready, 1)

            def context(b, h, u):
                n, quarter = h * S2U + u, S // STRIPS
                pe.wait_ge(p_mask, b * (H * S2U) + n + 1 + LATE)
                if u == 0:
                    pe.wait_ge(ctx_evac, b * H + h + 1)
                if (h, u) == (H // 2, 0):
                    pe.wait_ge(placed, b + 1)
                if u < NB:
                    pieces = [(u, quarter * strip, quarter) for strip in range(STRIPS)]
                else:
                    pieces = [(kb, P * kb, P) for i in range(2) for kb in range(i, NB, 2)]
                for kb, q0, w in pieces:
                    strip, at = VW * (q0 // quarter), q0 % quarter
                    mm = pe.matmul(pC[strip:strip + VW, at:at + w], vext[:, kb, h % H, :], prob[n % RING][:, q0:q0 + w],
                                   start=(u == 0), stop=(u == NB), skip_group_check=True)
                mm.then_inc(pv_done, 1)

            for j in range(PIECES):
                project(0, j)
            pe.wait_ge(e_done, E_N)
            pe.wait_ge(m_done, 1)
            pe.wait_ge(pos, 2)
            super_scores().then_inc(m_ready, 1)
            for i in range(2):
                pe.wait_ge(m_done, 2 + i)
                values(i, pM).then_inc(m_ready, 1)
            for h in range(AHEAD):
                for n in range(S1U):
                    first_pass(0, h, n)
            pe.wait_ge(m_done, 4)
            row_of_maxima(0, 0).then_inc(m_ready, 1)

            def turn_context(half, dst):
                for t in range(4):
                    mm = pe.transpose(dst[:, P * t:P * t + P], vsh[:, 4 * half + t, :, :].rearrange("p h d -> p (h d)"), ident[:, :])
                return mm

            def project_out(half, dst):
                for t in range(4):
                    c = P * (4 * half + t)
                    mm = pe.matmul(dst[:, P * t:P * t + P], ctxT[:, c:c + P], w_o[:, :], start=True, stop=True)
                return mm

            def small_piece(b, place):
                h = place[0]
                name, part, parts = PARTS[place]
                if part == 0 and name in W_OF:
                    pe.wait_ge(w_done, b * W_N + W_PRO + W_OF[name])
                elif part == 0:
                    last = next(p for p in M_PLACES if p >= place)
                    pe.wait_ge(m_done, b * M_N + M_PRO + M_IDX[last])
                if name == "row":
                    mm = row_of_maxima(b, h + 1)
                elif name == "context":
                    mm = context_turned(b, h - 1)
                elif name in ("turn 0", "turn 1"):
                    if name == "turn 0":
                        pe.wait_ge(norm, b * NORM_N + NORM_N)
                    mm = turn_context(int(name[-1]), pE)
                elif name in ("project 0", "project 1"):
                    mm = project_out(int(name[-1]), (pE, pM)[int(name[-1])])
                elif name in ("shifted 0", "shifted 1"):
                    mm = values_shifted(int(name[-1]))
                elif name == "super":
                    if part == 0:
                        pe.wait_ge(pos, b * POS_N + POS_N + 2)
                    mm = super_scores(part, parts)
                else:
                    mm = values(int(name[-1]), (pM, pE)[int(name[-1])])
                if part == parts - 1:
                    mm.then_inc(w_ready if name in W_OF else m_ready, 1)

            for j in range(0, P, VW):
                pe.matmul(pC[j:j + VW, :], vext[:, 0, H - 1, :], prob[1][:, 0:S // STRIPS], start=True, stop=False, skip_group_check=True)
            with pe.Fori(0, B) as b:
                for h in range(H):
                    for u in range(S2U):
                        second_pass(b, h, u, 0)
                        first_pass(b, h + AHEAD, 2 * u)
                        second_pass(b, h, u, 1)
                        first_pass(b, h + AHEAD, 2 * u + 1)
                        if (h, u) == (2, 0):
                            pe.wait_ge(w_done, b * W_N + W_PRO + W_OF["shifted 0"] + 1)
                        if h == 2 and u < PIECES:
                            project(b + 1, u)
                        if u < LATE:
                            context(b, h - 1, S2U - LATE + u)
                        else:
                            context(b, h, u - LATE)
                        if (h, u) in PARTS:
                            small_piece(b, (h, u))
            for u in range(LATE):
                context(B, -1, S2U - LATE + u)
            pe.wait_ge(m_done, B * M_N + M_PRO)
            context_turned(B, -1).then_inc(m_ready, 1)
            pe.wait_ge(norm, (B + 1) * NORM_N)
            for j in range(4):
                pe.wait_ge(m_done, B * M_N + M_PRO + 1 + j)
                mm = turn_context(j, pM) if j < 2 else project_out(j - 2, pM)
                mm.then_inc(m_ready, 1)

        @block.scalar
        def _(act):
            act.sem_inc(p_exp, HPB)
            act.sem_inc(psup_done, 1)
            act.wait_ge(d_w, D_W)
            act.wait_ge(set_dve, DVE_BIAS)

            def evacuate(nb, j):
                act.wait_ge(e_ready, nb * PIECES + j + 1)
                half = slice(HALF * (j % 2), HALF * (j % 2) + HALF)
                src = (pE, *pA)[j % 4] if isinstance(nb, int) else pE
                if j < 2:
                    act.activation(xnT[:, half], src[:, :], ACT.Identity, bias=cols[:, 1:2], scale=cols[:, 0:1]).then_inc(e_done, 1)
                elif j < 4:
                    act.activation(qv[:, half], src[:, :], ACT.Identity, bias=bias_qv[:, :]).then_inc(e_done, 1)
                    act.activation(qu[:, half], src[:, :], ACT.Identity, bias=bias_qu[:, :]).then_inc(e_done, 1)
                elif j < 6:
                    act.activation(kc[:, half], src[:, :], ACT.Identity, bias=cols[:, 3:4]).then_inc(e_done, 1)
                else:
                    act.activation(rp[:, half], src[:, :], ACT.Copy).then_inc(e_done, 1)

            def high(nb, i):
                name, src = (("c", qu), ("k", kc), ("gl", g_lo), ("gu", g_up))[i]
                if i < 2:
                    act.wait_ge(e_done, nb * E_N + E_N)
                else:
                    act.wait_ge(pos, nb * POS_N + (8 if i == 2 else 14))
                act.activation(parts[name][0][:, :], src[:, 0:S], ACT.Copy).then_inc(hi_done, 1)

            def copied(name, src, done):
                half = int(name[-1])
                four = slice(4 * half, 4 * half + 4)
                if name.startswith("values"):
                    src = src[:, :].rearrange("p (t h d) -> p t h d", t=4, d=D)
                    act.activation(vext[:, four, 0:H // 2, 0:D], src[:, :, 0:H // 2, :], ACT.Copy)
                    dst, src = held[:, four, :, :], src[:, :, H // 2:H, :]
                elif name.startswith("turn"):
                    dst, src = ctxT[:, HALF * half:HALF * half + HALF], src[:, :]
                else:
                    dst, src = vsh[:, four, :, :].rearrange("p t h d -> p t (h d)"), src[:, :].rearrange("p (t e) -> p t e", e=E)
                act.activation(dst, src, ACT.Copy).then_inc(done, 1)

            def context_out(b, h):
                act.wait_ge(pv_done, b * (H * S2U) + (h + 1) * S2U + RING)
                act.activation(ctxp[:, :], pC[:, :], ACT.Copy).then_inc(ctx_evac, 1)

            for j in range(PIECES):
                evacuate(0, j)
            for i in range(4):
                high(0, i)
            act.wait_ge(set_pool, POOL_SET)
            for i in range(2):
                act.wait_ge(m_ready, 3 + i)
                copied(f"values {i}", pM, m_done)
            with act.Fori(0, B) as b:
                for h in range(H):
                    for u in range(S2U):
                        n = h * S2U + u
                        if h == 2 and 0 < u <= PIECES:
                            evacuate(b + 1, u - 1)
                        if u == LATE:
                            context_out(b, h - 1)
                        if (h, u) == (0, 5):
                            act.wait_ge(m_done, b * M_N + M_PRO)
                            act.wait_ge(w_done, b * W_N + W_PRO)
                            act.activation(vext[:, :, H // 2:H, 0:D], held[:, :, :, :], ACT.Copy).then_inc(placed, 1)
                        before = (h, u - 1) if u else (h - 1, S2U - 1)
                        if M_ORDER.get(before) in COPIES:
                            act.wait_ge(m_ready, b * M_N + M_PRO + M_IDX[before] + 1)
                            copied(M_ORDER[before], pM, m_done)
                        if W_ORDER.get(before) in COPIES:
                            act.wait_ge(w_ready, b * W_N + W_OF[W_ORDER[before]] + 1)
                            copied(W_ORDER[before], pE, w_done)
                        act.wait_ge(s2_ready, HPB * (b * (H * S2U) + n) + 2)
                        act.wait_ge(pv_done, b * (H * S2U) + n + 1)
                        act.activation(prob[n % RING][:, 0:HALF], pB[:, 0:HALF], ACT.Exp, scale=SCALE).then_inc(p_exp, 1)
                        act.wait_ge(s2_ready, HPB * (b * (H * S2U) + n) + 3)
                        act.activation(prob[n % RING][:, HALF:S], pB[:, HALF:S], ACT.Exp, scale=SCALE).then_inc(p_exp, 1)
                        if (h, u) == (3, 3):
                            act.wait_ge(stored, (b + 1) * ST_N)
                        if (h, u) in HIGH_AT:
                            high(b + 1, HIGH_AT.index((h, u)))
                    if h == 0:
                        act.wait_ge(norm, b * NORM_N + 2)
                        act.wait_ge(norm, b * NORM_N + NORM_N)
                    act.wait_ge(dsup_done, b * H + h + 1)
                    act.activation(psup[:, h, :], dsup[:, h, :], ACT.Exp, scale=SCALE).then_inc(psup_done, 1)
            context_out(B, -1)
            for j in range(2):
                act.wait_ge(m_ready, B * M_N + M_PRO + 2 + j)
                copied(f"turn {j}", pM, m_done)

        @block.vector
        def _(v):
            def stats(nb, t):
                if t == 0:
                    v.wait_ge(d_x, nb * 16 + 16)
                else:
                    own = known(v, nb * LN_N + 2 * t - 1)
                    if not isinstance(nb, int):
                        v.wait_ge(set_dve, DVE_SET)
                    v.wait_ge(ln, own)
                    v.bn_aggr(mv[:, t - 1, :], st6[:, t - 1, :]).then_inc(ln, 1)
                if t < NB:
                    v.bn_stats(st6[:, t, :], xt[:, t, :]).then_inc(ln, 1)

            def normalize(nb, t):
                if t == 0:
                    v.wait_ge(rs_done, nb * RS_N + RS_N)
                v.tensor_scalar(xn[:, t, :], xt[:, t, :], mv[:, t, 0:1], rs[:, 2, t:t + 1], ALU.subtract, ALU.mult).then_inc(ln, 1)

            def low(nb, i):
                name, src = (("c", qu), ("k", kc), ("gl", g_lo), ("gu", g_up))[i]
                v.wait_ge(hi_done, nb * HI_N + i + 1)
                v.tensor_tensor(parts[name][1][:, :], src[:, 0:S], parts[name][0][:, :].bitcast(F32), ALU.subtract).then_inc(low_done, 1)

            def arrived_m(b, i):
                v.wait_ge(m_ready, b * M_N + M_PRO + i + 1)

            def super_out(src, done):
                v.tensor_tensor(acc[:, :, :, 3], src[:, 0:NB * H].rearrange("p (n h) -> p h n", h=H), cmask[:, :, :], ALU.add).then_inc(done, 1)

            def first_pass(b, h, n):
                s = h % H
                pieces = known(v, b * (H * S1U) + h * S1U + n + 1)
                v.wait_ge(set_pool, POOL_SET)
                v.wait_ge(s1_ready, pieces)
                if n < NB * HPB:
                    qb, k0, _ = piece(n)
                    at = 7 * P - P * qb + k0
                    v.tensor_tensor_reduce(junk[:, n % S1_BUFS, :], pA[n % S1_BUFS][:, :], lmask[:, at:at + HALF], 1.0, -3.0e38, ALU.add, ALU.max,
                                           acc[:, s, qb, n % 2:n % 2 + 1]).then_inc(s1_read, 1)
                else:
                    g = n % 2
                    for i in range(4):
                        blk = 4 * g + i
                        ttr = v.tensor_tensor_reduce(junk[:, n % S1_BUFS, P * i:P * i + P], pA[n % S1_BUFS][:, P * i:P * i + P], umask[:, :], 1.0, -3.0e38, ALU.add, ALU.max,
                                                     acc[:, s, blk, 2:3])
                    ttr.then_inc(s1_read, 1)

            def maxima(b, h):
                s = h % H
                v.wait_ge(s1_read, b * (H * S1U) + (h + 1) * S1U)
                v.tensor_reduce(mneg[:, s, :], acc[:, s, :, :], AX.X, ALU.max, negate=True).then_inc(mx_done, 1)
                v.wait_ge(mx_done, b * H + h + 1)
                v.tensor_tensor(dsup[:, s, :], acc[:, s, :, 3], mneg[:, s, :].bitcast(F32), ALU.add).then_inc(dsup_done, 1)

            def row_out(h):
                v.tensor_copy(mrow[h % 2][:, :], pM[0:NB, 0:P]).then_inc(m_done, 1)

            def context_placed(h):
                v.tensor_copy(ctx_all[:, :, h % H, :].rearrange("p (c i) d -> p i c d", c=STRIPS),
                              pM[:, 0:S // STRIPS].rearrange("p (i c w) -> p i c w", c=STRIPS, w=VW)[:, :, :, 0:D + 1]).then_inc(m_done, 1)

            def normalized(b, i):
                pq = psup[:, :, :].rearrange("p h n -> p n h")
                if i == 0:
                    v.wait_ge(psup_done, b * H + 1)
                else:
                    v.wait_ge(norm, b * NORM_N + i)
                if i == 0:
                    v.tensor_tensor(vsh[:, :, :, :], vsh[:, :, :, :], pq.unsqueeze(3).to_broadcast([P, NB, H, D]), ALU.mult).then_inc(norm, 1)
                elif i == 1:
                    v.tensor_tensor(den[:, :, :], ctx_all[:, :, :, D], pq, ALU.add).then_inc(norm, 1)
                elif i == 2:
                    v.reciprocal(den[:, :, :], den[:, :, :]).then_inc(norm, 1)
                elif i == 3:
                    v.tensor_tensor(vsh[:, :, :, :], vsh[:, :, :, :], ctx_all[:, :, :, 0:D], ALU.add).then_inc(norm, 1)
                else:
                    v.tensor_tensor(vsh[:, :, :, :], vsh[:, :, :, :], den[:, :, :].unsqueeze(3).to_broadcast([P, NB, H, D]), ALU.mult).then_inc(norm, 1)

            def final(half, src, done):
                x2 = xres[:, 4 * half:4 * half + 4, :]
                v.tensor_tensor(x2, x2, src[:, :].rearrange("p (t e) -> p t e", e=E), ALU.add).then_inc(done, 1)

            def small_piece(b, place):
                name, h = PARTS[place][0], place[0]
                if name in W_OF:
                    v.wait_ge(w_ready, b * W_N + W_OF[name] + 1)
                else:
                    arrived_m(b, M_IDX[place])
                if name == "row":
                    row_out(h + 1)
                elif name == "context":
                    context_placed(h - 1)
                elif name == "super":
                    super_out(pE, w_done)
                elif name == "project 0":
                    v.wait_ge(res_done, b + 1)
                    final(0, pE, w_done)
                else:
                    final(1, pM, m_done)

            for t in range(NB + 1):
                stats(0, t)
            for t in (xnT, kc, rp, rq):
                v.memset(t[:, S:S + 1], 0.0).then_inc(set_dve, 1)
            v.memset(ctx_all[:, :, :, :], 1.0).then_inc(set_dve, 1)
            v.memset(psup[:, :, :], 0.0).then_inc(set_dve, 1)
            v.memset(vsh[:, :, :, :], 0.0).then_inc(set_dve, 1)
            v.memset(K[MROW:MROW + 1, :, :].bitcast(F32), 1.0).then_inc(set_dve, 1)
            v.wait_ge(d_w, D_W)
            v.tensor_tensor(bias_qv[:, :], cols[:, 2:3], vu[:, 0:1], ALU.add).then_inc(set_dve, 1)
            v.tensor_tensor(bias_qu[:, :], cols[:, 2:3], vu[:, 1:2], ALU.add).then_inc(set_dve, 1)
            v.memset(bv_wide[:, :], 1.0).then_inc(set_dve, 1)
            v.wait_ge(set_dve, 11)
            v.tensor_scalar(bv_wide[:, :], bv_wide[:, :], cols[:, 4:5], None, ALU.mult).then_inc(set_dve, 1)
            for t in range(NB):
                normalize(0, t)
            v.wait_ge(d_cst, D_CST)
            v.tensor_copy(parts["pe"][0][:, :], g_lo[:, :]).then_inc(set_dve, 1)
            v.wait_ge(set_dve, 13)
            v.tensor_tensor(parts["pe"][1][:, :], g_lo[:, :], parts["pe"][0][:, :].bitcast(F32), ALU.subtract).then_inc(set_dve, 1)
            v.wait_ge(set_dve, DVE_SET)
            v.wait_ge(set_pool, POOL_SET)
            v.wait_ge(m_ready, 1)
            v.tensor_tensor(bo_rows[:, :], bo_rows[:, :], pM[:, 0:E], ALU.add).then_inc(m_done, 1)
            for i in range(2):
                low(0, i)
            v.wait_ge(e_done, E_N)
            turned = xres[:, :, :].rearrange("p t e -> p (t e)")
            v.tensor_tensor(g_up[:, :], rp[:, 1:S + 1], rot[2][:, :], ALU.mult).then_inc(upper, 1)
            v.wait_ge(swapped, 32)
            v.tensor_tensor(turned, rq[:, 1:S + 1], rot[3][:, :], ALU.mult).then_inc(upper, 1)
            v.wait_ge(upper, 2)
            v.tensor_tensor(g_up[:, :], g_up[:, :], turned, ALU.add).then_inc(upper, 1)
            for i in range(2, 4):
                low(0, i)
            for t in range(NB + 1):
                stats(1, t)
            v.wait_ge(m_ready, 2)
            super_out(pM, m_done)
            v.wait_ge(m_done, 2)
            for h in range(AHEAD):
                for n in range(S1U):
                    first_pass(0, h, n)
                maxima(0, h)
            v.wait_ge(m_ready, 5)
            v.tensor_copy(mrow[0][:, :], pM[0:NB, 0:P]).then_inc(m_done, 1)
            with v.Fori(0, B) as b:
                for h in range(H):
                    for u in range(S2U):
                        first_pass(b, h + AHEAD, 2 * u)
                        before = (h, u - 1) if u else (h - 1, S2U - 1)
                        if {**M_ORDER, **W_ORDER}.get(before, COPIES[0]) not in COPIES:
                            small_piece(b, before)
                        first_pass(b, h + AHEAD, 2 * u + 1)
                        if h == 0 and u in NORMALIZE_AT:
                            if u == NORMALIZE_AT[1]:
                                v.wait_ge(m_done, b * M_N + M_PRO + M_IDX[0, 3] + 1)
                            normalized(b, NORMALIZE_AT.index(u))
                        if (2, 3) <= (h, u) <= (3, 2):
                            stats(b + 2, (h - 2) * S2U + u - 3)
                        if h == 1 and u < NB:
                            normalize(b + 1, u)
                        if (h, u) in LOW_AT:
                            low(b + 1, LOW_AT.index((h, u)))
                    if h == 6:
                        v.wait_ge(w_done, b * W_N + W_PRO + W_OF["super"] + 1)
                    maxima(b, h + AHEAD)
            v.wait_ge(m_ready, B * M_N + M_PRO + 1)
            context_placed(H - 1)
            v.wait_ge(m_done, B * M_N + M_PRO + 1)
            for i in range(5):
                normalized(B, i)
            v.wait_ge(res_done, B + 1)
            for j in range(2):
                v.wait_ge(m_ready, B * M_N + M_PRO + 4 + j)
                final(j, pM, m_done)


def att_consts():
    import numpy as np
    div = np.exp(np.arange(0, E, 2, dtype=np.float32) * np.float32(-np.log(10000.0) / E)).astype(np.float64)
    w = np.repeat(div, 2)[:, None]
    q = np.arange(S)[None, :].astype(np.float64)
    odd = (np.arange(E) % 2 == 1)[:, None]
    sg = np.where(odd, 1.0, -1.0)
    rot = np.stack([np.cos((S - 1 - q) * w), sg * np.sin((S - 1 - q) * w), np.cos((q + 2) * w), -sg * np.sin((q + 2) * w)]).astype(np.float32)
    pe = np.where(odd, np.cos(q * w), np.sin(q * w)).astype(np.float32)
    p = np.arange(P)
    hsum = (p[:, None] // D == np.arange(H)[None, :]).astype(np.float32)
    return rot, pe, hsum

def att_layout(i):
    import numpy as np
    a = {k[8:]: np.asarray(v) for k, v in i.items() if k.startswith("L0_attn_")}
    def diag(m):
        out = np.zeros((P, P), np.float32)
        for h in range(H):
            out[D * h:D * h + D, D * h:D * h + D] = m
        return out
    rot, pe, hsum = att_consts()
    return {"x": a["inputs"][:B], "wq": diag(a["Wq"]), "wk": diag(a["Wk"]), "wv": diag(a["Wv"]), "wp": diag(a["Wp"].T),
            "wo": a["Wo"], "cols": np.stack([a["ln_gamma"], a["ln_beta"], np.tile(a["bq"], H), np.tile(a["bk"], H), np.tile(a["bv"], H)], 1),
            "vu": np.stack([a["v_bias"].reshape(-1), a["u_bias"].reshape(-1)], 1),  "bo": a["bo"],
            "rot": rot, "pe": pe, "hsum": hsum}


def sum_tensors(nc, ctx):
    return {"x2": [ctx.enter_context(nc.sbuf_tensor(f"x2_{b}", [P, NB, E], F32)) for b in range(B)],
            "gate": ctx.enter_context(nc.sbuf_tensor("gate", [P, TOPK, B * NB], F32))}


def expert_tensors(nc, ctx):
    def sb(name, shape, dt=F32):
        return ctx.enter_context(nc.sbuf_tensor(name, shape, dt))
    return {"w1": sb("w1_all", [P, NX * 2 * F]), "w2": sb("w2_all", [P, NX * (F // P) * E]),
            "b1": sb("b1_all", [P, NX * 2 * CHUNKS]), "b2": sb("b2_all", [P, NX * E]),
            "ident": sb("ident_f", [P, P]),
            "tile_expert": sb("tile_expert", [P, TABLE]),
            "expert_no": sb("expert_no", [1, TABLE], I32), "row_no": sb("row_no", [1, TABLE], I32)}


def routing_phase(nc, dram, keep):
    ctx = ExitStack()
    with ctx:
        def sb(name, shape, dt=F32):
            return ctx.enter_context(nc.sbuf_tensor(name, shape, dt))

        def sem(name):
            return ctx.enter_context(nc.semaphore(name))

        wr1, wr2 = sb("wr1", [P, RH]), sb("wr2", [RH, NX])
        br1, lns, lnb, br2 = sb("br1", [P, RH]), sb("lns", [P, RH]), sb("lnb", [P, RH]), sb("br2", [P, NX])
        ident = keep["ident"]
        tri, ones = sb("tri", [P, P], BF16), sb("ones", [P, P], BF16)
        mhalf, iota8 = sb("mhalf_r", [P, NB]), sb("iota8", [P, NX])
        xb = [sb(f"xb{i}", [P, NB, E]) for i in range(UNROLL)]
        rows = [sb(f"rows_r{i}", [P, NB, ROW]) for i in range(UNROLL)]
        idx = [sb(f"idx{i}", [P, NB, TOPK], U32) for i in range(UNROLL)]
        st, mv, rs = sb("st_r", [P, NB, 6]), sb("mv_r", [P, NB, 2]), sb("rs_r", [P, NB])
        st2, mv2, rs2 = sb("st2", [P, NB, 6]), sb("mv2", [P, NB, 2]), sb("rs2", [P, NB])
        hT, gT = sb("hT", [P, S]), sb("gT_r", [RH, S])
        hr, hg = sb("hr", [P, NB, RH]), sb("hg", [P, NB, RH])
        lg, mx, mi = sb("lg", [P, NB, NX]), sb("mx", [P, NB, NX]), sb("mi", [P, NB, NX], U32)
        dlt, xf = sb("dlt", [P, B * NB]), sb("xf", [P, NB, TOPK])
        oh, both = sb("oh", [P, NB, TOPK, NX]), sb("both", [P, NB, NX], BF16)
        pos, prod, posf = sb("pos", [P, NB, NX]), sb("prod", [P, NB, TOPK, NX]), sb("posf", [P, NB, TOPK])
        carry = sb("carry", [P, NX])
        start = sb("start", [P, NX])
        cnt, ti32, tiles = sb("cnt", [P, NX]), sb("ti32", [P, NX], I32), sb("tiles", [P, NX])
        cum, tno = sb("cum", [P, NX]), sb("tno", [P, TABLE])
        past, used = sb("past", [P, TABLE, NX - 1], BF16), sb("used", [P, TABLE, NX - 1], BF16)
        first, cap = sb("first", [P, TABLE]), sb("cap", [P, TABLE])
        padrow, padi = sb("padrow", [P, HALVES, ROW]), sb("padi", [1, NX], I32)
        pidx = sb("pidx", [P, 1])
        ex = sb("ex", [P, B * NB])

        def pb(name, shape):
            return ctx.enter_context(nc.psum_tensor(name, shape, F32))
        pT, pH, pG = pb("pT", [P, S]), pb("pH", [P, NB * RH]), pb("pG", [RH, S])
        pL, pR = pb("pL", [P, NB * NX]), pb("pR", [P, NB * NX + NX])

        d_w, d_big = sem("router_in"), sem("experts_in")
        d_x = [sem(f"x_in_r{i}") for i in range(UNROLL)]
        setp, setd = sem("set_pool_r"), sem("set_dve_r")
        a_dve, a_rs, a_tr, a_ev = sem("a_dve"), sem("a_rs"), sem("a_tr"), sem("a_ev")
        b_h, b_dve, b_rs, b_gelu, b_gt, b_gev, b_lg = (sem(n) for n in ("b_h", "b_dve", "b_rs", "b_gelu", "b_gt", "b_gev", "b_lg"))
        c_dve, c_rank, rows_free = sem("c_dve"), sem("c_rank"), sem("rows_free")
        scat = [sem(f"scattered{i}") for i in range(2)]
        t_dve, t_exp, t_pad = sem("t_dve"), sem("t_exp"), sem("t_pad")
        block = ctx.enter_context(nc.Block())
        A_N, A_STATS = 2 * NB + NB + 1, 2 * NB
        B_STATS, B_N = 1 + 2 * NB, 1 + 2 * NB + NB + 2
        C_N, C_BOTH, C_IDX = 1 + 2 * NB + 5 + 5, 1 + 2 * NB + 5, 1 + 2 * NB + 5 + 5
        SCAT_N = 16 * NB * TOPK
        D_W, SETP, SETD = 16 * 6, 10, 3
        D_BIG = 16 * (2 * NX + 2 + B)

        @block.sync
        def _(sp):
            for t, n in ((wr1, "wr1"), (wr2, "wr2")):
                sp.dma_start(t[:, :], dram[n]).then_inc(d_w, 16)
            for t, n in ((br1, "br1"), (lns, "lns"), (lnb, "lnb"), (br2, "br2")):
                sp.dma_start(t[:, :], dram[n].partition_broadcast(P)).then_inc(d_w, 16)

            def load(nb, k):
                sp.dma_start(xb[k][:, :, :], dram["x2s"][bass.ds(nb % B + 1, 1)].rearrange("o (t p) e -> p (o t) e", p=P)).then_inc(d_x[k], 16)
            for k in range(UNROLL):
                load(k, k)
            for e in range(NX):
                sp.dma_start(keep["w1"][:, 2 * F * e:2 * F * (e + 1)], dram["w1"][e]).then_inc(d_big, 16)
                sp.dma_start(keep["w2"][:, F * e:F * (e + 1)].rearrange("p (c d) -> p c d", d=E),
                             dram["w2"][e].rearrange("(c p) d -> p c d", p=P)).then_inc(d_big, 16)
            sp.dma_start(keep["b1"][:, :], dram["b1"]).then_inc(d_big, 16)
            sp.dma_start(keep["b2"][:, :], dram["b2"].partition_broadcast(P)).then_inc(d_big, 16)
            for b in range(B):
                sp.dma_start(keep["x2"][b][:, :, :], dram["x2s"][b + 1].rearrange("(t p) e -> p t e", p=P)).then_inc(d_big, 16)
            with sp.Fori(0, B // UNROLL) as it:
                for k in range(UNROLL):
                    nb = it * UNROLL + k
                    sp.wait_ge(d_w, D_W)
                    sp.wait_ge(a_dve, known(sp, nb * A_N + A_N))
                    load(nb + UNROLL, k)
            for k in range(UNROLL):
                sp.wait_ge(d_x[k], (B // UNROLL + 1) * 16)
            sp.wait_ge(d_big, D_BIG)
            sp.wait_ge(t_dve, 2)
            for e in range(NX):
                row = nc.values_load(padi[0:1, e:e + 1], engines=(mybir.EngineType.SP,), min_val=0, max_val=NX * REGION - ROWS,
                                     skip_runtime_bounds_check_because="a region has room for every token and a tile")
                sp.dma_start(dram["xs"][bass.ds(row, ROWS), :].rearrange("(a p) r -> p a r", p=P), padrow[:, :, :]).then_inc(t_pad, 16)
            sp.wait_ge(t_pad, 16 * NX)

        @block.gpsimd
        def _(po):
            po.memset(ident[:, :], 0.0).then_inc(setp, 1)
            po.memset(tri[:, :], 1.0).then_inc(setp, 1)
            po.memset(mhalf[:, :], -0.5).then_inc(setp, 1)
            po.iota(iota8[:, :], pattern=[[1, NX]], base=0, channel_multiplier=0, allow_small_or_imprecise_dtypes=True).then_inc(setp, 1)
            po.iota(rows[UNROLL - 1][:, :, E], pattern=[[P, NB]], base=TOKENS - S, channel_multiplier=1, allow_small_or_imprecise_dtypes=True).then_inc(setp, 1)
            po.iota(carry[:, :], pattern=[[REGION, NX]], base=0, channel_multiplier=0, allow_small_or_imprecise_dtypes=True).then_inc(setp, 1)
            po.iota(tno[:, :], pattern=[[1, TABLE]], base=0, channel_multiplier=0, allow_small_or_imprecise_dtypes=True).then_inc(setp, 1)
            po.iota(pidx[:, :], pattern=[[0, 1]], base=0, channel_multiplier=1, allow_small_or_imprecise_dtypes=True).then_inc(setp, 1)
            po.wait_ge(setp, 8)
            po.affine_select(out=ident[:, :], in_=ident[:, :], compare_op=ALU.not_equal, fill=1.0, base=0,
                             pattern=[[-1, P]], channel_multiplier=1).then_inc(setp, 1)
            po.affine_select(out=tri[:, :], in_=tri[:, :], compare_op=ALU.is_gt, fill=0.0, base=0,
                             pattern=[[1, P]], channel_multiplier=-1).then_inc(setp, 1)

            def rstd(done, out, var, eps, stats, stats_n, nb):
                have, mine = known(po, stats_n), known(po, nb * 2 + 1)
                po.wait_ge(setp, SETP)
                po.wait_ge(stats, have)
                po.tensor_scalar(out[:, :], var[:, :, 1], eps, None, ALU.add).then_inc(done, 1)
                po.wait_ge(done, mine)
                po.tensor_tensor(out[:, :], out[:, :], mhalf[:, :], ALU.pow).then_inc(done, 1)

            def rstd_a(nb):
                rstd(a_rs, rs, mv, LN_EPS, a_dve, nb * A_N + A_STATS, nb)

            def rstd_b(nb):
                rstd(b_rs, rs2, mv2, ROUTER_EPS, b_dve, nb * B_N + B_STATS, nb)

            po.sem_inc(rows_free, 1)
            rstd_a(0)
            rstd_a(1)
            rstd_b(0)
            rstd_a(2)
            with po.Fori(0, B // UNROLL) as it:
                for k in range(UNROLL):
                    nb = it * UNROLL + k
                    rstd_b(nb + 1)
                    placed = known(po, nb * C_N + C_IDX)
                    po.wait_ge(setp, SETP)
                    po.wait_ge(c_dve, placed)
                    for t in range(NB):
                        if t == 3:
                            if k > 0:
                                po.wait_ge(scat[(k - 1) % 2], it * (2 * SCAT_N) + (k + 1) // 2 * SCAT_N)
                                po.sem_inc(rows_free, 1)
                            rstd_a(nb + 3)
                        for j in range(TOPK):
                            po.indirect_dma_start(dram["xs"], bass.IndirectOffsetOnAxis(idx[k][:, t, j:j + 1], 0),
                                                  rows[k][:, t, :], None).then_inc(scat[k % 2], 16)
                for k in range(2):
                    po.wait_ge(scat[k], (it + 1) * (2 * SCAT_N))
                po.sem_inc(rows_free, 1)

        @block.tensor
        def _(pe):
            pe.wait_ge(d_w, D_W)
            pe.wait_ge(setp, SETP)
            pe.wait_ge(setd, SETD)

            def turn(nb, k):
                pe.wait_ge(a_dve, nb * A_N + A_N)
                if not (isinstance(nb, int) and nb == 0):
                    pe.wait_ge(a_ev, nb * 2)
                for t in range(NB):
                    mm = pe.transpose(pT[:, P * t:P * t + P], rows[k][:, t, 0:E], ident[:, :])
                mm.then_inc(a_tr, 1)

            def hidden(nb):
                pe.wait_ge(a_ev, nb * 2 + 2)
                if not (isinstance(nb, int) and nb == 0):
                    pe.wait_ge(b_dve, (nb - 1) * B_N + 1)
                for t in range(NB):
                    mm = pe.matmul(pH[:, RH * t:RH * t + RH], hT[:, P * t:P * t + P], wr1[:, :], start=True, stop=True)
                mm.then_inc(b_h, 1)

            def logits(nb):
                active, read = known(pe, nb + 1), known(pe, nb * 2)
                pe.wait_ge(setd, SETD)
                pe.wait_ge(b_gelu, active)
                if not (isinstance(nb, int) and nb == 0):
                    pe.wait_ge(b_gev, read)
                for t in range(NB):
                    mm = pe.transpose(pG[:, P * t:P * t + P], hg[:, t, :], ident[:, :])
                mm.then_inc(b_gt, 1)
                pe.wait_ge(b_gev, nb * 2 + 2)
                if not (isinstance(nb, int) and nb == 0):
                    pe.wait_ge(c_dve, (nb - 1) * C_N + 1)
                for t in range(NB):
                    mm = pe.matmul(pL[:, NX * t:NX * t + NX], gT[:, P * t:P * t + P], wr2[:, :], start=True, stop=True)
                mm.then_inc(b_lg, 1)

            def ranks(nb):
                pe.wait_ge(c_dve, nb * C_N + C_BOTH)
                pe.matmul(pR[:, 0:NB * NX], tri[:, :], both[:, :, :].rearrange("p t e -> p (t e)"), start=True, stop=False, skip_group_check=True)
                for t in range(NB - 1):
                    w = NB - 1 - t
                    pe.matmul(pR[:, NX * (t + 1):NX * NB].rearrange("p (t e) -> p t e", e=NX), ones[:, :],
                              both[:, t:t + 1, :].to_broadcast([P, w, NX]), start=False, stop=(t == NB - 2), skip_group_check=True)
                for t in range(NB):
                    mm = pe.matmul(pR[:, NX * NB:NX * NB + NX], ones[:, :], both[:, t, :], start=(t == 0), stop=(t == NB - 1), skip_group_check=True)
                mm.then_inc(c_rank, 1)

            turn(0, 0)
            hidden(0)
            turn(1, 1)
            hidden(1)
            logits(0)
            turn(2, 2)
            with pe.Fori(0, B // UNROLL) as it:
                for k in range(UNROLL):
                    nb = it * UNROLL + k
                    ranks(nb)
                    hidden(nb + 2)
                    logits(nb + 1)
                    turn(nb + 3, (k + 3) % UNROLL)

        @block.scalar
        def _(act):
            act.wait_ge(setp, SETP)

            def turned(nb):
                act.wait_ge(a_tr, nb + 1)
                if not (isinstance(nb, int) and nb == 0):
                    act.wait_ge(b_h, nb)
                for i in range(2):
                    act.activation(hT[:, 512 * i:512 * i + 512], pT[:, 512 * i:512 * i + 512], ACT.Copy).then_inc(a_ev, 1)

            def gelu(nb):
                act.wait_ge(b_dve, nb * B_N + B_N)
                if not (isinstance(nb, int) and nb == 0):
                    act.wait_ge(b_gt, nb)
                act.activation(hg[:, :, :], hr[:, :, :], ACT.Gelu_apprx_tanh).then_inc(b_gelu, 1)
                act.wait_ge(b_gt, nb + 1)
                if not (isinstance(nb, int) and nb == 0):
                    act.wait_ge(b_lg, nb)
                for i in range(2):
                    act.activation(gT[:, 512 * i:512 * i + 512], pG[:, 512 * i:512 * i + 512], ACT.Copy).then_inc(b_gev, 1)

            turned(0)
            turned(1)
            gelu(0)
            turned(2)
            with act.Fori(0, B // UNROLL) as it:
                for k in range(UNROLL):
                    nb = it * UNROLL + k
                    gelu(nb + 1)
                    turned(nb + 3)
            act.wait_ge(c_dve, B * C_N)
            act.activation(ex[:, :], dlt[:, :], ACT.Exp).then_inc(t_exp, 1)

        @block.vector
        def _(v):
            v.memset(ones[:, :], 1.0).then_inc(setd, 1)
            v.memset(padrow[:, :, 0:E], 0.0).then_inc(setd, 1)
            v.memset(padrow[:, :, E + 1:E + 2], -1.0).then_inc(setd, 1)
            v.wait_ge(d_w, D_W)
            v.wait_ge(setp, SETP)
            v.wait_ge(setd, SETD)

            def stats(nb, k, sem_, at, src, st_, mv_):
                for t in range(NB):
                    v.bn_stats(st_[:, t, :], src(t)).then_inc(sem_, 1)
                v.wait_ge(sem_, at + NB)
                for t in range(NB):
                    v.bn_aggr(mv_[:, t, :], st_[:, t, :]).then_inc(sem_, 1)

            def a1(nb, k, m):
                have = known(v, nb * A_N + NB)
                v.wait_ge(d_x[k], m * 16 + 16)
                for t in range(NB):
                    v.bn_stats(st[:, t, :], xb[k][:, t, :]).then_inc(a_dve, 1)
                v.wait_ge(setp, SETP)
                v.wait_ge(a_dve, have)
                for t in range(NB):
                    v.bn_aggr(mv[:, t, :], st[:, t, :]).then_inc(a_dve, 1)

            def a2(nb, k, waits=True):
                if waits:
                    v.wait_ge(rows_free, nb - 2)
                last = rows[(k - 1) % UNROLL][:, :, E]
                v.wait_ge(a_dve, nb * A_N) if not (isinstance(nb, int) and nb == 0) else None
                v.tensor_scalar(rows[k][:, :, E], last, float(S), None, ALU.add).then_inc(a_dve, 1)
                v.wait_ge(a_rs, nb * 2 + 2)
                for t in range(NB):
                    v.tensor_scalar(rows[k][:, t, 0:E], xb[k][:, t, :], mv[:, t, 0:1], rs[:, t:t + 1], ALU.subtract, ALU.mult).then_inc(a_dve, 1)

            def b1(nb):
                have, bias = known(v, nb * B_N + 1 + NB), known(v, nb * B_N + 1)
                v.wait_ge(b_h, nb + 1)
                if not (isinstance(nb, int) and nb == 0):
                    v.wait_ge(b_gelu, nb)
                v.tensor_tensor(hr[:, :, :], pH[:, :].rearrange("p (t e) -> p t e", e=RH),
                                br1[:, :].unsqueeze(1).to_broadcast([P, NB, RH]), ALU.add).then_inc(b_dve, 1)
                v.wait_ge(setp, SETP)
                v.wait_ge(b_dve, bias)
                for t in range(NB):
                    v.bn_stats(st2[:, t, :], hr[:, t, :]).then_inc(b_dve, 1)
                v.wait_ge(setp, SETP)
                v.wait_ge(b_dve, have)
                for t in range(NB):
                    v.bn_aggr(mv2[:, t, :], st2[:, t, :]).then_inc(b_dve, 1)

            def b2(nb):
                v.wait_ge(b_rs, nb * 2 + 2)
                for t in range(NB):
                    v.tensor_scalar(hr[:, t, :], hr[:, t, :], mv2[:, t, 0:1], rs2[:, t:t + 1], ALU.subtract, ALU.mult).then_inc(b_dve, 1)
                v.wait_ge(b_dve, nb * B_N + B_STATS + NB)
                v.tensor_tensor(hr[:, :, :], hr[:, :, :], lns[:, :].unsqueeze(1).to_broadcast([P, NB, RH]), ALU.mult).then_inc(b_dve, 1)
                v.wait_ge(b_dve, nb * B_N + B_STATS + NB + 1)
                v.tensor_tensor(hr[:, :, :], hr[:, :, :], lnb[:, :].unsqueeze(1).to_broadcast([P, NB, RH]), ALU.add).then_inc(b_dve, 1)

            def c1(nb, k):
                at = nb * C_N
                v.wait_ge(b_lg, nb + 1)
                v.tensor_tensor(lg[:, :, :], pL[:, :].rearrange("p (t e) -> p t e", e=NX),
                                br2[:, :].unsqueeze(1).to_broadcast([P, NB, NX]), ALU.add).then_inc(c_dve, 1)
                biased, best = known(v, at + 1), known(v, at + 1 + NB)
                v.wait_ge(setp, SETP)
                v.wait_ge(c_dve, biased)
                for t in range(NB):
                    v.max(mx[:, t, :], lg[:, t, :]).then_inc(c_dve, 1)
                v.wait_ge(setp, SETP)
                v.wait_ge(c_dve, best)
                for t in range(NB):
                    v.max_index(mi[:, t, :], mx[:, t, :], lg[:, t, :]).then_inc(c_dve, 1)
                v.tensor_tensor(dlt[:, bass.ds(nb * NB, NB)], mx[:, :, 1], mx[:, :, 0], ALU.subtract).then_inc(c_dve, 1)
                v.wait_ge(c_dve, at + 2 + 2 * NB)
                v.tensor_copy(xf[:, :, :], mi[:, :, 0:TOPK]).then_inc(c_dve, 1)
                v.wait_ge(c_dve, at + 3 + 2 * NB)
                v.tensor_copy(rows[k][:, :, E + 1], xf[:, :, 0]).then_inc(c_dve, 1)
                v.tensor_tensor(oh[:, :, :, :], xf[:, :, :].unsqueeze(3).to_broadcast([P, NB, TOPK, NX]),
                                iota8[:, :].unsqueeze(1).unsqueeze(1).to_broadcast([P, NB, TOPK, NX]), ALU.is_equal).then_inc(c_dve, 1)
                v.wait_ge(c_dve, at + 5 + 2 * NB)
                v.tensor_tensor(both[:, :, :], oh[:, :, 0, :], oh[:, :, 1, :], ALU.add).then_inc(c_dve, 1)

            def c2(nb, k):
                at = nb * C_N + C_BOTH
                v.wait_ge(c_rank, nb + 1)
                v.tensor_tensor(pos[:, :, :], pR[:, 0:NB * NX].rearrange("p (t e) -> p t e", e=NX),
                                carry[:, :].unsqueeze(1).to_broadcast([P, NB, NX]), ALU.add).then_inc(c_dve, 1)
                v.wait_ge(c_dve, at + 1)
                v.tensor_tensor(carry[:, :], carry[:, :], pR[:, NB * NX:NB * NX + NX], ALU.add).then_inc(c_dve, 1)
                v.wait_ge(c_dve, at + 2)
                v.tensor_tensor(prod[:, :, :, :], oh[:, :, :, :], pos[:, :, :].unsqueeze(2).to_broadcast([P, NB, TOPK, NX]), ALU.mult).then_inc(c_dve, 1)
                v.wait_ge(c_dve, at + 3)
                v.tensor_reduce(posf[:, :, :], prod[:, :, :, :], AX.X, ALU.add).then_inc(c_dve, 1)
                v.wait_ge(c_dve, at + 4)
                v.tensor_copy(idx[k][:, :, :], posf[:, :, :]).then_inc(c_dve, 1)

            a1(0, 0, 0)
            a2(0, 0, False)
            a1(1, 1, 0)
            a2(1, 1, False)
            b1(0)
            b2(0)
            a1(2, 2, 0)
            a2(2, 2, False)
            with v.Fori(0, B // UNROLL) as it:
                for k in range(UNROLL):
                    nb = it * UNROLL + k
                    c1(nb, k)
                    b1(nb + 1)
                    c2(nb, k)
                    b2(nb + 1)
                    a1(nb + 3, (k + 3) % UNROLL, it + (k + 3) // UNROLL)
                    a2(nb + 3, (k + 3) % UNROLL)
            v.wait_ge(setp, SETP)
            v.wait_ge(c_dve, B * C_N)
            v.tensor_scalar(padrow[:, :, E], pidx[:, :].to_broadcast([P, HALVES]), float((TOPK + 1) * TOKENS), None, ALU.add).then_inc(t_dve, 1)
            v.tensor_copy(padi[:, :], carry[0:1, :]).then_inc(t_dve, 1)
            v.tensor_scalar(start[:, :], iota8[:, :], float(REGION), None, ALU.mult).then_inc(t_dve, 1)
            v.wait_ge(t_dve, 3)
            v.tensor_tensor(cnt[:, :], carry[:, :], start[:, :], ALU.subtract).then_inc(t_dve, 1)
            v.wait_ge(t_dve, 4)
            v.tensor_scalar(ti32[:, :], cnt[:, :], float(ROWS - 1), None, ALU.add).then_inc(t_dve, 1)
            v.wait_ge(t_dve, 5)
            v.tensor_scalar(ti32[:, :], ti32[:, :], ROWS.bit_length() - 1, None, ALU.arith_shift_right).then_inc(t_dve, 1)
            v.wait_ge(t_dve, 6)
            v.tensor_copy(tiles[:, :], ti32[:, :]).then_inc(t_dve, 1)
            v.wait_ge(t_dve, 7)
            v.tensor_copy(cum[:, 0:1], tiles[:, 0:1]).then_inc(t_dve, 1)
            for e in range(1, NX):
                v.wait_ge(t_dve, 7 + e)
                v.tensor_tensor(cum[:, e:e + 1], cum[:, e - 1:e], tiles[:, e:e + 1], ALU.add).then_inc(t_dve, 1)
            v.wait_ge(t_dve, 15)
            every = lambda a: a.unsqueeze(1).to_broadcast([P, TABLE, NX - 1])
            v.tensor_tensor(past[:, :, :], tno[:, :].unsqueeze(2).to_broadcast([P, TABLE, NX - 1]), every(cum[:, 0:NX - 1]), ALU.is_ge).then_inc(t_dve, 1)
            v.wait_ge(t_dve, 16)
            v.tensor_reduce(keep["tile_expert"][:, :], past[:, :, :], AX.X, ALU.add).then_inc(t_dve, 1)
            v.tensor_tensor(used[:, :, :], past[:, :, :], every(tiles[:, 0:NX - 1]), ALU.mult).then_inc(t_dve, 1)
            v.wait_ge(t_dve, 18)
            v.tensor_reduce(first[:, :], used[:, :, :], AX.X, ALU.add).then_inc(t_dve, 1)
            v.tensor_scalar(cap[:, :], keep["tile_expert"][:, :], float(NX - 1), -float(REGION), ALU.subtract, ALU.mult).then_inc(t_dve, 1)
            v.wait_ge(t_dve, 20)
            v.tensor_tensor(first[:, :], tno[:, :], first[:, :], ALU.subtract).then_inc(t_dve, 1)
            v.tensor_scalar(cap[:, :], cap[:, :], cnt[:, NX - 1:NX], None, ALU.add).then_inc(t_dve, 1)
            v.wait_ge(t_dve, 22)
            v.tensor_scalar(first[:, :], first[:, :], float(ROWS), None, ALU.mult).then_inc(t_dve, 1)
            v.wait_ge(t_dve, 23)
            v.tensor_tensor(first[:, :], first[:, :], cap[:, :], ALU.min).then_inc(t_dve, 1)
            v.wait_ge(t_dve, 24)
            v.tensor_scalar(cap[:, :], keep["tile_expert"][:, :], float(REGION), None, ALU.mult).then_inc(t_dve, 1)
            v.wait_ge(t_dve, 25)
            v.tensor_tensor(keep["row_no"][:, :], first[0:1, :], cap[0:1, :], ALU.add).then_inc(t_dve, 1)
            v.tensor_copy(keep["expert_no"][:, :], keep["tile_expert"][0:1, :]).then_inc(t_dve, 1)
            v.wait_ge(t_exp, 1)
            g0, g1 = keep["gate"][:, 0, :], keep["gate"][:, 1, :]
            v.tensor_scalar(g0, ex[:, :], 1.0, None, ALU.add).then_inc(t_dve, 1)
            v.wait_ge(t_dve, 28)
            v.reciprocal(g0, g0).then_inc(t_dve, 1)
            v.wait_ge(t_dve, 29)
            v.tensor_tensor(g1, ex[:, :], g0, ALU.mult).then_inc(t_dve, 1)
            v.wait_ge(t_dve, 30)


def expert_phase(nc, dram, keep):
    ctx = ExitStack()
    with ctx:
        def sb(name, shape, dt=F32):
            return ctx.enter_context(nc.sbuf_tensor(name, shape, dt))

        def pb(name, shape):
            return ctx.enter_context(nc.psum_tensor(name, shape, F32))

        def sem(name):
            return ctx.enter_context(nc.semaphore(name))
        two = range(2)
        ident = keep["ident"]
        xg = [sb(f"xg{i}", [P, HALVES, ROW]) for i in range(TURNS)]
        xT = [(sb(f"xT_h{i}", [P, ROWS], F32R), sb(f"xT_l{i}", [P, ROWS], F32R)) for i in two]
        w1 = [(sb(f"w1_h{i}", [P, 2 * F], F32R), sb(f"w1_l{i}", [P, 2 * F], F32R)) for i in two]
        gl, g = [sb(f"gl{i}", [P, CHUNKS, ROWS]) for i in two], [sb(f"g{i}", [P, CHUNKS, ROWS]) for i in two]
        yb = [sb(f"yb{i}", [P, HALVES, E]) for i in range(TURNS)]
        other, dst = [sb(f"other{i}", [P, HALVES]) for i in range(TURNS)], [sb(f"dst{i}", [P, HALVES], U32) for i in range(TURNS)]
        pad_slot = sb("pad_slot", [P, TURNS * HALVES])
        pLin, pGate = [pb(f"pLin{i}", [P, 2, ROWS]) for i in two], [pb(f"pGate{i}", [P, 2, ROWS]) for i in two]
        pTurn = pb("pTurn", [P, ROWS])
        pY = [pb(f"pY{i}", [P, HALVES, E]) for i in two]
        x_in = [sem(f"rows_in{i}") for i in range(TURNS)]
        x_tr, x_hi, x_lo, up_gate, up_lin = (sem(n) for n in ("x_turned", "x_high", "x_low", "gate_up", "linear_up"))
        w_hi, w_lo = sem("w1_high"), sem("w1_low")
        gelu, prod, choice, places = (sem(n) for n in ("gelu_done", "product_done", "choice", "places"))
        down, y_done, going = (sem(n) for n in ("down_done", "y_done", "going"))
        y_out = [sem(f"y_out{i}") for i in range(TURNS)]
        block = ctx.enter_context(nc.Block())
        STEPS = TILES // TURNS

        def load_experts(engine, i, n):
            return nc.values_load_multi_w_load_instructions(keep["expert_no"][0:1, bass.ds(i, n)], engines=(engine,), min_val=0, max_val=NX - 1,
                                                            skip_runtime_bounds_check_because="a count of the seven first experts")[1]

        def steps(eng, step):
            for k in range(TURNS):
                step(0, k)
            with eng.Fori(1, STEPS) as it:
                for k in range(TURNS):
                    step(it, k)

        @block.sync
        def _(sp):
            def load(i, k):
                row = nc.values_load(keep["row_no"][0:1, bass.ds(i, 1)], engines=(mybir.EngineType.SP,), min_val=0, max_val=NX * REGION - ROWS,
                                     skip_runtime_bounds_check_because="a tile of a region")
                sp.dma_start(xg[k][:, :, :], dram["xs"][bass.ds(row, ROWS), :].rearrange("(a p) r -> p a r", p=P)).then_inc(x_in[k], 16)

            def step(it, k):
                i = it * TURNS + k
                sp.wait_ge(x_tr, known(sp, i + 1))
                sp.wait_ge(places, known(sp, i + 1))
                load(i + TURNS, k)
            for k in range(TURNS):
                load(k, k)
            steps(sp, step)
            for k in range(TURNS):
                sp.wait_ge(x_in[k], (STEPS + 1) * 16)

        @block.gpsimd
        def _(po):
            def place(i, k):
                k, tile = k % TURNS, known(po, i + 1)
                po.wait_ge(going, 2)
                po.wait_ge(choice, tile)
                for a in range(HALVES):
                    at = k * HALVES + a
                    last = po.tensor_scalar(dst[k][:, a:a + 1], other[k][:, a:a + 1], xg[k][:, a, E:E + 1], pad_slot[:, at:at + 1], ALU.add, ALU.min)
                last.then_inc(places, 1)

            def step(it, k):
                i = it * TURNS + k
                place(i + 1, k + 1)
                tile = known(po, i + 1)
                po.wait_ge(going, 2)
                po.wait_ge(places, tile)
                po.wait_ge(y_done, tile)
                for a in range(HALVES):
                    po.indirect_dma_start(dram["ys"], bass.IndirectOffsetOnAxis(dst[k][:, a:a + 1], 0), yb[k][:, a, :], None).then_inc(y_out[k], 16)
            po.sem_inc(going, 1)
            po.iota(pad_slot[:, :], pattern=[[P, TURNS * HALVES]], base=TOPK * TOKENS, channel_multiplier=1, allow_small_or_imprecise_dtypes=True).then_inc(going, 1)
            place(0, 0)
            steps(po, step)
            for k in range(TURNS):
                po.wait_ge(y_out[k], STEPS * HALVES * 16)

        @block.tensor
        def _(pe):
            def turn(it, k):
                pe.wait_ge(x_in[k], it * 16 + 16)
                for a in range(HALVES):
                    mm = pe.transpose(pTurn[:, P * a:P * a + P], xg[k][:, a, 0:E], ident[:, :])
                mm.then_inc(x_tr, 1)

            def up(k, pair):
                for half, banks, done in ((1, pGate, up_gate), (0, pLin, up_lin)):
                    for c in two:
                        at = half * F + (2 * pair + c) * P
                        for n, (w, x) in enumerate(((0, 0), (0, 1), (1, 0))):
                            mm = pe.matmul(banks[pair][:, c, :], w1[k % 2][w][:, at:at + P], xT[k % 2][x][:, :], start=(n == 0), stop=(n == 2))
                    mm.then_inc(done, 1)

            def out(k, ex):
                for a in range(HALVES):
                    for c in range(CHUNKS):
                        mm = pe.matmul(pY[k % 2][:, a, :], g[k % 2][:, c, P * a:P * a + P], keep["w2"][:, bass.ds(ex * F + c * E, E)],
                                       start=(c == 0), stop=(c == CHUNKS - 1))
                mm.then_inc(down, 1)

            def step(it, k):
                i = it * TURNS + k
                if k == 0:
                    step.experts = load_experts(mybir.EngineType.PE, i, TURNS)
                pe.wait_ge(w_lo, i + 2)
                pe.wait_ge(x_lo, i + 2)
                for pair in two:
                    pe.wait_ge(prod, i * CHUNKS + 2 * pair + 2)
                    up(k + 1, pair)
                turn(it + (k + 2) // TURNS, (k + 2) % TURNS)
                out(k, step.experts[k])

            turn(0, 0)
            pe.wait_ge(x_lo, 1)
            turn(0, 1)
            pe.wait_ge(w_lo, 1)
            for pair in two:
                up(0, pair)
            steps(pe, step)

        @block.scalar
        def _(act):
            def turned(i, k):
                act.wait_ge(x_tr, i + 1)
                act.activation(xT[k % 2][0][:, :], pTurn[:, :], ACT.Copy).then_inc(x_hi, 1)

            def weights(k, ex):
                act.activation(w1[k % 2][0][:, :], keep["w1"][:, bass.ds(ex * (2 * F), 2 * F)], ACT.Copy).then_inc(w_hi, 1)

            def gelus(i, k, ex):
                for c in range(CHUNKS):
                    if c % 2 == 0:
                        act.wait_ge(up_gate, i * 2 + c // 2 + 1)
                    act.activation(gl[k % 2][:, c, :], pGate[c // 2][:, c % 2, :], ACT.Gelu_apprx_tanh,
                                   bias=keep["b1"][:, bass.ds(ex * (2 * CHUNKS) + (CHUNKS + c), 1)]).then_inc(gelu, 1)

            def step(it, k):
                i = it * TURNS + k
                if k == 0:
                    step.experts = load_experts(mybir.EngineType.Activation, i, TURNS + 2)
                act.wait_ge(up_lin, i * 2 + 2)
                weights(k, step.experts[k + 2])
                gelus(i + 1, k + 1, step.experts[k + 1])
                turned(i + 2, k)

            ex = load_experts(mybir.EngineType.Activation, 0, 2)
            for k in two:
                weights(k, ex[k])
                turned(k, k)
            gelus(0, 0, ex[0])
            steps(act, step)

        @block.vector
        def _(v):
            def low(i, k):
                v.wait_ge(x_hi, i + 1)
                v.tensor_tensor(xT[k % 2][1][:, :], pTurn[:, :], xT[k % 2][0][:, :].bitcast(F32), ALU.subtract).then_inc(x_lo, 1)

            def weights(i, k, ex):
                v.wait_ge(w_hi, i + 1)
                v.tensor_tensor(w1[k % 2][1][:, :], keep["w1"][:, bass.ds(ex * (2 * F), 2 * F)], w1[k % 2][0][:, :].bitcast(F32), ALU.subtract).then_inc(w_lo, 1)

            def products(i, k, ex):
                for c in range(CHUNKS):
                    if c % 2 == 0:
                        v.wait_ge(up_lin, i * 2 + c // 2 + 1)
                    v.wait_ge(gelu, i * CHUNKS + c + 1)
                    v.scalar_tensor_tensor(g[k % 2][:, c, :], pLin[c // 2][:, c % 2, :], keep["b1"][:, bass.ds(ex * (2 * CHUNKS) + c, 1)],
                                           gl[k % 2][:, c, :], ALU.add, ALU.mult).then_inc(prod, 1)

            def slot(it, k):
                if not (isinstance(it, int) and it == 0):
                    v.wait_ge(y_out[k], it * (HALVES * 16))
                v.tensor_scalar(other[k][:, :], xg[k][:, :, E + 1], keep["tile_expert"][:, bass.ds(it * TURNS + k, 1)], -float(TOKENS), ALU.is_equal, ALU.mult).then_inc(choice, 1)

            def step(it, k):
                i = it * TURNS + k
                if k == 0:
                    step.experts = load_experts(mybir.EngineType.DVE, i, TURNS + 2)
                weights(i + 2, k, step.experts[k + 2])
                products(i + 1, k + 1, step.experts[k + 1])
                slot(it + (k + 1) // TURNS, (k + 1) % TURNS)
                low(i + 2, k)
                v.wait_ge(down, i + 1)
                v.tensor_tensor(yb[k][:, :, :], pY[k % 2][:, :, :], keep["b2"][:, bass.ds(step.experts[k] * E, E)].unsqueeze(1).to_broadcast([P, HALVES, E]), ALU.add).then_inc(y_done, 1)

            ex = load_experts(mybir.EngineType.DVE, 0, 2)
            for k in two:
                weights(k, k, ex[k])
                low(k, k)
            products(0, 0, ex[0])
            slot(0, 0)
            steps(v, step)


def combine_phase(nc, dram, keep):
    ctx = ExitStack()
    with ctx:
        def sb(name, shape, dt=F32):
            return ctx.enter_context(nc.sbuf_tensor(name, shape, dt))

        def sem(name):
            return ctx.enter_context(nc.semaphore(name))
        x2 = keep["x2"]
        y = [[sb(f"y{j}_{b}", [P, NB, E]) for b in range(B)] for j in range(TOPK)]
        d_in = [sem(f"sum_in{b}") for b in range(B)]
        scaled, s_dve, d_out = sem("first_scaled"), sem("summed"), sem("out_done")
        block = ctx.enter_context(nc.Block())

        @block.sync
        def _(sp):
            for b in range(B):
                for j in range(TOPK):
                    lo = TOKENS * j + S * b
                    sp.dma_start(y[j][b][:, :, :], dram["ys"][lo:lo + S].rearrange("(t p) e -> p t e", p=P)).then_inc(d_in[b], 16)
            for b in range(B):
                sp.wait_ge(s_dve, (b + 1) * (NB + 1))
                sp.dma_start(dram["out"][b].rearrange("(t p) e -> p t e", p=P), x2[b][:, :, :]).then_inc(d_out, 16)
            sp.wait_ge(d_out, B * 16)

        @block.scalar
        def _(act):
            for b in range(B):
                act.wait_ge(d_in[b], TOPK * 16)
                for t in range(NB):
                    c = b * NB + t
                    act.activation(y[0][b][:, t, :], y[0][b][:, t, :], ACT.Copy, scale=keep["gate"][:, 0, c:c + 1]).then_inc(scaled, 1)

        @block.vector
        def _(v):
            for b in range(B):
                v.wait_ge(d_in[b], TOPK * 16)
                for t in range(NB):
                    c = b * NB + t
                    v.scalar_tensor_tensor(x2[b][:, t, :], y[1][b][:, t, :], keep["gate"][:, 1, c:c + 1], x2[b][:, t, :], ALU.mult, ALU.add).then_inc(s_dve, 1)
                v.wait_ge(scaled, (b + 1) * NB)
                v.wait_ge(s_dve, b * (NB + 1) + NB)
                v.tensor_tensor(x2[b][:, :, :], x2[b][:, :, :], y[0][b][:, :, :], ALU.add).then_inc(s_dve, 1)


def ffn_layout(i):
    import numpy as np
    a = {k[7:]: np.asarray(v) for k, v in i.items() if k.startswith("L0_ffn_")}
    return {"wr1": a["Wr1"], "br1": a["br1"], "lns": a["ln_scale"], "lnb": a["ln_bias"], "wr2": a["Wr2"], "br2": a["br2"],
            "w1": a["W1"], "w2": a["W2"], "b1": a["b1"].reshape(-1, P).T, "b2": a["b2"].reshape(-1)}


def kernel(**inputs):
    import numpy as np
    import concourse.bacc as bacc
    from concourse.bass_utils import run_bass_kernel_spmd as run
    nc = bacc.Bacc("TRN2", target_bir_lowering=False, num_devices=1)
    arrays = {k: np.ascontiguousarray(v) for k, v in {**att_layout(inputs), **ffn_layout(inputs)}.items()}
    dram = {k: nc.dram_tensor("in_" + k, v.shape, F32, kind="ExternalInput").ap() for k, v in arrays.items()}
    dram["out"] = nc.dram_tensor("out", [B, S, E], F32, kind="ExternalOutput").ap()
    dram["operands"] = nc.dram_tensor("split_operands", [B + 1, 3, H, 4, D, S], F32).ap()
    dram["x2s"] = nc.dram_tensor("after_attention", [B + 1, S, E], F32).ap()
    dram["xs"] = nc.dram_tensor("routed_rows", [NX * REGION, ROW], F32).ap()
    dram["ys"] = nc.dram_tensor("expert_rows", [TOPK * TOKENS + TURNS * ROWS, E], F32).ap()
    attention_phase(nc, dram)
    with ExitStack() as ctx:
        keep = sum_tensors(nc, ctx)
        with ExitStack() as inner:
            experts = {**keep, **expert_tensors(nc, inner)}
            routing_phase(nc, dram, experts)
            expert_phase(nc, dram, experts)
        combine_phase(nc, dram, keep)
    return run(nc, [{"in_" + k: v for k, v in arrays.items()}], core_ids=[0]).results[0]["out"]
```
